# Optimizing a Trainium2 kernel written in Bass

```python
import numpy as np
import jax
import jax.numpy as jnp

def _softmax(x, axis=-1):
    return jax.nn.softmax(x, axis=axis)

def _gelu(x):
    return jax.nn.gelu(x, approximate=True)

def _silu(x):
    return jax.nn.silu(x)

def _sigmoid(x):
    return jax.nn.sigmoid(x)

def _layernorm(x, axis=-1, eps=1e-05):
    m = jnp.mean(x, axis=axis, keepdims=True)
    v = jnp.var(x, axis=axis, keepdims=True)
    return (x - m) / jnp.sqrt(v + eps)

def _scatter_add(tgt, idx, src, axis=0):
    return tgt.at[idx].add(src)

def _segment_sum(src, seg, n):
    return jax.ops.segment_sum(src, seg, n)
kernel_name = 'mk_hybrid_d1_jaxref_r8_391246'

def setup_inputs(seed: int=0):
    np.random.seed(seed)
    _w = jnp.asarray

    def _L0_attn_a_setup():
        import jax, jax.numpy as jnp
        import numpy as np
        B, N, D, H, DH = (2, 256, 128, 16, 64)
        key = jax.random.key(seed)
        ks = jax.random.split(key, 5)
        x = jax.random.normal(ks[0], (B, N, D), dtype=jnp.float32)
        Wq = jax.random.normal(ks[1], (D, H * DH), dtype=jnp.float32) * 0.02
        Wk = jax.random.normal(ks[2], (D, H * DH), dtype=jnp.float32) * 0.02
        Wv = jax.random.normal(ks[3], (D, H * DH), dtype=jnp.float32) * 0.02
        Wo = jax.random.normal(ks[4], (H * DH, D), dtype=jnp.float32) * 0.02
        bo = jnp.zeros((D,), dtype=jnp.float32)
        return {'x': x, 'Wq': Wq, 'Wk': Wk, 'Wv': Wv, 'Wo': Wo, 'bo': bo}
    _L0_attn_a_in = _L0_attn_a_setup()

    def _L0_attn_b_setup():
        import jax, jax.numpy as jnp
        import numpy as np
        D_MODEL = 128
        D_STATE = 128
        D_CONV = 4
        EXPAND = 2
        D_HEAD = 64
        NGROUPS = 1
        CHUNK = 32
        D_INNER = EXPAND * D_MODEL
        D_SSM = D_INNER
        NHEADS = D_SSM // D_HEAD
        CONV_DIM = D_SSM + 2 * NGROUPS * D_STATE
        D_IN_PROJ = 2 * D_INNER + 2 * NGROUPS * D_STATE + NHEADS
        EPS = 1e-05

        def _silu(x):
            return x * jax.nn.sigmoid(x)
        key = jax.random.key(seed)
        ks = jax.random.split(key, 8)
        B, L = (2, 256)
        u = jax.random.normal(ks[0], (B, L, D_MODEL), jnp.float32)
        W_in = jax.random.normal(ks[1], (D_IN_PROJ, D_MODEL), jnp.float32) * D_MODEL ** (-0.5)
        conv_w = jax.random.normal(ks[2], (CONV_DIM, D_CONV), jnp.float32) * 0.2
        conv_b = jax.random.normal(ks[3], (CONV_DIM,), jnp.float32) * 0.1
        dt = jnp.exp(jax.random.uniform(ks[4], (NHEADS,)) * (np.log(0.1) - np.log(0.001)) + np.log(0.001))
        dt_bias = dt + jnp.log(-jnp.expm1(-dt))
        A_log = jnp.log(jax.random.uniform(ks[5], (NHEADS,), minval=1.0, maxval=16.0))
        D = jnp.ones((NHEADS,), jnp.float32)
        norm_w = jnp.ones((D_SSM,), jnp.float32)
        W_out = jax.random.normal(ks[6], (D_MODEL, D_INNER), jnp.float32) * D_INNER ** (-0.5)
        return dict(u=u, W_in=W_in, conv_w=conv_w, conv_b=conv_b, dt_bias=dt_bias, A_log=A_log, D=D, norm_w=norm_w, W_out=W_out)
    _L0_attn_b_in = _L0_attn_b_setup()

    def _L0_ffn_setup():
        import jax, jax.numpy as jnp
        import numpy as np
        D_MODEL = 128
        N_EXPERTS = 8
        TOP_K = 2
        HIDDEN = 4 * D_MODEL
        key = jax.random.key(seed)
        ks = jax.random.split(key, 6)
        B, S = (2, 256)
        x = jax.random.normal(ks[0], (B, S, D_MODEL), dtype=jnp.float32)
        shared_w1 = jax.random.normal(ks[1], (HIDDEN, D_MODEL), dtype=jnp.float32) * 0.02
        shared_w2 = jax.random.normal(ks[2], (D_MODEL, HIDDEN), dtype=jnp.float32) * 0.02
        experts_w1 = jax.random.normal(ks[3], (N_EXPERTS, HIDDEN, D_MODEL), dtype=jnp.float32) * 0.02
        experts_w2 = jax.random.normal(ks[4], (N_EXPERTS, D_MODEL, HIDDEN), dtype=jnp.float32) * 0.02
        gate_w = jax.random.normal(ks[5], (N_EXPERTS, D_MODEL), dtype=jnp.float32) * 0.02
        return {'x': x, 'shared_w1': shared_w1, 'shared_w2': shared_w2, 'experts_w1': experts_w1, 'experts_w2': experts_w2, 'gate_w': gate_w}
    _L0_ffn_in = _L0_ffn_setup()
    _d = {'L0_attn_a_x': _L0_attn_a_in['x'], 'L0_attn_a_Wq': _L0_attn_a_in['Wq'], 'L0_attn_a_Wk': _L0_attn_a_in['Wk'], 'L0_attn_a_Wv': _L0_attn_a_in['Wv'], 'L0_attn_a_Wo': _L0_attn_a_in['Wo'], 'L0_attn_a_bo': _L0_attn_a_in['bo'], 'L0_attn_b_W_in': _L0_attn_b_in['W_in'], 'L0_attn_b_conv_w': _L0_attn_b_in['conv_w'], 'L0_attn_b_conv_b': _L0_attn_b_in['conv_b'], 'L0_attn_b_dt_bias': _L0_attn_b_in['dt_bias'], 'L0_attn_b_A_log': _L0_attn_b_in['A_log'], 'L0_attn_b_D': _L0_attn_b_in['D'], 'L0_attn_b_norm_w': _L0_attn_b_in['norm_w'], 'L0_attn_b_W_out': _L0_attn_b_in['W_out'], 'L0_ffn_shared_w1': _L0_ffn_in['shared_w1'], 'L0_ffn_shared_w2': _L0_ffn_in['shared_w2'], 'L0_ffn_experts_w1': _L0_ffn_in['experts_w1'], 'L0_ffn_experts_w2': _L0_ffn_in['experts_w2'], 'L0_ffn_gate_w': _L0_ffn_in['gate_w']}
    _x0 = _d['L0_attn_a_x']
    _d['L0_attn_a_x'] = jax.random.normal(jax.random.fold_in(jax.random.key(seed), 1), (8, 256, 128), dtype=_x0.dtype)
    del _x0
    return _d

def reference(L0_attn_a_x, L0_attn_a_Wq, L0_attn_a_Wk, L0_attn_a_Wv, L0_attn_a_Wo, L0_attn_a_bo, L0_attn_b_W_in, L0_attn_b_conv_w, L0_attn_b_conv_b, L0_attn_b_dt_bias, L0_attn_b_A_log, L0_attn_b_D, L0_attn_b_norm_w, L0_attn_b_W_out, L0_ffn_shared_w1, L0_ffn_shared_w2, L0_ffn_experts_w1, L0_ffn_experts_w2, L0_ffn_gate_w):

    def _L0_attn_a_ref(x, Wq, Wk, Wv, Wo, bo):
        import jax, jax.numpy as jnp
        import numpy as np
        B, N, D, H, DH = (2, 256, 128, 16, 64)
        b, n, _ = x.shape
        scale = DH ** (-0.5)
        q = (x @ Wq).reshape(b, n, H, DH)
        k = (x @ Wk).reshape(b, n, H, DH)
        v = (x @ Wv).reshape(b, n, H, DH)
        base = (2.0 ** 8) ** (1.0 / H)
        slope = 1.0 / base ** jnp.arange(1, H + 1, dtype=jnp.float32)
        pos = jnp.arange(n, dtype=jnp.float32)
        bias = slope[:, None, None] * (pos[:, None] - pos[None, :])
        scores = jnp.einsum('bihd,bjhd->bhij', q, k) * scale + bias[None]
        causal = pos[:, None] >= pos[None, :]
        scores = jnp.where(causal[None, None], scores, jnp.float32(-1e+30))
        attn = jax.nn.softmax(scores, axis=-1)
        out = jnp.einsum('bhij,bjhd->bihd', attn, v).reshape(b, n, H * DH)
        return out @ Wo + bo

    def _L0_attn_b_ref(u, W_in, conv_w, conv_b, dt_bias, A_log, D, norm_w, W_out):
        import jax, jax.numpy as jnp
        import numpy as np
        D_MODEL = 128
        D_STATE = 128
        D_CONV = 4
        EXPAND = 2
        D_HEAD = 64
        NGROUPS = 1
        CHUNK = 32
        D_INNER = EXPAND * D_MODEL
        D_SSM = D_INNER
        NHEADS = D_SSM // D_HEAD
        CONV_DIM = D_SSM + 2 * NGROUPS * D_STATE
        D_IN_PROJ = 2 * D_INNER + 2 * NGROUPS * D_STATE + NHEADS
        EPS = 1e-05

        def _silu(x):
            return x * jax.nn.sigmoid(x)
        B, L, _ = u.shape
        zxbcdt = u @ W_in.T
        z, xBC, dt_raw = jnp.split(zxbcdt, [D_SSM, D_SSM + CONV_DIM], axis=-1)
        xpad = jnp.pad(xBC, ((0, 0), (D_CONV - 1, 0), (0, 0)))
        xBC = sum((xpad[:, k:k + L, :] * conv_w[:, k] for k in range(D_CONV))) + conv_b
        xBC = _silu(xBC)
        x, Bm, Cm = jnp.split(xBC, [D_SSM, D_SSM + NGROUPS * D_STATE], axis=-1)
        x = x.reshape(B, L, NHEADS, D_HEAD)
        Bm = Bm.reshape(B, L, NGROUPS, D_STATE)
        Cm = Cm.reshape(B, L, NGROUPS, D_STATE)
        A = -jnp.exp(A_log)
        dt = jax.nn.softplus(dt_raw + dt_bias)
        nc = L // CHUNK
        hpg = NHEADS // NGROUPS
        xc = x.reshape(B, nc, CHUNK, NHEADS, D_HEAD)
        Bc = jnp.repeat(Bm.reshape(B, nc, CHUNK, NGROUPS, D_STATE), hpg, axis=3)
        Cc = jnp.repeat(Cm.reshape(B, nc, CHUNK, NGROUPS, D_STATE), hpg, axis=3)
        dtc = dt.reshape(B, nc, CHUNK, NHEADS)
        dA = dtc * A
        cum = jnp.cumsum(dA, axis=2)
        tril = jnp.tril(jnp.ones((CHUNK, CHUNK), bool))
        seg = cum[:, :, :, None, :] - cum[:, :, None, :, :]
        Lmat = jnp.exp(jnp.where(tril[None, None, :, :, None], seg, -jnp.inf))
        CB = jnp.einsum('bclhn,bcshn->bclsh', Cc, Bc)
        M = CB * Lmat * dtc[:, :, None, :, :]
        Y_intra = jnp.einsum('bclsh,bcshp->bclhp', M, xc)
        decay_states = jnp.exp(cum[:, :, -1:, :] - cum)
        S = jnp.einsum('bclhn,bclh,bclhp->bchpn', Bc, decay_states * dtc, xc)
        chunk_decay = jnp.exp(cum[:, :, -1, :])

        def step(carry, inp):
            d, s = inp
            new = carry * d[:, :, None, None] + s
            return (new, carry)
        init = jnp.zeros((B, NHEADS, D_HEAD, D_STATE), u.dtype)
        _, prev = jax.lax.scan(step, init, (jnp.moveaxis(chunk_decay, 1, 0), jnp.moveaxis(S, 1, 0)))
        prev = jnp.moveaxis(prev, 0, 1)
        Y_inter = jnp.einsum('bclhn,bclh,bchpn->bclhp', Cc, jnp.exp(cum), prev)
        y = (Y_intra + Y_inter).reshape(B, L, NHEADS, D_HEAD) + D[None, None, :, None] * x
        y = y.reshape(B, L, D_SSM)
        yg = y * _silu(z)
        var = jnp.mean(yg * yg, axis=-1, keepdims=True)
        y = yg * jax.lax.rsqrt(var + EPS) * norm_w
        return y @ W_out.T

    def _L0_ffn_ref(x, shared_w1, shared_w2, experts_w1, experts_w2, gate_w):
        import jax, jax.numpy as jnp
        import numpy as np
        D_MODEL = 128
        N_EXPERTS = 8
        TOP_K = 2
        HIDDEN = 4 * D_MODEL
        B, S, D = x.shape
        T = B * S
        x_flat = x.reshape(T, D)
        shared = jnp.einsum('td,dh->th', x_flat, shared_w1.T)
        shared = jnp.einsum('th,hd->td', jax.nn.silu(shared), shared_w2.T)
        gate_logits = x_flat @ gate_w.T
        top_k_gates, top_k_idx = jax.lax.top_k(gate_logits, TOP_K)
        top_k_gates = jax.nn.softmax(top_k_gates, axis=1)
        gates = jnp.zeros((T, N_EXPERTS), dtype=x.dtype)
        gates = gates.at[jnp.arange(T)[:, None], top_k_idx].set(top_k_gates)
        h = jnp.einsum('td,ehd->teh', x_flat, experts_w1)
        expert_out = jnp.einsum('teh,edh->ted', jax.nn.silu(h), experts_w2)
        selected = jnp.einsum('ted,te->td', expert_out, gates)
        return (shared + selected).reshape(B, S, D)
    x = L0_attn_a_x
    x = x + _L0_attn_a_ref(_layernorm(x, axis=-1), L0_attn_a_Wq, L0_attn_a_Wk, L0_attn_a_Wv, L0_attn_a_Wo, L0_attn_a_bo)
    x = x + _L0_ffn_ref(_layernorm(x, axis=-1), L0_ffn_shared_w1, L0_ffn_shared_w2, L0_ffn_experts_w1, L0_ffn_experts_w2, L0_ffn_gate_w)
    x = x + _L0_attn_b_ref(_layernorm(x, axis=-1), L0_attn_b_W_in, L0_attn_b_conv_w, L0_attn_b_conv_b, L0_attn_b_dt_bias, L0_attn_b_A_log, L0_attn_b_D, L0_attn_b_norm_w, L0_attn_b_W_out)
    x = x + _L0_ffn_ref(_layernorm(x, axis=-1), L0_ffn_shared_w1, L0_ffn_shared_w2, L0_ffn_experts_w1, L0_ffn_experts_w2, L0_ffn_gate_w)
    return x

_drawn_inputs = setup_inputs


def setup_inputs(seed=0):
    import zlib

    import numpy as np

    out = dict(_drawn_inputs(seed))
    spreads = {'L0_attn_a_bo': (0.0, 0.1), 'L0_attn_b_D': (1.0, 0.2), 'L0_attn_b_norm_w': (1.0, 0.2)}
    factors = {'L0_attn_a_Wq': 8.0, 'L0_attn_a_Wk': 8.0, 'L0_attn_b_A_log': 6.824}
    for name, (base, spread) in spreads.items():
        noise = np.random.default_rng([zlib.crc32(name.encode()), seed]).standard_normal(out[name].shape)
        drawn = base * np.exp(spread * noise) if base else spread * noise
        out[name] = jnp.asarray(drawn.astype(out[name].dtype))
    for name, factor in factors.items():
        out[name] = (out[name] * factor).astype(out[name].dtype)
    return out
```

```python
from contextlib import ExitStack

import numpy as np
import concourse.bass as bass
from concourse import mybir
from concourse.alu_op_type import AluOpType as ALU

F32 = mybir.dt.float32
BF16 = mybir.dt.bfloat16
I32 = mybir.dt.int32
U32 = mybir.dt.uint32
ACT = mybir.ActivationFunctionType
AX = mybir.AxisListType

P = 128
B, N, D = 8, 256, 128
T = B * N // P
TB = N // P
H, DH = 16, 64
PAIRS = H // 2
EPS = 1e-5
SCALE = DH ** -0.5
LARGE = 3.0e38


def phase_semaphore(nc, sems, name):
    sems.append(nc.alloc_semaphore(name))
    return sems[-1]


def end_phase(nc, sems):
    nc.clear_and_free_semaphores(sems)
    nc.all_engine_barrier()
    sems.clear()


def attention_steps(has_next):
    s = []
    for p in range(PAIRS):
        s.append(("scores", p))
        if p >= 1:
            s.append(("turn", p - 1))
        s.append(("exps", p))
        if p >= 2:
            s.append(("values", p - 2))
        if p >= 3:
            s.append(("outT", p - 3))
        if has_next and p == 3:
            s.append(("stats", 0))
        if has_next and p == 4:
            s.append(("norm", 0))
        if has_next and p == 5:
            s.append(("xT", 0))
    jobs = [("job", j) for j in range(20)] if has_next else []
    s += jobs[0:3] + [("turn", 7), ("values", 6), ("outT", 5)]
    s += jobs[3:8] + [("values", 7), ("outT", 6)] + jobs[8:16] + [("outT", 7)] + jobs[16:20]
    return s + [("project", 0)]


def attention_phase(nc, sems, dram, X, w):
    QW = 3 * P
    JOBS = 20
    with ExitStack() as ctx:
        def sb(name, shape, dt=F32):
            return ctx.enter_context(nc.sbuf_tensor(name, shape, dt))

        def sem(name):
            return phase_semaphore(nc, sems, name)

        wq = sb("wq", [P, H * DH])
        wk = sb("wk", [P, H * DH])
        wv = sb("wv", [P, H * DH])
        wo = sb("wo", [P, PAIRS, D])
        bo = sb("bo", [P, D])
        ident = sb("ident", [P, P])
        rel_i = sb("rel_i", [P, QW], I32)
        rel = sb("rel", [P, QW])
        relm = sb("relm", [P, QW])
        bias = sb("bias", [P, H, QW])
        XB = sb("XB", [P, T, D])
        stats = sb("stats", [P, TB, 6])
        mv = sb("mv", [P, TB, 2])
        veps = sb("veps", [P, TB])
        half = sb("half", [P, TB])
        rstd = sb("rstd", [P, TB])
        xn = sb("xn", [P, TB, D])
        xT = sb("xT", [P, N])
        qT = sb("qT", [P, PAIRS, N])
        kT = sb("kT", [P, PAIRS, N])
        V = sb("V", [P, TB, H, DH + 1])
        S = sb("S", [P, 4, QW])
        low = sb("low", [P, 4, 2])
        E = sb("E", [P, 4, QW])
        ET = sb("ET", [P, 2, 2, QW])
        rden = sb("rden", [P, 2, 4])
        O = sb("O", [P, TB, H * DH])
        OT = sb("OT", [P, PAIRS, N])
        bank = [ctx.enter_context(nc.psum_tensor(f"bank{i}", [P, 512], F32)) for i in range(8)]
        turned = [bank[4], bank[5]]
        O_ps, side = bank[6], bank[7]
        job_bank = [bank[7], bank[0], bank[1]]

        clear = sb("clear", [P, 3, D])

        later_in = sem("later_in")
        clear_ok = sem("clear_ok")
        x_in = sem("x_in")
        w_in = sem("w_in")
        wo_in = sem("wo_in")
        bo_in = sem("bo_in")
        consts = sem("consts")
        bias_ok = sem("bias_ok")
        xb_ok = sem("xb_ok")
        mean_ok = sem("mean_ok")
        stat_ok = sem("stat_ok")
        var_ok = sem("var_ok")
        rstd_ok = sem("rstd_ok")
        xn_ok = sem("xn_ok")
        s_ok = sem("s_ok")
        low_ok = sem("low_ok")
        e_ok = sem("e_ok")
        et_ps = sem("et_ps")
        et_even = sem("et_even")
        et_odd = sem("et_odd")
        o_ps = sem("o_ps")
        rden_ok = sem("rden_ok")
        o_ok = sem("o_ok")
        side_ps = sem("side_ps")
        side_ok = sem("side_ok")
        job_ps = sem("job_ps")
        job_act = sem("job_act")
        job_dve = sem("job_dve")
        y_ps = sem("y_ps")
        x_ok = sem("x_ok")
        passed = sem("passed")

        STEPS = attention_steps(True)
        LAST = attention_steps(False)
        SIDES = PAIRS + 1

        def side_index(step, p, steps):
            return 3 if step == "xT" else p + (p > 2 and steps is STEPS)

        TURN_BEFORE_JOB = {0: 4, 3: 5, 9: 6, 18: 7}
        JOB_BEFORE_TURN = {5: 0, 6: 6, 7: 15}

        with nc.Block() as block:
            @block.sync
            def _(sp):
                for g in range(2):
                    sp.dma_start(X[:, 8 * g:8 * g + 8, :],
                                 dram["x"].rearrange("(t p) d -> p t d", p=P)[:, 8 * g:8 * g + 8, :])\
                      .then_inc(x_in, 16)
                    if g == 0:
                        sp.wait_ge(x_in, 16)
                sp.dma_start(wo[:, :, :], dram["wo"].rearrange("(c p) d -> p c d", p=P)).then_inc(wo_in, 16)
                for name in w:
                    sp.dma_start(w[name][:, :], dram[name]).then_inc(later_in, 16)
                sp.wait_ge(clear_ok, 1)
                for j in range(0, NSLOT, 3):
                    sp.dma_start(dram["slots_x"][j * P:j * P + 3 * P, :].rearrange("(t p) d -> p t d", p=P),
                                 clear[:, :, :]).then_inc(later_in, 16)
                sp.wait_ge(later_in, 16 * (len(w) + NSLOT // 3))

            @block.gpsimd
            def _(pool):
                pool.dma_start(bo[:, :], dram["bo"].rearrange("(a d) -> a d", a=1).broadcast_to([P, D]))\
                    .then_inc(bo_in, 16)
                pool.memset(clear[:, :, :], 0.0).then_inc(clear_ok, 1)
                pool.memset(ident[:, :], 1.0).then_inc(consts, 1)
                pool.wait_ge(consts, 1)
                pool.affine_select(out=ident[:, :], in_=ident[:, :], compare_op=ALU.is_equal, fill=0.0,
                                   base=0, pattern=[[-1, P]], channel_multiplier=1).then_inc(consts, 1)
                pool.memset(half[:, :], -0.5).then_inc(consts, 1)
                pool.memset(V[:, :, :, DH:DH + 1], 1.0).then_inc(consts, 1)
                pool.iota(rel_i[:, 0:P], [[-1, P]], base=0, channel_multiplier=1).then_inc(consts, 1)
                pool.iota(rel_i[:, P:QW], [[-1, N]], base=P, channel_multiplier=1).then_inc(consts, 1)
                pool.wait_ge(consts, 6)
                pool.tensor_copy(rel[:, :], rel_i[:, :]).then_inc(consts, 1)
                pool.wait_ge(consts, 7)
                pool.affine_select(out=relm[:, 0:P], in_=rel[:, 0:P], compare_op=ALU.is_ge, fill=-1e33,
                                   base=0, pattern=[[-1, P]], channel_multiplier=1).then_inc(consts, 1)
                pool.affine_select(out=relm[:, P:QW], in_=rel[:, P:QW], compare_op=ALU.is_ge, fill=-1e33,
                                   base=P, pattern=[[-1, N]], channel_multiplier=1).then_inc(consts, 1)
                pool.wait_ge(consts, 9)
                root = np.float32((2.0 ** 8) ** (1.0 / H))
                slopes = (np.float32(1.0) / root ** np.arange(1, H + 1, dtype=np.float32)) / np.float32(SCALE)

                def reciprocal_root(b):
                    pool.wait_ge(var_ok, b + 1)
                    pool.tensor_tensor(rstd[:, :], veps[:, :], half[:, :], ALU.pow).then_inc(rstd_ok, 1)

                reciprocal_root(0)
                for h in range(H):
                    pool.tensor_scalar(bias[:, h, :], relm[:, :], float(slopes[h]), None, ALU.mult)\
                        .then_inc(bias_ok, 1)
                pool.wait_ge(bo_in, 16)
                pool.wait_ge(x_in, 32)
                pool.tensor_tensor(XB[:, :, :], X[:, :, :],
                                   bo[:, :].rearrange("p (a d) -> p a d", a=1).broadcast_to([P, T, D]),
                                   ALU.add).then_inc(xb_ok, 1)
                with pool.Fori(1, B) as b:
                    reciprocal_root(b)

            @block.vector
            def _(dve):
                def row_stats(b):
                    for t in range(TB):
                        dve.bn_stats(stats[:, t, :], X[:, bass.ds(b * TB + t, 1), :]).then_inc(mean_ok, 1)
                    dve.wait_ge(x_in, 32)
                    dve.wait_ge(mean_ok, b * 4 + 2)
                    dve.sem_inc(passed, 1)
                    for t in range(TB):
                        dve.bn_aggr(mv[:, t, :], stats[:, t, :]).then_inc(mean_ok, 1)
                    dve.wait_ge(mean_ok, b * 4 + 4)
                    dve.tensor_scalar(veps[:, :], mv[:, :, 1], EPS, None, ALU.add).then_inc(var_ok, 1)

                def row_norm(b):
                    dve.wait_ge(rstd_ok, b + 1)
                    for t in range(TB):
                        last = dve.tensor_scalar(xn[:, t, :], X[:, bass.ds(b * TB + t, 1), :],
                                                 mv[:, t, 0:1], rstd[:, t:t + 1], ALU.subtract, ALU.mult)
                    last.then_inc(xn_ok, 1)

                def project_out(b, j):
                    if j % 2 == 0:
                        return
                    dve.wait_ge(job_ps, b * JOBS + j + 1)
                    copy_job(dve.tensor_copy, j).then_inc(job_dve, 1)

                def copy_job(copy, j):
                    ps = job_bank[j % 3]
                    if j < 16:
                        dst = qT if j % 4 in (0, 3) else kT
                        return copy(dst[:, j // 2, :], ps[:, 0:N])
                    t, half_v = (j - 16) // 2, (j - 16) % 2
                    return copy(V[:, t, 8 * half_v:8 * half_v + 8, 0:DH],
                                ps[:, :].rearrange("p (h d) -> p h d", d=DH))

                def run(b, steps):
                    for step, p in steps:
                        if step == "scores":
                            for h in (2 * p, 2 * p + 1):
                                dve.wait_ge(bias_ok, h + 1)
                                dve.wait_ge(s_ok, b * H + h + 1)
                                if h >= 4:
                                    dve.wait_ge(e_ok, b * H + h - 3)
                                dve.sem_inc(passed, 1)
                                sc = bank[2 * (p % 2) + h % 2]
                                for q, (c0, c1) in enumerate(((0, P), (P, QW))):
                                    last = dve.tensor_tensor_reduce(
                                        S[:, h % 4, c0:c1], sc[:, c0:c1], bias[:, h, c0:c1], -SCALE, LARGE,
                                        ALU.add, ALU.min, low[:, h % 4, q:q + 1])
                                last.then_inc(low_ok, 1)
                        elif step == "turn":
                            dve.wait_ge(et_ps, b * H + 2 * p + 2)
                            if p >= 2:
                                dve.wait_ge(o_ps, b * PAIRS + p - 1)
                            dve.tensor_copy(ET[:, p % 2, 1, :], turned[1][:, 0:QW]).then_inc(et_odd, 1)
                        elif step == "values":
                            dve.wait_ge(o_ps, b * PAIRS + p + 1)
                            ov = O_ps[:, 0:4 * (DH + 1)].rearrange("p (h t d) -> p t h d", h=2, t=TB)
                            dve.reciprocal(rden[:, p % 2, :].rearrange("p (t h) -> p t h", t=TB),
                                           ov[:, :, :, DH]).then_inc(rden_ok, 1)
                            dve.wait_ge(rden_ok, b * PAIRS + p + 1)
                            for t in range(TB):
                                last = dve.tensor_tensor(
                                    O[:, t, P * p:P * p + P].rearrange("p (h d) -> p h d", h=2),
                                    ov[:, t, :, 0:DH],
                                    rden[:, p % 2, 2 * t:2 * t + 2].rearrange("p (h a) -> p h a", a=1)
                                    .broadcast_to([P, 2, DH]), ALU.mult)
                            last.then_inc(o_ok, 1)
                        elif step == "stats":
                            row_stats(b + 1)
                        elif step == "norm":
                            row_norm(b + 1)
                        elif step == "job":
                            project_out(b + 1, p)
                        elif step == "project":
                            dve.wait_ge(y_ps, b + 1)
                            dve.wait_ge(xb_ok, 1)
                            dve.tensor_tensor(X[:, bass.ds(b * TB, TB), :],
                                              O_ps[:, 0:TB * D].rearrange("p (t d) -> p t d", t=TB),
                                              XB[:, bass.ds(b * TB, TB), :], ALU.add).then_inc(x_ok, 1)

                dve.sem_inc(x_ok, 1)
                dve.wait_ge(x_in, 16)
                row_stats(0)
                row_norm(0)
                for j in range(JOBS):
                    project_out(0, j)
                with dve.Fori(0, B - 1) as b:
                    run(b, STEPS)
                run(B - 1, LAST)

            @block.scalar
            def _(act):
                act.dma_start(wq[:, :], dram["wq"]).then_inc(w_in, 16)
                act.wait_ge(w_in, 16)
                act.dma_start(wk[:, :], dram["wk"]).then_inc(w_in, 16)
                act.wait_ge(w_in, 32)
                act.dma_start(wv[:, :], dram["wv"]).then_inc(w_in, 16)

                def job_out(b, j):
                    if j % 2:
                        return
                    act.wait_ge(job_ps, b * JOBS + j + 1)
                    ps = job_bank[j % 3]
                    if j < 16:
                        dst = qT if j % 4 in (0, 3) else kT
                        act.activation(dst[:, j // 2, :], ps[:, 0:N], ACT.Copy).then_inc(job_act, 1)
                    else:
                        t, half_v = (j - 16) // 2, (j - 16) % 2
                        act.activation(V[:, t, 8 * half_v:8 * half_v + 8, 0:DH],
                                       ps[:, :].rearrange("p (h d) -> p h d", d=DH), ACT.Copy)\
                           .then_inc(job_act, 1)

                def side_out(b, step, p, dst, steps):
                    act.wait_ge(side_ps, b * SIDES + side_index(step, p, steps) + 2)
                    act.activation(dst, side[:, 0:N], ACT.Copy).then_inc(side_ok, 1)

                def run(b, steps):
                    for step, p in steps:
                        if step == "exps":
                            for h in (2 * p, 2 * p + 1):
                                act.wait_ge(low_ok, b * H + h + 1)
                                if h >= 4:
                                    act.wait_ge(et_ps, b * H + h - 3)
                                for q, (c0, c1) in enumerate(((0, P), (P, QW))):
                                    last = act.activation(E[:, h % 4, c0:c1], S[:, h % 4, c0:c1], ACT.Exp,
                                                          bias=low[:, h % 4, q:q + 1], scale=-1.0)
                                last.then_inc(e_ok, 1)
                        elif step == "turn":
                            act.wait_ge(et_ps, b * H + 2 * p + 1)
                            if p >= 2:
                                act.wait_ge(o_ps, b * PAIRS + p - 1)
                            act.activation(ET[:, p % 2, 0, :], turned[0][:, 0:QW], ACT.Copy)\
                               .then_inc(et_even, 1)
                        elif step == "outT":
                            side_out(b, step, p, OT[:, p, :], steps)
                        elif step == "xT":
                            side_out(b, step, p, xT[:, :], steps)
                        elif step == "job":
                            job_out(b + 1, p)

                act.wait_ge(side_ps, 1)
                act.activation(xT[:, :], side[:, 0:N], ACT.Copy).then_inc(side_ok, 1)
                for j in range(JOBS):
                    job_out(0, j)
                with act.Fori(0, B - 1) as b:
                    run(b, STEPS)
                run(B - 1, LAST)

            @block.tensor
            def _(pe):
                def transposes_x():
                    for t in range(TB):
                        last = pe.transpose(side[:, P * t:P * t + P], xn[:, t, :], ident[:, :])
                    last.then_inc(side_ps, 1)

                def job_free(b, j):
                    pe.wait_ge(job_dve if j % 2 else job_act, b * (JOBS // 2) + j // 2 + 1)

                def job(b, j):
                    if j >= 3:
                        job_free(b, j - 3)
                    ps = job_bank[j % 3]
                    if j < 16:
                        c = j // 2
                        w = wq if j % 4 in (0, 3) else wk
                        pe.matmul(ps[:, 0:N], w[:, P * c:P * c + P], xT[:, :], start=True, stop=True)\
                          .then_inc(job_ps, 1)
                    else:
                        t, half_v = (j - 16) // 2, (j - 16) % 2
                        pe.matmul(ps[:, :], xT[:, P * t:P * t + P], wv[:, 512 * half_v:512 * half_v + 512],
                                  start=True, stop=True).then_inc(job_ps, 1)

                def run(b, steps):
                    for step, p in steps:
                        if step == "scores":
                            if p == 0:
                                for j in (17, 18, 19):
                                    job_free(b, j)
                            if p >= 2:
                                pe.wait_ge(low_ok, b * H + 2 * p - 2)
                            for h in (2 * p, 2 * p + 1):
                                rows = slice(DH * (h % 2), DH * (h % 2) + DH)
                                sc = bank[2 * (p % 2) + h % 2]
                                pe.matmul(sc[:, 0:P], qT[rows, p, 0:P], kT[rows, p, 0:P], start=True, stop=True)
                                pe.matmul(sc[:, P:QW], qT[rows, p, P:N], kT[rows, p, :], start=True, stop=True)\
                                  .then_inc(s_ok, 1)
                        elif step == "turn":
                            for h in (2 * p, 2 * p + 1):
                                pe.wait_ge(e_ok, b * H + h + 1)
                                if p >= 1:
                                    pe.wait_ge(et_odd if h % 2 else et_even, b * PAIRS + p)
                                for k in range(3):
                                    last = pe.transpose(turned[h % 2][:, P * k:P * k + P],
                                                        E[:, h % 4, P * k:P * k + P], ident[:, :])
                                last.then_inc(et_ps, 1)
                        elif step == "values":
                            if p == 0:
                                pe.wait_ge(x_ok, b + 1)
                            else:
                                pe.wait_ge(o_ok, b * PAIRS + p)
                            pe.wait_ge(et_even, b * PAIRS + p + 1)
                            pe.wait_ge(et_odd, b * PAIRS + p + 1)
                            for e in range(2):
                                h = 2 * p + e
                                for t in range(TB):
                                    c = (2 * e + t) * (DH + 1)
                                    for k in range(t + 1):
                                        last = pe.matmul(O_ps[:, c:c + DH + 1],
                                                         ET[:, p % 2, e, P * (t + k):P * (t + k) + P],
                                                         V[:, k, h, :], start=(k == 0), stop=(k == t))
                            last.then_inc(o_ps, 1)
                        elif step == "outT":
                            pe.wait_ge(o_ok, b * PAIRS + p + 1)
                            pe.wait_ge(side_ok, b * SIDES + side_index(step, p, steps) + 1)
                            if p in JOB_BEFORE_TURN and steps is STEPS:
                                job_free(b + 1, JOB_BEFORE_TURN[p])
                            for t in range(TB):
                                last = pe.transpose(side[:, P * t:P * t + P], O[:, t, P * p:P * p + P], ident[:, :])
                            last.then_inc(side_ps, 1)
                        elif step == "xT":
                            pe.wait_ge(xn_ok, b + 2)
                            pe.wait_ge(side_ok, b * SIDES + side_index(step, p, steps) + 1)
                            transposes_x()
                        elif step == "job":
                            if p in TURN_BEFORE_JOB:
                                pe.wait_ge(side_ok, b * SIDES + side_index("outT", TURN_BEFORE_JOB[p], steps) + 2)
                            job(b + 1, p)
                        elif step == "project":
                            pe.wait_ge(side_ok, b * SIDES + SIDES + (steps is STEPS))
                            pe.wait_ge(o_ok, b * PAIRS + PAIRS)
                            pe.wait_ge(wo_in, 16)
                            for t in range(TB):
                                for c in range(PAIRS):
                                    last = pe.matmul(O_ps[:, D * t:D * t + D], OT[:, c, P * t:P * t + P],
                                                     wo[:, c, :], start=(c == 0), stop=(c == PAIRS - 1))
                            last.then_inc(y_ps, 1)

                pe.wait_ge(consts, 9)
                pe.wait_ge(xn_ok, 1)
                transposes_x()
                pe.wait_ge(side_ok, 1)
                pe.wait_ge(w_in, 48)
                for j in range(JOBS):
                    job(0, j)
                with pe.Fori(0, B - 1) as b:
                    run(b, STEPS)
                run(B - 1, LAST)


E_N = 8
HID = 512
HC = HID // P
NSLOT = 2 * B * N // P + E_N - 1
LAYERS = 2


def ffn_phase(nc, sems, dram, X, w, layer):
    GROUP = 4
    with ExitStack() as ctx:
        def sb(name, shape, dt=F32):
            return ctx.enter_context(nc.sbuf_tensor(f"f{layer}_{name}", shape, dt))

        def sem(name):
            return phase_semaphore(nc, sems, f"f{layer}_{name}")

        stats = sb("stats", [P, T, 6])
        mv = sb("mv", [P, T, 2])
        veps = sb("veps", [P, T])
        half = sb("half", [P, T])
        rstd = sb("rstd", [P, T])
        xn = sb("xn", [P, T, D])
        xT = sb("xT", [P, T * P])
        ident = sb("ident", [P, P])
        prior_i = sb("prior_i", [P, E_N], I32)
        prior = sb("prior", [P, E_N])
        tile_i = sb("tile_i", [1, NSLOT], I32)
        tile_no = sb("tile_no", [1, NSLOT])
        below_f = sb("below_f", [P, P])
        below = sb("below", [P, P], BF16)
        ones = sb("ones", [P, P], BF16)
        L = sb("L", [P, T, E_N])
        eq = sb("eq", [P, T, E_N])
        rank = sb("rank", [P, T, E_N])
        first = sb("first", [P, T, E_N])
        second = sb("second", [P, T, E_N])
        best = sb("best", [P, 2, T])
        top = sb("top", [P, 2, T])
        gap = sb("gap", [P, T])
        ratio = sb("ratio", [P, T])
        gate = sb("gate", [P, 2, T])
        picked = sb("picked", [P, 2 * T + 1, E_N], BF16)
        count = sb("count", [P, E_N])
        count_i = sb("count_i", [P, E_N], I32)
        tiles_i = sb("tiles_i", [P, E_N], I32)
        tiles = sb("tiles", [P, E_N])
        one8 = sb("one8", [P, E_N])
        ends = sb("ends", [P, E_N])
        starts = sb("starts", [P, E_N])
        place = sb("place", [P, T, E_N])
        slot = sb("slot", [P, 2, T])
        slot_i = sb("slot_i", [P, 2, T], I32)
        after = sb("after", [1, NSLOT, E_N])
        tile_e = sb("tile_e", [1, NSLOT])
        tile_w = sb("tile_w", [1, NSLOT], I32)
        hT_s = sb("hT_s", [P, 2, HC, GROUP * P])
        xg = sb("xg", [P, 2, D])
        xgT = sb("xgT", [P, 2, P])
        hs = sb("hs", [P, 2, HID])
        hT = sb("hT", [P, 2, HID])
        yo = sb("yo", [P, 2, D])
        G = sb("G", [P, 2, T, D])
        bank = [ctx.enter_context(nc.psum_tensor(f"f{layer}_bank{i}", [P, 512], F32)) for i in range(8)]

        consts = sem("consts")
        stat = sem("stat")
        var_ok = sem("var_ok")
        rstd_ok = sem("rstd_ok")
        xn_ok = sem("xn_ok")
        xT_ps = sem("xT_ps")
        xT_ok = sem("xT_ok")
        logit_ps = sem("logit_ps")
        gap_ok = sem("gap_ok")
        ratio_ok = sem("ratio_ok")
        picked_ok = sem("picked_ok")
        place_ps = sem("place_ps")
        slot_ok = sem("slot_ok")
        tile_ok = sem("tile_ok")
        sent = sem("sent")
        sh_ps = sem("sh_ps")
        sh_ok = sem("sh_ok")
        so_ps = sem("so_ps")
        so_ok = sem("so_ok")
        xg_in = [sem(f"xg_in{i}") for i in range(2)]
        y_out = [sem(f"y_out{i}") for i in range(2)]
        xt_ps = sem("xt_ps")
        xt_ok = sem("xt_ok")
        h_ps = sem("h_ps")
        hs_ok = sem("hs_ok")
        ht_ps = sem("ht_ps")
        ht_ok = sem("ht_ok")
        y_ps = sem("y_ps")
        y_ok = sem("y_ok")
        back = [sem(f"back{t}") for t in range(T)]
        x_ok = sem("x_ok")

        slots_x, slots_y = dram["slots_x"], dram["slots_y"]
        J = NSLOT

        with nc.Block() as block:
            @block.sync
            def _(sp):
                def load(j, n):
                    sp.dma_start(xg[:, n % 2, :], slots_x[bass.ds(j * P, P), :]).then_inc(xg_in[n % 2], 16)

                def step(j, n):
                    if n + 2 < J:
                        sp.wait_ge(xt_ps, j + 1)
                        load(j + 2, n)
                    if n >= 2:
                        sp.wait_ge(y_ok, j - 1)
                        sp.dma_start(slots_y[bass.ds((j - 2) * P, P), :], yo[:, n % 2, :])\
                          .then_inc(y_out[n % 2], 16)

                sp.wait_ge(sent, 16 * 2 * T)
                load(0, 0)
                load(1, 1)
                for j in range(3):
                    step(j, j)
                with sp.Fori(0, (J - 5) // 2) as i:
                    step(i * 2 + 3, 3)
                    step(i * 2 + 4, 4)
                for j in range(J - 2, J + 2):
                    step(j, j)

            @block.gpsimd
            def _(pool):
                pool.memset(ident[:, :], 1.0).then_inc(consts, 1)
                pool.memset(below_f[:, :], 1.0).then_inc(consts, 1)
                pool.memset(half[:, :], -0.5).then_inc(consts, 1)
                pool.memset(ones[:, :], 1.0).then_inc(consts, 1)
                pool.memset(picked[:, :, :], 0.0).then_inc(consts, 1)
                pool.iota(prior_i[:, :], [[-1, E_N]], base=E_N, channel_multiplier=0).then_inc(consts, 1)
                pool.iota(tile_i[:, :], [[1, NSLOT]], base=0, channel_multiplier=0).then_inc(consts, 1)
                pool.memset(one8[:, :], 1.0).then_inc(consts, 1)
                pool.wait_ge(consts, 8)
                pool.affine_select(out=ident[:, :], in_=ident[:, :], compare_op=ALU.is_equal, fill=0.0,
                                   base=0, pattern=[[-1, P]], channel_multiplier=1).then_inc(consts, 1)
                pool.affine_select(out=below[:, :], in_=below_f[:, :], compare_op=ALU.is_gt, fill=0.0,
                                   base=0, pattern=[[1, P]], channel_multiplier=-1).then_inc(consts, 1)
                pool.tensor_copy(prior[:, :], prior_i[:, :]).then_inc(consts, 1)
                pool.tensor_copy(tile_no[:, :], tile_i[:, :]).then_inc(consts, 1)
                pool.wait_ge(var_ok, 1)
                pool.tensor_tensor(rstd[:, :], veps[:, :], half[:, :], ALU.pow).then_inc(rstd_ok, 1)
                pool.wait_ge(slot_ok, 1)
                for t in range(T):
                    for k in range(2):
                        pool.indirect_dma_start(
                            slots_x, bass.IndirectOffsetOnAxis(ap=slot_i[:, k, t:t + 1].bitcast(U32), axis=0),
                            xn[:, t, :], None).then_inc(sent, 16)
                for n in range(2):
                    pool.wait_ge(y_out[n], 16 * ((J + 1 - n) // 2))
                for t in range(T):
                    for k in range(2):
                        pool.indirect_dma_start(
                            G[:, k, t, :], None, slots_y,
                            bass.IndirectOffsetOnAxis(ap=slot_i[:, k, t:t + 1].bitcast(U32), axis=0))\
                            .then_inc(back[t], 16)

            @block.vector
            def _(dve):
                n = 0

                def chain(instruction):
                    nonlocal n
                    n += 1
                    instruction.then_inc(stat, 1)
                    dve.wait_ge(stat, n)

                def spread(x, k):
                    return x.rearrange("p (t a) -> p t a", a=1).broadcast_to([P, T, k])

                dve.wait_ge(consts, 12)
                with dve.Fori(0, T) as t:
                    dve.bn_stats(stats[:, bass.ds(t, 1), :], X[:, bass.ds(t, 1), :]).then_inc(stat, 1)
                dve.wait_ge(stat, T)
                for t in range(T):
                    dve.bn_aggr(mv[:, t, :], stats[:, t, :]).then_inc(stat, 1)
                n = 2 * T
                dve.wait_ge(stat, n)
                dve.tensor_scalar(veps[:, :], mv[:, :, 1], EPS, None, ALU.add).then_inc(var_ok, 1)
                dve.wait_ge(rstd_ok, 1)
                with dve.Fori(0, T) as t:
                    dve.tensor_scalar(xn[:, bass.ds(t, 1), :], X[:, bass.ds(t, 1), :], mv[:, bass.ds(t, 1), 0],
                                      rstd[:, bass.ds(t, 1)], ALU.subtract, ALU.mult).then_inc(xn_ok, 1)
                for g in range(2):
                    dve.wait_ge(xT_ps, 2 * g + 2)
                    dve.tensor_copy(xT[:, 512 * (2 * g + 1):512 * (2 * g + 2)], bank[2 * g + 1][:, :])\
                       .then_inc(xT_ok, 1)

                dve.wait_ge(logit_ps, 1)
                pr = prior[:, :].rearrange("p (a e) -> p a e", a=1).broadcast_to([P, T, E_N])
                chain(dve.tensor_copy(L[:, :, :], bank[4][:, 0:T * E_N].rearrange("p (t e) -> p t e", e=E_N)))
                for k, choice in enumerate((first, second)):
                    chain(dve.tensor_reduce(best[:, k, :], L[:, :, :], AX.X, ALU.max))
                    chain(dve.tensor_tensor(eq[:, :, :], L[:, :, :], spread(best[:, k, :], E_N), ALU.is_equal))
                    chain(dve.tensor_tensor(rank[:, :, :], eq[:, :, :], pr, ALU.mult))
                    chain(dve.tensor_reduce(top[:, k, :], rank[:, :, :], AX.X, ALU.max))
                    chain(dve.tensor_tensor(choice[:, :, :], spread(top[:, k, :], E_N), pr, ALU.is_equal))
                    if k == 0:
                        chain(dve.scalar_tensor_tensor(out=L[:, :, :], in0=first[:, :, :], scalar=-LARGE,
                                                       in1=L[:, :, :], op0=ALU.mult, op1=ALU.add))
                dve.tensor_tensor(gap[:, :], best[:, 1, :], best[:, 0, :], ALU.subtract).then_inc(gap_ok, 1)
                dve.tensor_tensor(picked[:, T:2 * T, :], first[:, :, :], second[:, :, :], ALU.add)\
                   .then_inc(picked_ok, 1)
                dve.wait_ge(ratio_ok, 1)
                chain(dve.tensor_scalar(gap[:, :], ratio[:, :], 1.0, None, ALU.add))
                chain(dve.reciprocal(gate[:, 0, :], gap[:, :]))
                chain(dve.tensor_tensor(gate[:, 1, :], ratio[:, :], gate[:, 0, :], ALU.mult))

                dve.wait_ge(place_ps, 1)
                pl = bank[5][:, 0:T * E_N].rearrange("p (t e) -> p t e", e=E_N)
                chain(dve.tensor_scalar(count_i[:, :], bank[5][:, T * E_N:(T + 1) * E_N], float(P - 1), None,
                                        ALU.add))
                chain(dve.tensor_scalar(tiles_i[:, :], count_i[:, :], 7, None, ALU.logical_shift_right))
                chain(dve.tensor_copy(tiles[:, :], tiles_i[:, :]))
                chain(dve.tensor_tensor_scan(ends[:, :], one8[:, :], tiles[:, :], 0.0, ALU.mult, ALU.add))
                chain(dve.tensor_tensor(starts[:, :], ends[:, :], tiles[:, :], ALU.subtract))
                chain(dve.tensor_scalar(starts[:, :], starts[:, :], float(P), None, ALU.mult))
                chain(dve.tensor_tensor(place[:, :, :], pl,
                                        starts[:, :].rearrange("p (a e) -> p a e", a=1)
                                        .broadcast_to([P, T, E_N]), ALU.add))
                for k, choice in enumerate((first, second)):
                    chain(dve.tensor_tensor(rank[:, :, :], choice[:, :, :], place[:, :, :], ALU.mult))
                    chain(dve.tensor_reduce(slot[:, k, :], rank[:, :, :], AX.X, ALU.add))
                dve.tensor_copy(slot_i[:, :, :], slot[:, :, :]).then_inc(slot_ok, 1)
                chain(dve.tensor_tensor(
                    after[:, :, :], tile_no[:, :].rearrange("p (j a) -> p j a", a=1).broadcast_to([1, NSLOT, E_N]),
                    ends[0:1, :].rearrange("p (a e) -> p a e", a=1).broadcast_to([1, NSLOT, E_N]), ALU.is_ge))
                chain(dve.tensor_reduce(tile_e[:, :], after[:, :, :], AX.X, ALU.add))
                dve.tensor_scalar(tile_w[:, :], tile_e[:, :], float(E_N - 1), float(HID), ALU.min, ALU.mult)\
                   .then_inc(tile_ok, 1)

                dve.sem_inc(so_ok, 1)
                with dve.Fori(0, T // GROUP) as g:
                    dve.wait_ge(so_ps, g + 1)
                    Xg = X[:, bass.ds(GROUP * g, GROUP), :]
                    dve.tensor_tensor(Xg, bank[6][:, :].rearrange("p (t d) -> p t d", d=D), Xg, ALU.add)\
                       .then_inc(so_ok, 1)

                def turn_x(j, n):
                    dve.wait_ge(xt_ps, j + 1)
                    dve.tensor_copy(xgT[:, n % 2, :], bank[n % 2][:, 0:P]).then_inc(xt_ok, 1)

                def step(j, n):
                    if 1 <= n <= J:
                        dve.wait_ge(ht_ps, j)
                        if n >= 3:
                            dve.wait_ge(y_ps, j - 2)
                        dve.tensor_copy(hT[:, (n - 1) % 2, :], bank[4 + (n - 1) % 2][:, :]).then_inc(ht_ok, 1)
                    if n + 1 < J:
                        turn_x(j + 1, n + 1)

                turn_x(0, 0)
                for j in range(3):
                    step(j, j)
                with dve.Fori(0, (J - 5) // 2) as i:
                    step(i * 2 + 3, 3)
                    step(i * 2 + 4, 4)
                for j in range(J - 2, J + 2):
                    step(j, j)

                for t in range(T):
                    dve.wait_ge(back[t], 32)
                    for k in range(2):
                        dve.scalar_tensor_tensor(out=X[:, t, :], in0=G[:, k, t, :], scalar=gate[:, k, t:t + 1],
                                                 in1=X[:, t, :], op0=ALU.mult, op1=ALU.add).then_inc(x_ok, 1)
                        dve.wait_ge(x_ok, 2 * t + k + 1)

            @block.scalar
            def _(act):
                for g in range(2):
                    act.wait_ge(xT_ps, 2 * g + 1)
                    act.activation(xT[:, 1024 * g:1024 * g + 512], bank[2 * g][:, :], ACT.Copy).then_inc(xT_ok, 1)
                act.wait_ge(gap_ok, 1)
                act.activation(ratio[:, :], gap[:, :], ACT.Exp).then_inc(ratio_ok, 1)
                act.sem_inc(sh_ok, 1)
                with act.Fori(0, T // GROUP // 2) as pair:
                    for u in range(2):
                        g = pair * 2 + u
                        for c in range(HC):
                            act.wait_ge(sh_ps, g * HC + c + 1)
                            act.activation(hT_s[:, u, c, :], bank[c % 4][:, :], ACT.Silu).then_inc(sh_ok, 1)

                def step(j, n):
                    if n < J:
                        act.wait_ge(h_ps, j + 1)
                        if n >= 2:
                            act.wait_ge(ht_ps, j - 1)
                        act.activation(hs[:, n % 2, :], bank[2 + n % 2][:, :], ACT.Silu).then_inc(hs_ok, 1)
                    if n >= 2:
                        act.wait_ge(y_ps, j - 1)
                        if n >= 4:
                            act.wait_ge(y_out[n % 2], 16 * ((j - 2) // 2) if isinstance(j, int)
                                        else (j - n % 2 - 2) * 8)
                        act.activation(yo[:, n % 2, :], bank[6 + n % 2][:, 0:D], ACT.Copy).then_inc(y_ok, 1)

                for j in range(5):
                    step(j, j)
                with act.Fori(0, (J - 5) // 2) as i:
                    step(i * 2 + 5, 5)
                    step(i * 2 + 6, 6)
                for j in range(J, J + 2):
                    step(j, j)

            @block.tensor
            def _(pe):
                pe.wait_ge(consts, 12)
                pe.wait_ge(xn_ok, T)
                for t in range(T):
                    last = pe.transpose(bank[t // 4][:, P * (t % 4):P * (t % 4) + P], xn[:, t, :], ident[:, :])
                    if t % 4 == 3:
                        last.then_inc(xT_ps, 1)
                pe.wait_ge(xT_ok, 4)
                for t in range(T):
                    last = pe.matmul(bank[4][:, E_N * t:E_N * t + E_N], xT[:, P * t:P * t + P], w["gate"][:, :],
                                     start=True, stop=True)
                last.then_inc(logit_ps, 1)
                pe.wait_ge(picked_ok, 1)
                width = (T + 1) * E_N
                flat = picked[:, :, :].rearrange("p t e -> p (t e)")
                pe.matmul(bank[5][:, 0:width], below[:, :], flat[:, T * E_N:T * E_N + width], start=True, stop=False)
                with pe.Fori(1, T) as k:
                    pe.matmul(bank[5][:, 0:width], ones[:, :], flat[:, bass.ds((T - k) * E_N, width)],
                              start=False, stop=False)
                pe.matmul(bank[5][:, 0:width], ones[:, :], flat[:, 0:width], start=False, stop=True)\
                  .then_inc(place_ps, 1)

                with pe.Fori(0, T // GROUP // 2) as pair:
                    for u in range(2):
                        g = pair * 2 + u
                        for c in range(HC):
                            pe.wait_ge(sh_ok, g * HC + 1)
                            pe.matmul(bank[c][:, :], w["s1"][:, P * c:P * c + P],
                                      xT[:, bass.ds(g * GROUP * P, GROUP * P)], start=True, stop=True)\
                              .then_inc(sh_ps, 1)
                        pe.wait_ge(sh_ok, g * HC + HC + 1)
                        pe.wait_ge(so_ok, g + 1)
                        for t in range(GROUP):
                            for c in range(HC):
                                last = pe.matmul(bank[6][:, D * t:D * t + D], hT_s[:, u, c, P * t:P * t + P],
                                                 w["s2"][:, D * c:D * c + D], start=(c == 0), stop=(c == HC - 1))
                        last.then_inc(so_ps, 1)

                def turn_x(j, n):
                    pe.wait_ge(xg_in[n % 2], 16 * (j // 2 + 1) if isinstance(j, int) else (j - n % 2) * 8 + 16)
                    if n >= 2:
                        pe.wait_ge(xt_ok, j - 1)
                    pe.transpose(bank[n % 2][:, 0:P], xg[:, n % 2, :], ident[:, :]).then_inc(xt_ps, 1)

                def step(j, n):
                    if n < J:
                        pe.wait_ge(xt_ok, j + 1)
                        if n >= 2:
                            pe.wait_ge(hs_ok, j - 1)
                        e = pe.value_load(tile_w[0:1, bass.ds(j, 1)], min_val=0, max_val=(E_N - 1) * HID)
                        pe.matmul(bank[2 + n % 2][:, :], xgT[:, n % 2, :], w["e1"][:, bass.ds(e, HID)],
                                  start=True, stop=True).then_inc(h_ps, 1)
                    if 1 <= n <= J:
                        m = (n - 1) % 2
                        pe.wait_ge(hs_ok, j)
                        if n >= 3:
                            pe.wait_ge(ht_ok, j - 2)
                        for c in range(HC):
                            last = pe.transpose(bank[4 + m][:, P * c:P * c + P], hs[:, m, P * c:P * c + P],
                                                ident[:, :])
                        last.then_inc(ht_ps, 1)
                    if n >= 2:
                        pe.wait_ge(ht_ok, j - 1)
                        if n >= 4:
                            pe.wait_ge(y_ok, j - 3)
                        e = pe.value_load(tile_w[0:1, bass.ds(j - 2, 1)], min_val=0, max_val=(E_N - 1) * HID)
                        for c in range(HC):
                            last = pe.matmul(bank[6 + n % 2][:, 0:D], hT[:, n % 2, P * c:P * c + P],
                                             w["e2"][:, bass.ds(e + c * D, D)], start=(c == 0), stop=(c == HC - 1))
                        last.then_inc(y_ps, 1)
                    if n + 1 < J:
                        turn_x(j + 1, n + 1)

                pe.wait_ge(tile_ok, 1)
                pe.wait_ge(sh_ok, T // GROUP * HC + 1)
                pe.wait_ge(so_ok, T // GROUP + 1)
                turn_x(0, 0)
                for j in range(5):
                    step(j, j)
                with pe.Fori(0, (J - 7) // 2) as i:
                    step(i * 2 + 5, 5)
                    step(i * 2 + 6, 6)
                for j in range(J - 2, J + 2):
                    step(j, j)
NH = 4
HD = 64
CH = NH * HD
TAPS = 4


def mixer_phase(nc, sems, dram, X):
    ROWS = 2
    G = B // ROWS
    GT = ROWS * TB
    BLK = 3
    with ExitStack() as ctx:
        def sb(name, shape, dt=F32):
            return ctx.enter_context(nc.sbuf_tensor(f"m_{name}", shape, dt))

        def sem(name):
            return phase_semaphore(nc, sems, f"m_{name}")

        w_in = sb("w_in", [P, 3 * CH + NH])
        conv_w = sb("conv_w", [P, 4, TAPS])
        conv_b = sb("conv_b", [P, 4])
        dt_bias = sb("dt_bias", [P, NH])
        a_log = sb("a_log", [P, NH])
        d_skip = sb("d_skip", [P, NH])
        norm_w = sb("norm_w", [P, 2])
        w_out = sb("w_out", [P, 2, D])
        stats = sb("stats", [P, T, 6])
        mv = sb("mv", [P, T, 2])
        veps = sb("veps", [P, T])
        half = sb("half", [P, T])
        rstd = sb("rstd", [P, T])
        xn = sb("xn", [P, T, D])
        xT = sb("xT", [P, T * P])
        ident = sb("ident", [P, P])
        upto = sb("upto", [P, P])
        mask = sb("mask", [P, BLK, P])
        a_neg = sb("a_neg", [P, NH])
        raw = sb("raw", [P, T, NH])
        mag = sb("mag", [P, T, NH])
        small = sb("small", [P, T, NH])
        onep = sb("onep", [P, T, NH])
        step_ = sb("step_", [P, T, NH])
        inv = sb("inv", [P, T, NH])
        log1 = sb("log1", [P, T, NH])
        tiny = sb("tiny", [P, T, NH])
        dt = sb("dt", [P, T, NH])
        dA = sb("dA", [P, T * NH])
        cum = sb("cum", [P, T * NH])
        cum_rows = sb("cum_rows", [T * NH, P])
        spread = sb("spread", [P, T * NH, P])
        to_end = sb("to_end", [P, T * NH])
        z = sb("z", [P, T, CH])
        U = sb("U", [P, 4, ROWS, TAPS - 1 + N])
        acc = sb("acc", [P, 4, ROWS * N])
        xbc = sb("xbc", [P, 4, ROWS * N])
        xs = sb("xs", [P, GT, CH])
        xdt = sb("xdt", [P, GT, CH])
        xskip = sb("xskip", [P, GT, CH])
        cb = sb("cb", [P, ROWS, BLK, P])
        decay = sb("decay", [P, ROWS, BLK, NH, P])
        y = sb("y", [P, GT, CH])
        squares = sb("squares", [P, GT, CH])
        ssq = sb("ssq", [P, GT])
        msq = sb("msq", [P, GT])
        yr = sb("yr", [P, GT])
        yT = sb("yT", [P, 2, GT * P])
        bank = [ctx.enter_context(nc.psum_tensor(f"m_bank{i}", [P, 512], F32)) for i in range(8)]

        w_ok = sem("w_ok")
        p_in = sem("p_in")
        consts = sem("consts")
        stat = sem("stat")
        var_ok = sem("var_ok")
        rstd_ok = sem("rstd_ok")
        xn_ok = sem("xn_ok")
        xT_ps = sem("xT_ps")
        xT_ok = sem("xT_ok")
        dt_ps = sem("dt_ps")
        raw_ok = sem("raw_ok")
        small_ok = sem("small_ok")
        onep_ok = sem("onep_ok")
        log_ok = sem("log_ok")
        dA_ok = sem("dA_ok")
        cum_ps = sem("cum_ps")
        cum_ok = sem("cum_ok")
        rows_ps = sem("rows_ps")
        rows_ok = sem("rows_ok")
        rows_out = sem("rows_out")
        spread_in = sem("spread_in")
        end_ok = sem("end_ok")
        z_ps = sem("z_ps")
        z_ok = sem("z_ok")
        xbc_ps = sem("xbc_ps")
        tap_ok = sem("tap_ok")
        conv = sem("conv")
        xbc_ok = sem("xbc_ok")
        seg_ok = sem("seg_ok")
        min_ok = sem("min_ok")
        decay_ok = sem("decay_ok")
        x_ps = sem("x_ps")
        xs_ok = sem("xs_ok")
        xdt_ok = sem("xdt_ok")
        cb_ps = sem("cb_ps")
        cb_ok = sem("cb_ok")
        m_ok = sem("m_ok")
        skip_ok = sem("skip_ok")
        y_ps = sem("y_ps")
        y1_ok = sem("y1_ok")
        yg_ok = sem("yg_ok")
        ssq_ok = sem("ssq_ok")
        msq_ok = sem("msq_ok")
        yr_ok = sem("yr_ok")
        yT_ps = sem("yT_ps")
        yT_ok = sem("yT_ok")
        o_ps = sem("o_ps")
        x_ok = sem("x_ok")

        with nc.Block() as block:
            @block.sync
            def _(sp):
                for name, tile in (("w_in", w_in), ("conv_w", conv_w), ("conv_b", conv_b), ("norm_w", norm_w),
                                   ("w_out", w_out)):
                    sp.dma_start(tile[:], dram[name]).then_inc(w_ok, 16)
                for name, tile in (("dt_bias", dt_bias), ("a_log", a_log), ("d_skip", d_skip)):
                    sp.dma_start(tile[:, :], dram[name].broadcast_to([P, NH])).then_inc(p_in, 16)
                sp.wait_ge(rows_ok, 1)
                sp.dma_start(dram["cum_rows"], cum_rows[:, :]).then_inc(rows_out, 16)
                sp.wait_ge(rows_out, 16)
                for g in range(G):
                    r = GT * NH
                    sp.dma_start(spread[:, g * r:(g + 1) * r, :],
                                 dram["cum_rows"][g * r:(g + 1) * r, :].rearrange("(a r) l -> a r l", a=1)
                                 .broadcast_to([P, r, P])).then_inc(spread_in, 16)

            @block.gpsimd
            def _(pool):
                pool.memset(ident[:, :], 1.0).then_inc(consts, 1)
                pool.memset(upto[:, :], 1.0).then_inc(consts, 1)
                pool.memset(mask[:, :, :], 1.0).then_inc(consts, 1)
                pool.memset(half[:, :], -0.5).then_inc(consts, 1)
                pool.memset(U[:, :, :, 0:TAPS - 1], 0.0).then_inc(consts, 1)
                pool.wait_ge(consts, 5)
                pool.affine_select(out=ident[:, :], in_=ident[:, :], compare_op=ALU.is_equal, fill=0.0,
                                   base=0, pattern=[[-1, P]], channel_multiplier=1).then_inc(consts, 1)
                for tri in (upto[:, :], mask[:, 0, :], mask[:, 2, :]):
                    pool.affine_select(out=tri, in_=tri, compare_op=ALU.is_ge, fill=0.0,
                                       base=0, pattern=[[1, P]], channel_multiplier=-1).then_inc(consts, 1)
                pool.wait_ge(var_ok, 1)
                pool.tensor_tensor(rstd[:, :], veps[:, :], half[:, :], ALU.pow).then_inc(rstd_ok, 1)

                def over(x, n):
                    return x.rearrange("p (h a) -> p h a", a=1).broadcast_to([P, NH, n])

                def segments(g):
                    if not (isinstance(g, int) and g == 0):
                        pool.wait_ge(decay_ok, g * ROWS)
                        pool.wait_ge(y_ps, g)
                    for q in range(ROWS):
                        c0 = (g * GT + q * TB) * NH
                        near, far = bass.ds(c0, NH), bass.ds(c0 + NH, NH)
                        pool.tensor_tensor(decay[:, q, 0, :, :], spread[:, near, :], over(cum[:, near], P),
                                           ALU.subtract)
                        pool.tensor_tensor(decay[:, q, 1, :, :], spread[:, far, :], over(to_end[:, near], P),
                                           ALU.add)
                        pool.tensor_tensor(decay[:, q, 2, :, :], spread[:, far, :], over(cum[:, far], P),
                                           ALU.subtract).then_inc(seg_ok, 1)

                def skip(g):
                    pool.wait_ge(xs_ok, (g + 1) * 2)
                    pool.wait_ge(y1_ok, g * ROWS + 1)
                    for t in range(GT):
                        last = pool.tensor_tensor(xskip[:, t, :].rearrange("p (h d) -> p h d", h=NH),
                                                  xs[:, t, :].rearrange("p (h d) -> p h d", h=NH),
                                                  over(d_skip[:, :], HD), ALU.mult)
                    last.then_inc(skip_ok, 1)

                def mean_square(g):
                    pool.wait_ge(msq_ok, g + 1)
                    pool.wait_ge(x_ok, g * GT + 1)
                    pool.tensor_tensor(yr[:, :], msq[:, :], half[:, 0:GT], ALU.pow).then_inc(yr_ok, 1)

                pool.wait_ge(end_ok, 1)
                pool.wait_ge(p_in, 48)
                segments(0)

                def turn(g, has_next):
                    skip(g)
                    if has_next:
                        segments(g + 1)
                    mean_square(g)

                with pool.Fori(0, G - 1) as g:
                    turn(g, True)
                turn(G - 1, False)

            @block.vector
            def _(dve):
                n = 0

                def chain(instruction):
                    nonlocal n
                    n += 1
                    instruction.then_inc(stat, 1)
                    dve.wait_ge(stat, n)

                def every(x):
                    return x.rearrange("p (a h) -> p a h", a=1).broadcast_to([P, T, NH])

                with dve.Fori(0, T) as t:
                    dve.bn_stats(stats[:, bass.ds(t, 1), :], X[:, bass.ds(t, 1), :]).then_inc(stat, 1)
                dve.wait_ge(stat, T)
                for t in range(T):
                    dve.bn_aggr(mv[:, t, :], stats[:, t, :]).then_inc(stat, 1)
                n = 2 * T
                dve.wait_ge(stat, n)
                dve.tensor_scalar(veps[:, :], mv[:, :, 1], EPS, None, ALU.add).then_inc(var_ok, 1)
                dve.wait_ge(rstd_ok, 1)
                with dve.Fori(0, T) as t:
                    dve.tensor_scalar(xn[:, bass.ds(t, 1), :], X[:, bass.ds(t, 1), :], mv[:, bass.ds(t, 1), 0],
                                      rstd[:, bass.ds(t, 1)], ALU.subtract, ALU.mult).then_inc(xn_ok, 1)
                for g in range(2):
                    dve.wait_ge(xT_ps, 2 * g + 2)
                    dve.tensor_copy(xT[:, 512 * (2 * g + 1):512 * (2 * g + 2)], bank[2 * g + 1][:, :])\
                       .then_inc(xT_ok, 1)

                dve.wait_ge(dt_ps, 1)
                dve.wait_ge(p_in, 48)
                chain(dve.tensor_tensor(raw[:, :, :], bank[4][:, 0:T * NH].rearrange("p (t h) -> p t h", h=NH),
                                        every(dt_bias[:, :]), ALU.add))
                chain(dve.tensor_scalar(mag[:, :, :], raw[:, :, :], -1.0, None, ALU.mult))
                dve.tensor_tensor(mag[:, :, :], raw[:, :, :], mag[:, :, :], ALU.max).then_inc(raw_ok, 1)
                dve.wait_ge(small_ok, 2)
                dve.tensor_scalar(onep[:, :, :], small[:, :, :], 1.0, None, ALU.add).then_inc(onep_ok, 1)
                dve.wait_ge(onep_ok, 1)
                chain(dve.tensor_scalar(step_[:, :, :], onep[:, :, :], -1.0, None, ALU.add))
                chain(dve.tensor_scalar(tiny[:, :, :], step_[:, :, :], 0.0, None, ALU.is_equal))
                chain(dve.tensor_tensor(inv[:, :, :], step_[:, :, :], tiny[:, :, :], ALU.add))
                chain(dve.reciprocal(inv[:, :, :], inv[:, :, :]))
                chain(dve.tensor_tensor(inv[:, :, :], inv[:, :, :], small[:, :, :], ALU.mult))
                chain(dve.tensor_tensor(tiny[:, :, :], tiny[:, :, :], small[:, :, :], ALU.mult))
                chain(dve.scalar_tensor_tensor(out=tiny[:, :, :], in0=raw[:, :, :], scalar=0.0, in1=tiny[:, :, :],
                                               op0=ALU.max, op1=ALU.add))
                dve.wait_ge(log_ok, 1)
                chain(dve.tensor_tensor(inv[:, :, :], inv[:, :, :], log1[:, :, :], ALU.mult))
                chain(dve.tensor_tensor(dt[:, :, :], inv[:, :, :], tiny[:, :, :], ALU.add))
                chain(dve.tensor_scalar(a_neg[:, :], a_neg[:, :], -1.0, None, ALU.mult))
                dve.tensor_tensor(dA[:, :].rearrange("p (t h) -> p t h", h=NH), dt[:, :, :], every(a_neg[:, :]),
                                  ALU.mult).then_inc(dA_ok, 1)
                dve.wait_ge(cum_ps, 1)
                dve.tensor_copy(cum[:, :], bank[5][:, 0:T * NH]).then_inc(cum_ok, 1)
                dve.wait_ge(rows_ps, 1)
                dve.tensor_copy(cum_rows[:, :], bank[6][0:T * NH, 0:P]).then_inc(rows_ok, 1)
                n0 = n

                def convolve(g):
                    for c in range(4):
                        dve.wait_ge(tap_ok, (g * 4 + c) * 2 + 2)
                        for k in range(TAPS - 1):
                            a = acc[:, c, :].rearrange("p (r l) -> p r l", r=ROWS)
                            dve.scalar_tensor_tensor(out=a, in0=U[:, c, :, k:k + N], scalar=conv_w[:, c, k:k + 1],
                                                     in1=a, op0=ALU.mult, op1=ALU.add).then_inc(conv, 1)
                            dve.wait_ge(conv, (g * 4 + c) * (TAPS - 1) + k + 1)

                dve.wait_ge(w_ok, 80)
                convolve(0)
                dve.wait_ge(spread_in, 16 * G)
                dve.tensor_tensor(to_end[:, :], spread[:, :, P - 1], cum[:, :], ALU.subtract).then_inc(end_ok, 1)

                dve.sem_inc(y1_ok, 1)
                dve.sem_inc(x_ok, 1)

                def turn(g, has_next):
                    for q in range(ROWS):
                        dve.wait_ge(seg_ok, g * ROWS + q + 1)
                        dve.tensor_scalar(decay[:, q, :, :, :], decay[:, q, :, :, :], 0.0, None, ALU.min)\
                           .then_inc(min_ok, 1)
                    for q in range(ROWS):
                        dve.wait_ge(x_ps, g * ROWS + q + 1)
                        for u in range(TB):
                            t = q * TB + u
                            last = dve.tensor_tensor(
                                xdt[:, t, :].rearrange("p (h d) -> p h d", h=NH),
                                bank[q][:, CH * u:CH * u + CH].rearrange("p (h d) -> p h d", h=NH),
                                dt[:, bass.ds(g * GT + t, 1), :].rearrange("p b (h a) -> p (b h) a", a=1)
                                .broadcast_to([P, NH, HD]), ALU.mult)
                        last.then_inc(xdt_ok, 1)
                    for q in range(ROWS):
                        dve.wait_ge(cb_ps, g * ROWS + q + 1)
                        dve.tensor_tensor(cb[:, q, :, :], bank[2 + q][:, 0:BLK * P].rearrange("p (k l) -> p k l", k=BLK),
                                          mask[:, :, :], ALU.mult).then_inc(cb_ok, 1)
                        dve.wait_ge(cb_ok, g * ROWS + q + 1)
                        dve.wait_ge(decay_ok, g * ROWS + q + 1)
                        dve.tensor_tensor(decay[:, q, :, :, :], decay[:, q, :, :, :],
                                          cb[:, q, :, :].rearrange("p k (a l) -> p k a l", a=1)
                                          .broadcast_to([P, BLK, NH, P]), ALU.mult).then_inc(m_ok, 1)
                    if has_next:
                        convolve(g + 1)
                    dve.wait_ge(skip_ok, g + 1)
                    for q in range(ROWS):
                        dve.wait_ge(y_ps, g + 1)
                        yq = y[:, q * TB:q * TB + TB, :].rearrange("p t c -> p (t c)")
                        dve.tensor_tensor(yq, bank[4 + q][:, :],
                                          xskip[:, q * TB:q * TB + TB, :].rearrange("p t c -> p (t c)"), ALU.add)\
                           .then_inc(y1_ok, 1)
                        dve.wait_ge(y1_ok, g * ROWS + q + 2)
                        dve.tensor_tensor(yq, yq, z[:, bass.ds(g * GT + q * TB, TB), :].rearrange("p t c -> p (t c)"),
                                          ALU.mult).then_inc(yg_ok, 1)
                    dve.wait_ge(ssq_ok, (g + 1) * GT + 1)
                    dve.tensor_scalar(msq[:, :], ssq[:, :], 1.0 / CH, EPS, ALU.mult, ALU.add).then_inc(msq_ok, 1)
                    dve.wait_ge(yr_ok, g + 1)
                    dve.wait_ge(o_ps, g + 1)
                    for t in range(GT):
                        Xt = X[:, bass.ds(g * GT + t, 1), :].rearrange("p a d -> p (a d)")
                        dve.scalar_tensor_tensor(out=Xt, in0=bank[6][:, D * t:D * t + D], scalar=yr[:, t:t + 1],
                                                 in1=Xt, op0=ALU.mult, op1=ALU.add).then_inc(x_ok, 1)

                with dve.Fori(0, G - 1) as g:
                    turn(g, True)
                turn(G - 1, False)

            @block.scalar
            def _(act):
                for g in range(2):
                    act.wait_ge(xT_ps, 2 * g + 1)
                    act.activation(xT[:, 1024 * g:1024 * g + 512], bank[2 * g][:, :], ACT.Copy).then_inc(xT_ok, 1)
                act.wait_ge(p_in, 48)
                act.activation(a_neg[:, :], a_log[:, :], ACT.Exp).then_inc(small_ok, 1)
                act.wait_ge(raw_ok, 1)
                act.activation(small[:, :, :], mag[:, :, :], ACT.Exp, scale=-1.0).then_inc(small_ok, 1)
                act.wait_ge(onep_ok, 1)
                act.activation(log1[:, :, :], onep[:, :, :], ACT.Ln).then_inc(log_ok, 1)

                def taps(g):
                    for c in range(4):
                        act.wait_ge(xbc_ps, g * 4 + c + 1)
                        ps = bank[(0, 1, 2, 7)[c]][:, :]
                        act.activation(U[:, c, :, TAPS - 1:TAPS - 1 + N], ps.rearrange("p (r l) -> p r l", r=ROWS),
                                       ACT.Copy).then_inc(tap_ok, 1)
                        act.activation(acc[:, c, :], ps, ACT.Identity, bias=conv_b[:, c:c + 1],
                                       scale=conv_w[:, c, TAPS - 1:TAPS]).then_inc(tap_ok, 1)

                def silu(g):
                    for c in range(4):
                        act.wait_ge(conv, (g * 4 + c + 1) * (TAPS - 1))
                        act.activation(xbc[:, c, :], acc[:, c, :], ACT.Silu).then_inc(xbc_ok, 1)

                act.wait_ge(w_ok, 80)
                taps(0)
                for t in range(T // 2):
                    act.wait_ge(z_ps, t + 1)
                    act.activation(z[:, 2 * t:2 * t + 2, :], bank[(3, 4, 5, 6)[t % 4]][:, :]
                                   .rearrange("p (t c) -> p t c", t=2), ACT.Silu).then_inc(z_ok, 1)
                silu(0)

                act.sem_inc(ssq_ok, 1)

                def turn(g, has_next):
                    for q in range(ROWS):
                        act.wait_ge(min_ok, g * ROWS + q + 1)
                        act.activation(decay[:, q, :, :, :], decay[:, q, :, :, :], ACT.Exp).then_inc(decay_ok, 1)
                    for q in range(ROWS):
                        act.wait_ge(x_ps, g * ROWS + q + 1)
                        act.wait_ge(xdt_ok, g * ROWS + q + 1)
                        act.activation(xs[:, q * TB:q * TB + TB, :], bank[q][:, :].rearrange("p (t c) -> p t c", t=TB),
                                       ACT.Copy).then_inc(xs_ok, 1)
                    if has_next:
                        taps(g + 1)
                        silu(g + 1)
                    act.wait_ge(ssq_ok, g * GT + 1)
                    for t in range(GT):
                        act.wait_ge(yg_ok, g * ROWS + t // TB + 1)
                        act.activation(squares[:, t, :], y[:, t, :], ACT.Square, accum_out=ssq[:, t:t + 1])\
                           .then_inc(ssq_ok, 1)
                    for k in range(2):
                        act.wait_ge(yT_ps, g * 2 + k + 1)
                        act.activation(yT[:, k, :], bank[4 + k][:, :], ACT.Copy, scale=norm_w[:, k:k + 1])\
                           .then_inc(yT_ok, 1)

                with act.Fori(0, G - 1) as g:
                    turn(g, True)
                turn(G - 1, False)

            @block.tensor
            def _(pe):
                pe.wait_ge(consts, 9)
                pe.wait_ge(xn_ok, T)
                for t in range(T):
                    last = pe.transpose(bank[t // 4][:, P * (t % 4):P * (t % 4) + P], xn[:, t, :], ident[:, :])
                    if t % 4 == 3:
                        last.then_inc(xT_ps, 1)
                pe.wait_ge(xT_ok, 4)
                pe.wait_ge(w_ok, 80)
                for t in range(T):
                    last = pe.matmul(bank[4][:, NH * t:NH * t + NH], xT[:, P * t:P * t + P],
                                     w_in[:, 3 * CH:3 * CH + NH], start=True, stop=True)
                last.then_inc(dt_ps, 1)

                def project(g):
                    for c in range(4):
                        pe.matmul(bank[(0, 1, 2, 7)[c]][:, :], w_in[:, CH + P * c:CH + P * c + P],
                                  xT[:, bass.ds(g * ROWS * N, ROWS * N)], start=True, stop=True).then_inc(xbc_ps, 1)

                project(0)
                pe.wait_ge(dA_ok, 1)
                pe.matmul(bank[5][:, 0:T * NH], upto[:, :], dA[:, :], start=True, stop=True).then_inc(cum_ps, 1)
                pe.wait_ge(cum_ok, 1)
                pe.transpose(bank[6][0:T * NH, 0:P], cum[:, :], ident[:, :]).then_inc(rows_ps, 1)
                pe.wait_ge(rows_ok, 1)
                for t in range(T):
                    if t % 2 == 0 and t >= 8:
                        pe.wait_ge(z_ok, t // 2 - 3)
                    last = pe.matmul(bank[(3, 4, 5, 6)[t // 2 % 4]][:, CH * (t % 2):CH * (t % 2) + CH],
                                     xT[:, P * t:P * t + P], w_in[:, 0:CH], start=True, stop=True)
                    if t % 2:
                        last.then_inc(z_ps, 1)
                pe.wait_ge(z_ok, T // 2)

                def turn(g, has_next):
                    pe.wait_ge(xbc_ok, g * 4 + 4)
                    for q in range(ROWS):
                        for u in range(TB):
                            for k in range(2):
                                last = pe.transpose(bank[q][:, CH * u + P * k:CH * u + P * k + P],
                                                    xbc[:, k, P * (q * TB + u):P * (q * TB + u) + P], ident[:, :])
                        last.then_inc(x_ps, 1)
                    for q in range(ROWS):
                        s = N * q
                        pe.matmul(bank[2 + q][:, 0:N], xbc[:, 2, s:s + P], xbc[:, 3, s:s + N], start=True, stop=True)
                        pe.matmul(bank[2 + q][:, N:N + P], xbc[:, 2, s + P:s + N], xbc[:, 3, s + P:s + N],
                                  start=True, stop=True).then_inc(cb_ps, 1)
                    if has_next:
                        pe.wait_ge(xs_ok, g * 2 + 2)
                        pe.wait_ge(cb_ok, g * ROWS + 2)
                        project(g + 1)
                    for q in range(ROWS):
                        pe.wait_ge(m_ok, g * ROWS + q + 1)
                        pe.wait_ge(xdt_ok, g * ROWS + q + 1)
                        for u in range(TB):
                            for h in range(NH):
                                for s in range(u + 1):
                                    last = pe.matmul(bank[4 + q][:, CH * u + HD * h:CH * u + HD * h + HD],
                                                     decay[:, q, u + s, h, :],
                                                     xdt[:, q * TB + s, HD * h:HD * h + HD],
                                                     start=(s == 0), stop=(s == u))
                    last.then_inc(y_ps, 1)
                    pe.wait_ge(yg_ok, g * ROWS + ROWS)
                    for k in range(2):
                        for t in range(GT):
                            last = pe.transpose(bank[4 + k][:, P * t:P * t + P], y[:, t, P * k:P * k + P], ident[:, :])
                        last.then_inc(yT_ps, 1)
                    pe.wait_ge(yT_ok, g * 2 + 2)
                    pe.wait_ge(x_ok, g * GT + 1)
                    for t in range(GT):
                        for k in range(2):
                            last = pe.matmul(bank[6][:, D * t:D * t + D], yT[:, k, P * t:P * t + P], w_out[:, k, :],
                                             start=(k == 0), stop=(k == 1))
                    last.then_inc(o_ps, 1)

                with pe.Fori(0, G - 1) as g:
                    turn(g, True)
                turn(G - 1, False)


W_SHAPES = {"s1": [P, HID], "s2": [P, HC * D], "e1": [P, E_N * HID], "e2": [P, E_N * HC * D], "gate": [P, E_N]}


def hybrid_kernel(nc, dram, out, phases="afmf"):
    dram = dict(dram)
    dram["slots_x"] = nc.dram_tensor("slots_x", [NSLOT * P, D], F32).ap()
    dram["slots_y"] = nc.dram_tensor("slots_y", [NSLOT * P, D], F32).ap()
    dram["cum_rows"] = nc.dram_tensor("cum_rows", [T * NH, P], F32).ap()
    with ExitStack() as ctx:
        X = ctx.enter_context(nc.sbuf_tensor("X", [P, T, D], F32))
        w = {n: ctx.enter_context(nc.sbuf_tensor(f"w_{n}", s, F32)) for n, s in W_SHAPES.items()}
        stored = ctx.enter_context(nc.semaphore("stored"))
        layer = 0
        sems = []
        for phase in phases:
            if phase == "a":
                attention_phase(nc, sems, dram, X, w)
            elif phase == "f":
                ffn_phase(nc, sems, dram, X, w, layer)
                layer += 1
            elif phase == "m":
                mixer_phase(nc, sems, dram, X)
            end_phase(nc, sems)
        with nc.Block() as block:
            @block.sync
            def _(sp):
                sp.dma_start(out.rearrange("(t p) d -> p t d", p=P), X[:, :, :]).then_inc(stored, 16)
                sp.wait_ge(stored, 16)


def laid_out(i):
    c = np.ascontiguousarray
    a, b, f = (lambda n, k=k: np.asarray(i[k + n]) for k in ("L0_attn_a_", "L0_attn_b_", "L0_ffn_"))
    return {
        "x": c(a("x").reshape(B * N, D)), "wq": c(a("Wq")), "wk": c(a("Wk")), "wv": c(a("Wv")),
        "wo": c(a("Wo")), "bo": c(a("bo")),
        "s1": c(f("shared_w1").T),
        "s2": c(f("shared_w2").reshape(D, HC, P).transpose(2, 1, 0).reshape(P, HC * D)),
        "e1": c(f("experts_w1").transpose(2, 0, 1).reshape(D, E_N * HID)),
        "e2": c(f("experts_w2").reshape(E_N, D, HC, P).transpose(3, 0, 2, 1).reshape(P, E_N * HC * D)),
        "gate": c(f("gate_w").T),
        "w_in": c(b("W_in").T), "conv_w": c(b("conv_w").reshape(4, P, 4).transpose(1, 0, 2)),
        "conv_b": c(b("conv_b").reshape(4, P).T), "dt_bias": c(b("dt_bias").reshape(1, 4)),
        "a_log": c(b("A_log").reshape(1, 4)), "d_skip": c(b("D").reshape(1, 4)),
        "norm_w": c(b("norm_w").reshape(2, P).T),
        "w_out": c(b("W_out").T.reshape(2, P, D).transpose(1, 0, 2)),
    }


def kernel(**inputs):
    import concourse.bacc as bacc
    from concourse.bass_utils import run_bass_kernel_spmd

    nc = bacc.Bacc("TRN2", target_bir_lowering=False, num_devices=1)
    arrays = {f"in_{n}": a for n, a in laid_out(inputs).items()}
    dram = {n[3:]: nc.dram_tensor(n, list(a.shape), F32, kind="ExternalInput").ap() for n, a in arrays.items()}
    out = nc.dram_tensor("out_x", [B * N, D], F32, kind="ExternalOutput").ap()
    hybrid_kernel(nc, dram, out)
    result = run_bass_kernel_spmd(nc, [arrays], core_ids=[0])
    return result.results[0]["out_x"].reshape(B, N, D)
```

```python
from contextlib import ExitStack

import numpy as np
import concourse.bass as bass
from concourse import mybir
from concourse.alu_op_type import AluOpType as ALU

F32 = mybir.dt.float32
BF16 = mybir.dt.bfloat16
I32 = mybir.dt.int32
U32 = mybir.dt.uint32
ACT = mybir.ActivationFunctionType
AX = mybir.AxisListType

P = 128
B, N, D = 8, 256, 128
T = B * N // P
TB = N // P
H, DH = 16, 64
PAIRS = H // 2
EPS = 1e-5
SCALE = DH ** -0.5
LARGE = 3.0e38


def phase_semaphore(nc, sems, name):
    sems.append(nc.alloc_semaphore(name))
    return sems[-1]


def end_phase(nc, sems):
    nc.clear_and_free_semaphores(sems)
    nc.all_engine_barrier()
    sems.clear()


def attention_steps(has_next):
    s = []
    for p in range(PAIRS):
        s.append(("scores", p))
        if p >= 1:
            s.append(("turn", p - 1))
        s.append(("exps", p))
        if p >= 2:
            s.append(("values", p - 2))
        if p >= 3:
            s.append(("outT", p - 3))
        if has_next and p == 3:
            s.append(("stats", 0))
        if has_next and p == 4:
            s.append(("norm", 0))
        if has_next and p == 5:
            s.append(("xT", 0))
    jobs = [("job", j) for j in range(20)] if has_next else []
    s += jobs[0:3] + [("turn", 7), ("values", 6), ("outT", 5)]
    s += jobs[3:8] + [("values", 7), ("outT", 6)] + jobs[8:16] + [("outT", 7)] + jobs[16:20]
    return s + [("project", 0)]


def attention_phase(nc, sems, dram, X, w):
    QW = 3 * P
    JOBS = 20
    with ExitStack() as ctx:
        def sb(name, shape, dt=F32):
            return ctx.enter_context(nc.sbuf_tensor(name, shape, dt))

        def sem(name):
            return phase_semaphore(nc, sems, name)

        wq = sb("wq", [P, H * DH])
        wk = sb("wk", [P, H * DH])
        wv = sb("wv", [P, H * DH])
        wo = sb("wo", [P, PAIRS, D])
        bo = sb("bo", [P, D])
        ident = sb("ident", [P, P])
        rel_i = sb("rel_i", [P, QW], I32)
        rel = sb("rel", [P, QW])
        relm = sb("relm", [P, QW])
        bias = sb("bias", [P, H, QW])
        XB = sb("XB", [P, T, D])
        stats = sb("stats", [P, TB, 6])
        mv = sb("mv", [P, TB, 2])
        veps = sb("veps", [P, TB])
        half = sb("half", [P, TB])
        rstd = sb("rstd", [P, TB])
        xn = sb("xn", [P, TB, D])
        xT = sb("xT", [P, N])
        qT = sb("qT", [P, PAIRS, N])
        kT = sb("kT", [P, PAIRS, N])
        V = sb("V", [P, TB, H, DH + 1])
        S = sb("S", [P, 4, QW])
        low = sb("low", [P, 4, 2])
        E = sb("E", [P, 4, QW])
        ET = sb("ET", [P, 2, 2, QW])
        rden = sb("rden", [P, 2, 4])
        O = sb("O", [P, TB, H * DH])
        OT = sb("OT", [P, PAIRS, N])
        bank = [ctx.enter_context(nc.psum_tensor(f"bank{i}", [P, 512], F32)) for i in range(8)]
        turned = [bank[4], bank[5]]
        O_ps, side = bank[6], bank[7]
        job_bank = [bank[7], bank[0], bank[1]]

        clear = sb("clear", [P, NSLOT, ROW])
        clear_i = sb("clear_i", [P, NSLOT], I32)

        later_in = sem("later_in")
        clear_ok = sem("clear_ok")
        x_in = sem("x_in")
        w_in = sem("w_in")
        wo_in = sem("wo_in")
        bo_in = sem("bo_in")
        consts = sem("consts")
        bias_ok = sem("bias_ok")
        xb_ok = sem("xb_ok")
        mean_ok = sem("mean_ok")
        stat_ok = sem("stat_ok")
        var_ok = sem("var_ok")
        rstd_ok = sem("rstd_ok")
        xn_ok = sem("xn_ok")
        s_ok = sem("s_ok")
        low_ok = sem("low_ok")
        e_ok = sem("e_ok")
        et_ps = sem("et_ps")
        et_even = sem("et_even")
        et_odd = sem("et_odd")
        o_ps = sem("o_ps")
        rden_ok = sem("rden_ok")
        o_ok = sem("o_ok")
        side_ps = sem("side_ps")
        side_ok = sem("side_ok")
        job_ps = sem("job_ps")
        job_act = sem("job_act")
        job_dve = sem("job_dve")
        y_ps = sem("y_ps")
        x_ok = sem("x_ok")
        passed = sem("passed")

        STEPS = attention_steps(True)
        LAST = attention_steps(False)
        SIDES = PAIRS + 1

        def side_index(step, p, steps):
            return 3 if step == "xT" else p + (p > 2 and steps is STEPS)

        TURN_BEFORE_JOB = {0: 4, 3: 5, 9: 6, 18: 7}
        JOB_BEFORE_TURN = {5: 0, 6: 6, 7: 15}

        with nc.Block() as block:
            @block.sync
            def _(sp):
                for g in range(2):
                    sp.dma_start(X[:, 8 * g:8 * g + 8, :],
                                 dram["x"].rearrange("(t p) d -> p t d", p=P)[:, 8 * g:8 * g + 8, :])\
                      .then_inc(x_in, 16)
                    if g == 0:
                        sp.wait_ge(x_in, 16)
                sp.dma_start(wo[:, :, :], dram["wo"].rearrange("(c p) d -> p c d", p=P)).then_inc(wo_in, 16)
                for name in w:
                    sp.dma_start(w[name][:, :], dram[name]).then_inc(later_in, 16)
                sp.wait_ge(clear_ok, 1)
                for layer in range(LAYERS):
                    sp.dma_start(dram[f"slots{layer}"].rearrange("(t p) d -> p t d", p=P), clear[:, :, :])\
                      .then_inc(later_in, 16)
                sp.wait_ge(later_in, 16 * (len(w) + LAYERS))

            @block.gpsimd
            def _(pool):
                pool.dma_start(bo[:, :], dram["bo"].rearrange("(a d) -> a d", a=1).broadcast_to([P, D]))\
                    .then_inc(bo_in, 16)
                pool.memset(ident[:, :], 1.0).then_inc(consts, 1)
                pool.wait_ge(consts, 1)
                pool.affine_select(out=ident[:, :], in_=ident[:, :], compare_op=ALU.is_equal, fill=0.0,
                                   base=0, pattern=[[-1, P]], channel_multiplier=1).then_inc(consts, 1)
                pool.memset(half[:, :], -0.5).then_inc(consts, 1)
                pool.memset(V[:, :, :, DH:DH + 1], 1.0).then_inc(consts, 1)
                pool.iota(rel_i[:, 0:P], [[-1, P]], base=0, channel_multiplier=1).then_inc(consts, 1)
                pool.iota(rel_i[:, P:QW], [[-1, N]], base=P, channel_multiplier=1).then_inc(consts, 1)
                pool.wait_ge(consts, 6)
                pool.tensor_copy(rel[:, :], rel_i[:, :]).then_inc(consts, 1)
                pool.wait_ge(consts, 7)
                pool.affine_select(out=relm[:, 0:P], in_=rel[:, 0:P], compare_op=ALU.is_ge, fill=-1e33,
                                   base=0, pattern=[[-1, P]], channel_multiplier=1).then_inc(consts, 1)
                pool.affine_select(out=relm[:, P:QW], in_=rel[:, P:QW], compare_op=ALU.is_ge, fill=-1e33,
                                   base=P, pattern=[[-1, N]], channel_multiplier=1).then_inc(consts, 1)
                pool.wait_ge(consts, 9)
                root = np.float32((2.0 ** 8) ** (1.0 / H))
                slopes = (np.float32(1.0) / root ** np.arange(1, H + 1, dtype=np.float32)) / np.float32(SCALE)

                def reciprocal_root(b):
                    pool.wait_ge(var_ok, b + 1)
                    pool.tensor_tensor(rstd[:, :], veps[:, :], half[:, :], ALU.pow).then_inc(rstd_ok, 1)

                reciprocal_root(0)
                for h in range(H):
                    pool.tensor_scalar(bias[:, h, :], relm[:, :], float(slopes[h]), None, ALU.mult)\
                        .then_inc(bias_ok, 1)
                pool.wait_ge(bo_in, 16)
                pool.wait_ge(x_in, 32)
                pool.tensor_tensor(XB[:, :, :], X[:, :, :],
                                   bo[:, :].rearrange("p (a d) -> p a d", a=1).broadcast_to([P, T, D]),
                                   ALU.add).then_inc(xb_ok, 1)
                pool.memset(clear[:, :, :], 0.0).then_inc(consts, 1)
                pool.iota(clear_i[:, :], [[P, NSLOT]], base=RESULTS, channel_multiplier=1).then_inc(consts, 1)
                pool.wait_ge(consts, 11)
                pool.tensor_copy(clear[:, :, D], clear_i[:, :]).then_inc(clear_ok, 1)
                with pool.Fori(1, B) as b:
                    reciprocal_root(b)

            @block.vector
            def _(dve):
                def row_stats(b):
                    for t in range(TB):
                        dve.bn_stats(stats[:, t, :], X[:, bass.ds(b * TB + t, 1), :]).then_inc(mean_ok, 1)
                    dve.wait_ge(x_in, 32)
                    dve.wait_ge(mean_ok, b * 4 + 2)
                    dve.sem_inc(passed, 1)
                    for t in range(TB):
                        dve.bn_aggr(mv[:, t, :], stats[:, t, :]).then_inc(mean_ok, 1)
                    dve.wait_ge(mean_ok, b * 4 + 4)
                    dve.tensor_scalar(veps[:, :], mv[:, :, 1], EPS, None, ALU.add).then_inc(var_ok, 1)

                def row_norm(b):
                    dve.wait_ge(rstd_ok, b + 1)
                    for t in range(TB):
                        last = dve.tensor_scalar(xn[:, t, :], X[:, bass.ds(b * TB + t, 1), :],
                                                 mv[:, t, 0:1], rstd[:, t:t + 1], ALU.subtract, ALU.mult)
                    last.then_inc(xn_ok, 1)

                def project_out(b, j):
                    if j % 2 == 0:
                        return
                    dve.wait_ge(job_ps, b * JOBS + j + 1)
                    copy_job(dve.tensor_copy, j).then_inc(job_dve, 1)

                def copy_job(copy, j):
                    ps = job_bank[j % 3]
                    if j < 16:
                        dst = qT if j % 4 in (0, 3) else kT
                        return copy(dst[:, j // 2, :], ps[:, 0:N])
                    t, half_v = (j - 16) // 2, (j - 16) % 2
                    return copy(V[:, t, 8 * half_v:8 * half_v + 8, 0:DH],
                                ps[:, :].rearrange("p (h d) -> p h d", d=DH))

                def run(b, steps):
                    for step, p in steps:
                        if step == "scores":
                            for h in (2 * p, 2 * p + 1):
                                dve.wait_ge(bias_ok, h + 1)
                                dve.wait_ge(s_ok, b * H + h + 1)
                                if h >= 4:
                                    dve.wait_ge(e_ok, b * H + h - 3)
                                dve.sem_inc(passed, 1)
                                sc = bank[2 * (p % 2) + h % 2]
                                for q, (c0, c1) in enumerate(((0, P), (P, QW))):
                                    last = dve.tensor_tensor_reduce(
                                        S[:, h % 4, c0:c1], sc[:, c0:c1], bias[:, h, c0:c1], -SCALE, LARGE,
                                        ALU.add, ALU.min, low[:, h % 4, q:q + 1])
                                last.then_inc(low_ok, 1)
                        elif step == "turn":
                            dve.wait_ge(et_ps, b * H + 2 * p + 2)
                            if p >= 2:
                                dve.wait_ge(o_ps, b * PAIRS + p - 1)
                            dve.tensor_copy(ET[:, p % 2, 1, :], turned[1][:, 0:QW]).then_inc(et_odd, 1)
                        elif step == "values":
                            dve.wait_ge(o_ps, b * PAIRS + p + 1)
                            ov = O_ps[:, 0:4 * (DH + 1)].rearrange("p (h t d) -> p t h d", h=2, t=TB)
                            dve.reciprocal(rden[:, p % 2, :].rearrange("p (t h) -> p t h", t=TB),
                                           ov[:, :, :, DH]).then_inc(rden_ok, 1)
                            dve.wait_ge(rden_ok, b * PAIRS + p + 1)
                            for t in range(TB):
                                last = dve.tensor_tensor(
                                    O[:, t, P * p:P * p + P].rearrange("p (h d) -> p h d", h=2),
                                    ov[:, t, :, 0:DH],
                                    rden[:, p % 2, 2 * t:2 * t + 2].rearrange("p (h a) -> p h a", a=1)
                                    .broadcast_to([P, 2, DH]), ALU.mult)
                            last.then_inc(o_ok, 1)
                        elif step == "stats":
                            row_stats(b + 1)
                        elif step == "norm":
                            row_norm(b + 1)
                        elif step == "job":
                            project_out(b + 1, p)
                        elif step == "project":
                            dve.wait_ge(y_ps, b + 1)
                            dve.wait_ge(xb_ok, 1)
                            dve.tensor_tensor(X[:, bass.ds(b * TB, TB), :],
                                              O_ps[:, 0:TB * D].rearrange("p (t d) -> p t d", t=TB),
                                              XB[:, bass.ds(b * TB, TB), :], ALU.add).then_inc(x_ok, 1)

                dve.sem_inc(x_ok, 1)
                dve.wait_ge(x_in, 16)
                row_stats(0)
                row_norm(0)
                for j in range(JOBS):
                    project_out(0, j)
                with dve.Fori(0, B - 1) as b:
                    run(b, STEPS)
                run(B - 1, LAST)

            @block.scalar
            def _(act):
                act.dma_start(wq[:, :], dram["wq"]).then_inc(w_in, 16)
                act.wait_ge(w_in, 16)
                act.dma_start(wk[:, :], dram["wk"]).then_inc(w_in, 16)
                act.wait_ge(w_in, 32)
                act.dma_start(wv[:, :], dram["wv"]).then_inc(w_in, 16)

                def job_out(b, j):
                    if j % 2:
                        return
                    act.wait_ge(job_ps, b * JOBS + j + 1)
                    ps = job_bank[j % 3]
                    if j < 16:
                        dst = qT if j % 4 in (0, 3) else kT
                        act.activation(dst[:, j // 2, :], ps[:, 0:N], ACT.Copy).then_inc(job_act, 1)
                    else:
                        t, half_v = (j - 16) // 2, (j - 16) % 2
                        act.activation(V[:, t, 8 * half_v:8 * half_v + 8, 0:DH],
                                       ps[:, :].rearrange("p (h d) -> p h d", d=DH), ACT.Copy)\
                           .then_inc(job_act, 1)

                def side_out(b, step, p, dst, steps):
                    act.wait_ge(side_ps, b * SIDES + side_index(step, p, steps) + 2)
                    act.activation(dst, side[:, 0:N], ACT.Copy).then_inc(side_ok, 1)

                def run(b, steps):
                    for step, p in steps:
                        if step == "exps":
                            for h in (2 * p, 2 * p + 1):
                                act.wait_ge(low_ok, b * H + h + 1)
                                if h >= 4:
                                    act.wait_ge(et_ps, b * H + h - 3)
                                for q, (c0, c1) in enumerate(((0, P), (P, QW))):
                                    last = act.activation(E[:, h % 4, c0:c1], S[:, h % 4, c0:c1], ACT.Exp,
                                                          bias=low[:, h % 4, q:q + 1], scale=-1.0)
                                last.then_inc(e_ok, 1)
                        elif step == "turn":
                            act.wait_ge(et_ps, b * H + 2 * p + 1)
                            if p >= 2:
                                act.wait_ge(o_ps, b * PAIRS + p - 1)
                            act.activation(ET[:, p % 2, 0, :], turned[0][:, 0:QW], ACT.Copy)\
                               .then_inc(et_even, 1)
                        elif step == "outT":
                            side_out(b, step, p, OT[:, p, :], steps)
                        elif step == "xT":
                            side_out(b, step, p, xT[:, :], steps)
                        elif step == "job":
                            job_out(b + 1, p)

                act.wait_ge(side_ps, 1)
                act.activation(xT[:, :], side[:, 0:N], ACT.Copy).then_inc(side_ok, 1)
                for j in range(JOBS):
                    job_out(0, j)
                with act.Fori(0, B - 1) as b:
                    run(b, STEPS)
                run(B - 1, LAST)

            @block.tensor
            def _(pe):
                def transposes_x():
                    for t in range(TB):
                        last = pe.transpose(side[:, P * t:P * t + P], xn[:, t, :], ident[:, :])
                    last.then_inc(side_ps, 1)

                def job_free(b, j):
                    pe.wait_ge(job_dve if j % 2 else job_act, b * (JOBS // 2) + j // 2 + 1)

                def job(b, j):
                    if j >= 3:
                        job_free(b, j - 3)
                    ps = job_bank[j % 3]
                    if j < 16:
                        c = j // 2
                        w = wq if j % 4 in (0, 3) else wk
                        pe.matmul(ps[:, 0:N], w[:, P * c:P * c + P], xT[:, :], start=True, stop=True)\
                          .then_inc(job_ps, 1)
                    else:
                        t, half_v = (j - 16) // 2, (j - 16) % 2
                        pe.matmul(ps[:, :], xT[:, P * t:P * t + P], wv[:, 512 * half_v:512 * half_v + 512],
                                  start=True, stop=True).then_inc(job_ps, 1)

                def run(b, steps):
                    for step, p in steps:
                        if step == "scores":
                            if p == 0:
                                for j in (17, 18, 19):
                                    job_free(b, j)
                            if p >= 2:
                                pe.wait_ge(low_ok, b * H + 2 * p - 2)
                            for h in (2 * p, 2 * p + 1):
                                rows = slice(DH * (h % 2), DH * (h % 2) + DH)
                                sc = bank[2 * (p % 2) + h % 2]
                                pe.matmul(sc[:, 0:P], qT[rows, p, 0:P], kT[rows, p, 0:P], start=True, stop=True)
                                pe.matmul(sc[:, P:QW], qT[rows, p, P:N], kT[rows, p, :], start=True, stop=True)\
                                  .then_inc(s_ok, 1)
                        elif step == "turn":
                            for h in (2 * p, 2 * p + 1):
                                pe.wait_ge(e_ok, b * H + h + 1)
                                if p >= 1:
                                    pe.wait_ge(et_odd if h % 2 else et_even, b * PAIRS + p)
                                for k in range(3):
                                    last = pe.transpose(turned[h % 2][:, P * k:P * k + P],
                                                        E[:, h % 4, P * k:P * k + P], ident[:, :])
                                last.then_inc(et_ps, 1)
                        elif step == "values":
                            if p == 0:
                                pe.wait_ge(x_ok, b + 1)
                            else:
                                pe.wait_ge(o_ok, b * PAIRS + p)
                            pe.wait_ge(et_even, b * PAIRS + p + 1)
                            pe.wait_ge(et_odd, b * PAIRS + p + 1)
                            for e in range(2):
                                h = 2 * p + e
                                for t in range(TB):
                                    c = (2 * e + t) * (DH + 1)
                                    for k in range(t + 1):
                                        last = pe.matmul(O_ps[:, c:c + DH + 1],
                                                         ET[:, p % 2, e, P * (t + k):P * (t + k) + P],
                                                         V[:, k, h, :], start=(k == 0), stop=(k == t))
                            last.then_inc(o_ps, 1)
                        elif step == "outT":
                            pe.wait_ge(o_ok, b * PAIRS + p + 1)
                            pe.wait_ge(side_ok, b * SIDES + side_index(step, p, steps) + 1)
                            if p in JOB_BEFORE_TURN and steps is STEPS:
                                job_free(b + 1, JOB_BEFORE_TURN[p])
                            for t in range(TB):
                                last = pe.transpose(side[:, P * t:P * t + P], O[:, t, P * p:P * p + P], ident[:, :])
                            last.then_inc(side_ps, 1)
                        elif step == "xT":
                            pe.wait_ge(xn_ok, b + 2)
                            pe.wait_ge(side_ok, b * SIDES + side_index(step, p, steps) + 1)
                            transposes_x()
                        elif step == "job":
                            if p in TURN_BEFORE_JOB:
                                pe.wait_ge(side_ok, b * SIDES + side_index("outT", TURN_BEFORE_JOB[p], steps) + 2)
                            job(b + 1, p)
                        elif step == "project":
                            pe.wait_ge(side_ok, b * SIDES + SIDES + (steps is STEPS))
                            pe.wait_ge(o_ok, b * PAIRS + PAIRS)
                            pe.wait_ge(wo_in, 16)
                            for t in range(TB):
                                for c in range(PAIRS):
                                    last = pe.matmul(O_ps[:, D * t:D * t + D], OT[:, c, P * t:P * t + P],
                                                     wo[:, c, :], start=(c == 0), stop=(c == PAIRS - 1))
                            last.then_inc(y_ps, 1)

                pe.wait_ge(consts, 9)
                pe.wait_ge(xn_ok, 1)
                transposes_x()
                pe.wait_ge(side_ok, 1)
                pe.wait_ge(w_in, 48)
                for j in range(JOBS):
                    job(0, j)
                with pe.Fori(0, B - 1) as b:
                    run(b, STEPS)
                run(B - 1, LAST)


E_N = 8
HID = 512
HC = HID // P
NSLOT = 2 * B * N // P + E_N - 1
LAYERS = 2
ROW = D + 2
RESULTS = 2 * T * P


def slot_steps(eng, step, end):
    for j in range(7):
        step(j, j)
    with eng.Fori(0, 7) as i:
        for u in range(7, 11):
            step(i * 4 + u, u)
    for j in range(35, end):
        step(j, j)


def uses_before(j, n):
    return (j - n % 4) * 4


def ffn_phase(nc, sems, dram, X, w, layer):
    GROUP = 4
    GROUPS = T // GROUP
    with ExitStack() as ctx:
        def sb(name, shape, dt=F32):
            return ctx.enter_context(nc.sbuf_tensor(f"f{layer}_{name}", shape, dt))

        def sem(name):
            return phase_semaphore(nc, sems, f"f{layer}_{name}")

        stats = sb("stats", [P, T, 6])
        mv = sb("mv", [P, T, 2])
        veps = sb("veps", [P, T])
        half = sb("half", [P, T])
        rstd = sb("rstd", [P, T])
        xn = sb("xn", [P, 2, T, ROW])
        xT = sb("xT", [P, T * P])
        ident = sb("ident", [P, P])
        prior_i = sb("prior_i", [P, E_N], I32)
        prior = sb("prior", [P, E_N])
        tile_i = sb("tile_i", [1, NSLOT], I32)
        tile_no = sb("tile_no", [1, NSLOT])
        result_i = sb("result_i", [P, T, 2], I32)
        below_f = sb("below_f", [P, P])
        below = sb("below", [P, P], BF16)
        ones = sb("ones", [P, P], BF16)
        L = sb("L", [P, T, E_N])
        eq = sb("eq", [P, T, E_N])
        rank = sb("rank", [P, T, E_N])
        first = sb("first", [P, T, E_N])
        second = sb("second", [P, T, E_N])
        best = sb("best", [P, 2, T])
        top = sb("top", [P, 2, T])
        gap = sb("gap", [P, T])
        ratio = sb("ratio", [P, T])
        whole = sb("whole", [P, T])
        picked = sb("picked", [P, 2 * T + 1, E_N], BF16)
        count_i = sb("count_i", [P, E_N], I32)
        tiles_i = sb("tiles_i", [P, E_N], I32)
        tiles = sb("tiles", [P, E_N])
        one8 = sb("one8", [P, E_N])
        ends = sb("ends", [P, E_N])
        starts = sb("starts", [P, E_N])
        place = sb("place", [P, T, E_N])
        slot = sb("slot", [P, 2, T])
        slot_i = sb("slot_i", [P, 2, T], I32)
        after = sb("after", [1, NSLOT, E_N])
        tile_e = sb("tile_e", [1, NSLOT])
        tile_w = sb("tile_w", [1, NSLOT], I32)
        hT_s = sb("hT_s", [P, 2, HC, GROUP * P])
        xg = sb("xg", [P, 4, ROW])
        xgT = sb("xgT", [P, 2, P])
        up = sb("up", [P, 2, HID])
        hT = sb("hT", [P, 2, HID])
        yo = sb("yo", [P, 4, D])
        to = sb("to", [P, 4], I32)
        gate = sb("gate", [P, 4])
        Y = sb("Y", [P, T, 2, D])
        bank = [ctx.enter_context(nc.psum_tensor(f"f{layer}_bank{i}", [P, 512], F32)) for i in range(8)]

        consts = sem("consts")
        mean_ok = sem("mean_ok")
        veps_ok = sem("veps_ok")
        rstd_ok = sem("rstd_ok")
        xn_ok = sem("xn_ok")
        copied = sem("copied")
        xT_ps = sem("xT_ps")
        xT_ok = sem("xT_ok")
        logit_ps = sem("logit_ps")
        stat = sem("stat")
        gap_ok = sem("gap_ok")
        ratio_ok = sem("ratio_ok")
        picked_ok = sem("picked_ok")
        place_ps = sem("place_ps")
        slot_ok = sem("slot_ok")
        tile_ok = sem("tile_ok")
        sent = sem("sent")
        sh_ps = sem("sh_ps")
        sh_ok = sem("sh_ok")
        so_ps = sem("so_ps")
        so_ok = sem("so_ok")
        xg_in = [sem(f"xg_in{i}") for i in range(4)]
        y_out = [sem(f"y_out{i}") for i in range(4)]
        up_ok = sem("up_ok")
        xt_ps = sem("xt_ps")
        xt_ok = sem("xt_ok")
        tag_ok = sem("tag_ok")
        h_ps = sem("h_ps")
        h_ok = sem("h_ok")
        y_ps = sem("y_ps")
        y_ok = sem("y_ok")
        back = [sem(f"back{g}") for g in range(GROUPS)]
        pool_x = sem("pool_x")
        dve_x = sem("dve_x")
        passed = sem("passed")

        slots, results = dram[f"slots{layer}"], dram[f"results{layer}"]
        J = NSLOT

        def add_results(eng, g, s, done):
            eng.wait_ge(so_ok, GROUPS)
            eng.wait_ge(back[g], 16)
            for k in range(2):
                eng.tensor_tensor(X[:, s, :], X[:, s, :], Y[:, s, k, :], ALU.add).then_inc(done, 1)
                eng.wait_ge(done, 2 * g + k + 1)

        with nc.Block() as block:
            @block.sync
            def _(sp):
                def load(j, n):
                    sp.dma_start(xg[:, n % 4, :], slots[bass.ds(j * P, P), :]).then_inc(xg_in[n % 4], 16)

                def step(j, n):
                    if n + 4 < J:
                        sp.wait_ge(tag_ok, j + 1)
                        load(j + 4, n)

                sp.wait_ge(sent, 16 * 2 * T)
                for j in range(4):
                    load(j, j)
                slot_steps(sp, step, J)
                for n in range(4):
                    sp.wait_ge(y_out[n], 16 * ((J + 3 - n) // 4))
                for g in range(GROUPS):
                    s = slice(GROUP * g, GROUP * g + GROUP)
                    sp.dma_start(Y[:, s, :, :], results[0:RESULTS, :].rearrange("(p t k) d -> p t k d", p=P, k=2)
                                 [:, s, :, :]).then_inc(back[g], 16)

            @block.gpsimd
            def _(pool):
                pool.memset(half[:, :], -0.5).then_inc(consts, 1)
                pool.memset(ident[:, :], 1.0).then_inc(consts, 1)
                pool.wait_ge(consts, 2)
                pool.affine_select(out=ident[:, :], in_=ident[:, :], compare_op=ALU.is_equal, fill=0.0,
                                   base=0, pattern=[[-1, P]], channel_multiplier=1).then_inc(consts, 1)

                def reciprocal_root(g):
                    pool.wait_ge(mean_ok, 2 * GROUP * (g + 1))
                    s = slice(GROUP * g, GROUP * g + GROUP)
                    pool.tensor_scalar(veps[:, s], mv[:, s, 1], EPS, None, ALU.add).then_inc(veps_ok, 1)
                    pool.wait_ge(veps_ok, g + 1)
                    pool.tensor_tensor(rstd[:, s], veps[:, s], half[:, s], ALU.pow).then_inc(rstd_ok, 1)

                for g in range(GROUPS):
                    reciprocal_root(g)
                pool.memset(below_f[:, :], 1.0).then_inc(consts, 1)
                pool.memset(ones[:, :], 1.0).then_inc(consts, 1)
                pool.memset(picked[:, :, :], 0.0).then_inc(consts, 1)
                pool.iota(prior_i[:, :], [[-1, E_N]], base=E_N, channel_multiplier=0).then_inc(consts, 1)
                pool.iota(tile_i[:, :], [[1, NSLOT]], base=0, channel_multiplier=0).then_inc(consts, 1)
                pool.iota(result_i[:, :, :], [[1, 2 * T]], base=0, channel_multiplier=2 * T).then_inc(consts, 1)
                pool.memset(one8[:, :], 1.0).then_inc(consts, 1)
                pool.wait_ge(consts, 10)
                pool.tensor_copy(prior[:, :], prior_i[:, :]).then_inc(consts, 1)
                pool.affine_select(out=below[:, :], in_=below_f[:, :], compare_op=ALU.is_gt, fill=0.0,
                                   base=0, pattern=[[1, P]], channel_multiplier=-1).then_inc(consts, 1)
                pool.tensor_copy(tile_no[:, :], tile_i[:, :]).then_inc(consts, 1)
                pool.tensor_copy(xn[:, :, :, D], result_i[:, :, :].rearrange("p t k -> p k t")).then_inc(consts, 1)
                pool.wait_ge(consts, 14)
                pool.wait_ge(copied, GROUPS)
                pool.wait_ge(slot_ok, 1)
                for t in range(T):
                    for k in range(2):
                        pool.indirect_dma_start(
                            slots, bass.IndirectOffsetOnAxis(ap=slot_i[:, k, t:t + 1].bitcast(U32), axis=0),
                            xn[:, k, t, :], None).then_inc(sent, 16)

                def step(j, n):
                    pool.wait_ge(y_ok, j + 1)
                    pool.sem_inc(passed, 1)
                    pool.indirect_dma_start(
                        results, bass.IndirectOffsetOnAxis(ap=to[:, n % 4:n % 4 + 1].bitcast(U32), axis=0),
                        yo[:, n % 4, :], None).then_inc(y_out[n % 4], 16)

                slot_steps(pool, step, J)
                for g in range(GROUPS):
                    add_results(pool, g, slice(GROUP * g, GROUP * g + 1), pool_x)

            @block.vector
            def _(dve):
                n = 0

                def chain(instruction):
                    nonlocal n
                    n += 1
                    instruction.then_inc(stat, 1)
                    dve.wait_ge(stat, n)

                def over_experts(x):
                    return x.rearrange("p (t a) -> p t a", a=1).broadcast_to([P, T, E_N])

                def row_stats(g):
                    for t in range(GROUP * g, GROUP * g + GROUP):
                        dve.bn_stats(stats[:, t, :], X[:, t, :]).then_inc(mean_ok, 1)
                    dve.wait_ge(mean_ok, 2 * GROUP * g + GROUP)
                    for t in range(GROUP * g, GROUP * g + GROUP):
                        dve.bn_aggr(mv[:, t, :], stats[:, t, :]).then_inc(mean_ok, 1)

                def row_norm(g):
                    dve.wait_ge(rstd_ok, g + 1)
                    for t in range(GROUP * g, GROUP * g + GROUP):
                        last = dve.tensor_scalar(xn[:, 0, t, 0:D], X[:, t, :], mv[:, t, 0:1], rstd[:, t:t + 1],
                                                 ALU.subtract, ALU.mult)
                    last.then_inc(xn_ok, 1)

                row_stats(0)
                for g in range(1, GROUPS):
                    row_stats(g)
                    row_norm(g - 1)
                row_norm(GROUPS - 1)

                dve.wait_ge(consts, 11)
                dve.wait_ge(logit_ps, 1)
                pr = prior[:, :].rearrange("p (a e) -> p a e", a=1).broadcast_to([P, T, E_N])
                chain(dve.tensor_copy(L[:, :, :], bank[4][:, 0:T * E_N].rearrange("p (t e) -> p t e", e=E_N)))
                for k, choice in enumerate((first, second)):
                    chain(dve.tensor_reduce(best[:, k, :], L[:, :, :], AX.X, ALU.max))
                    chain(dve.tensor_tensor(eq[:, :, :], L[:, :, :], over_experts(best[:, k, :]), ALU.is_equal))
                    chain(dve.tensor_tensor(rank[:, :, :], eq[:, :, :], pr, ALU.mult))
                    chain(dve.tensor_reduce(top[:, k, :], rank[:, :, :], AX.X, ALU.max))
                    chain(dve.tensor_tensor(choice[:, :, :], over_experts(top[:, k, :]), pr, ALU.is_equal))
                    if k == 0:
                        chain(dve.scalar_tensor_tensor(out=L[:, :, :], in0=first[:, :, :], scalar=-LARGE,
                                                       in1=L[:, :, :], op0=ALU.mult, op1=ALU.add))
                dve.tensor_tensor(picked[:, T:2 * T, :], first[:, :, :], second[:, :, :], ALU.add)\
                   .then_inc(picked_ok, 1)
                dve.tensor_tensor(gap[:, :], best[:, 1, :], best[:, 0, :], ALU.subtract).then_inc(gap_ok, 1)
                dve.wait_ge(ratio_ok, 1)
                chain(dve.tensor_scalar(whole[:, :], ratio[:, :], 1.0, None, ALU.add))
                chain(dve.reciprocal(xn[:, 0, :, D + 1], whole[:, :]))
                chain(dve.tensor_tensor(xn[:, 1, :, D + 1], ratio[:, :], xn[:, 0, :, D + 1], ALU.mult))

                dve.wait_ge(consts, 14)
                dve.wait_ge(place_ps, 1)
                pl = bank[5][:, 0:T * E_N].rearrange("p (t e) -> p t e", e=E_N)
                chain(dve.tensor_scalar(count_i[:, :], bank[5][:, T * E_N:(T + 1) * E_N], float(P - 1), None,
                                        ALU.add))
                chain(dve.tensor_scalar(tiles_i[:, :], count_i[:, :], 7, None, ALU.logical_shift_right))
                chain(dve.tensor_copy(tiles[:, :], tiles_i[:, :]))
                chain(dve.tensor_tensor_scan(ends[:, :], one8[:, :], tiles[:, :], 0.0, ALU.mult, ALU.add))
                chain(dve.tensor_tensor(starts[:, :], ends[:, :], tiles[:, :], ALU.subtract))
                chain(dve.tensor_scalar(starts[:, :], starts[:, :], float(P), None, ALU.mult))
                chain(dve.tensor_tensor(place[:, :, :], pl,
                                        starts[:, :].rearrange("p (a e) -> p a e", a=1)
                                        .broadcast_to([P, T, E_N]), ALU.add))
                for k, choice in enumerate((first, second)):
                    chain(dve.tensor_tensor(rank[:, :, :], choice[:, :, :], place[:, :, :], ALU.mult))
                    chain(dve.tensor_reduce(slot[:, k, :], rank[:, :, :], AX.X, ALU.add))
                dve.tensor_copy(slot_i[:, :, :], slot[:, :, :]).then_inc(slot_ok, 1)
                chain(dve.tensor_tensor(
                    after[:, :, :], tile_no[:, :].rearrange("p (j a) -> p j a", a=1).broadcast_to([1, NSLOT, E_N]),
                    ends[0:1, :].rearrange("p (a e) -> p a e", a=1).broadcast_to([1, NSLOT, E_N]), ALU.is_ge))
                chain(dve.tensor_reduce(tile_e[:, :], after[:, :, :], AX.X, ALU.add))
                dve.tensor_scalar(tile_w[:, :], tile_e[:, :], float(E_N - 1), float(HID), ALU.min, ALU.mult)\
                   .then_inc(tile_ok, 1)

                for g in range(GROUPS):
                    dve.wait_ge(so_ps, g + 1)
                    Xg = X[:, GROUP * g:GROUP * g + GROUP, :]
                    dve.tensor_tensor(Xg, bank[6][:, :].rearrange("p (t d) -> p t d", d=D), Xg, ALU.add)\
                       .then_inc(so_ok, 1)

                def weights(j, n):
                    start = dve.value_load(tile_w[0:1, bass.ds(j, 1)], min_val=0, max_val=(E_N - 1) * HID)
                    if n >= 2:
                        dve.wait_ge(h_ps, j - 1)
                    dve.tensor_copy(up[:, n % 2, :], w["e1"][:, bass.ds(start, HID)]).then_inc(up_ok, 1)

                def turn_x(j, n):
                    dve.wait_ge(xt_ps, j + 1)
                    dve.tensor_copy(xgT[:, n % 2, :], bank[n % 2][:, 0:P]).then_inc(xt_ok, 1)

                def step(j, n):
                    if n + 1 < J:
                        weights(j + 1, n + 1)
                        turn_x(j + 1, n + 1)
                    if n >= 1:
                        m = (n - 1) % 4
                        if n >= 5:
                            dve.wait_ge(y_out[m], uses_before(j - 1, n - 1))
                        dve.tensor_copy(to[:, m:m + 1], xg[:, m, D:D + 1])
                        dve.tensor_copy(gate[:, m:m + 1], xg[:, m, D + 1:D + 2]).then_inc(tag_ok, 1)

                dve.wait_ge(tile_ok, 1)
                weights(0, 0)
                turn_x(0, 0)
                slot_steps(dve, step, J + 1)
                for g in range(GROUPS):
                    add_results(dve, g, slice(GROUP * g + 1, GROUP * g + GROUP), dve_x)

            @block.scalar
            def _(act):
                for g in range(GROUPS):
                    act.wait_ge(xT_ps, g + 1)
                    act.activation(xT[:, 512 * g:512 * g + 512], bank[g][:, :], ACT.Copy).then_inc(xT_ok, 1)
                    s = slice(GROUP * g, GROUP * g + GROUP)
                    act.activation(xn[:, 1, s, 0:D], xn[:, 0, s, 0:D], ACT.Copy).then_inc(copied, 1)
                act.wait_ge(gap_ok, 1)
                act.activation(ratio[:, :], gap[:, :], ACT.Exp).then_inc(ratio_ok, 1)
                for g in range(GROUPS):
                    for c in range(HC):
                        act.wait_ge(sh_ps, g * HC + c + 1)
                        if g >= 2:
                            act.wait_ge(so_ps, g - 1)
                        act.activation(hT_s[:, g % 2, c, :], bank[c][:, :], ACT.Silu).then_inc(sh_ok, 1)

                def step(j, n):
                    if n < J:
                        act.wait_ge(h_ps, j + 1)
                        if n >= 2:
                            act.wait_ge(y_ps, j - 1)
                        act.activation(hT[:, n % 2, :], bank[2 + n % 2][:, :], ACT.Silu).then_inc(h_ok, 1)
                    if n >= 1:
                        act.wait_ge(tag_ok, j)
                        act.wait_ge(y_ps, j)
                        act.activation(yo[:, (n - 1) % 4, :], bank[4 + (n - 1) % 2][:, 0:D], ACT.Copy,
                                       scale=gate[:, (n - 1) % 4:(n - 1) % 4 + 1]).then_inc(y_ok, 1)

                slot_steps(act, step, J + 1)

            @block.tensor
            def _(pe):
                def logits(g):
                    pe.wait_ge(xT_ok, g + 1)
                    for t in range(GROUP * g, GROUP * g + GROUP):
                        last = pe.matmul(bank[4][:, E_N * t:E_N * t + E_N], xT[:, P * t:P * t + P],
                                         w["gate"][:, :], start=True, stop=True)
                    if g == GROUPS - 1:
                        last.then_inc(logit_ps, 1)

                def hidden(g):
                    for c in range(HC):
                        if g >= 1:
                            pe.wait_ge(sh_ok, (g - 1) * HC + c + 1)
                        pe.matmul(bank[c][:, :], w["s1"][:, P * c:P * c + P],
                                  xT[:, g * GROUP * P:(g + 1) * GROUP * P], start=True, stop=True)\
                          .then_inc(sh_ps, 1)

                def shared_out(g):
                    pe.wait_ge(sh_ok, (g + 1) * HC)
                    if g >= 1:
                        pe.wait_ge(so_ok, g)
                    for t in range(GROUP):
                        for c in range(HC):
                            last = pe.matmul(bank[6][:, D * t:D * t + D], hT_s[:, g % 2, c, P * t:P * t + P],
                                             w["s2"][:, D * c:D * c + D], start=(c == 0), stop=(c == HC - 1))
                    last.then_inc(so_ps, 1)

                pe.wait_ge(consts, 3)
                for g in range(GROUPS):
                    pe.wait_ge(xn_ok, g + 1)
                    for t in range(GROUP):
                        last = pe.transpose(bank[g][:, P * t:P * t + P], xn[:, 0, GROUP * g + t, 0:D], ident[:, :])
                    last.then_inc(xT_ps, 1)
                    if g >= 1:
                        logits(g - 1)
                logits(GROUPS - 1)
                hidden(0)
                pe.wait_ge(consts, 12)
                pe.wait_ge(picked_ok, 1)
                width = (T + 1) * E_N
                flat = picked[:, :, :].rearrange("p t e -> p (t e)")
                pe.matmul(bank[5][:, 0:width], below[:, :], flat[:, T * E_N:T * E_N + width], start=True, stop=False)
                for k in range(1, T + 1):
                    last = pe.matmul(bank[5][:, 0:width], ones[:, :],
                                     flat[:, (T - k) * E_N:(T - k) * E_N + width], start=False, stop=(k == T))
                last.then_inc(place_ps, 1)
                for g in range(1, GROUPS):
                    hidden(g)
                    shared_out(g - 1)
                shared_out(GROUPS - 1)

                def turn_x(j, n):
                    pe.wait_ge(xg_in[n % 4], uses_before(j, n) + 16)
                    if n >= 2:
                        pe.wait_ge(xt_ok, j - 1)
                    pe.transpose(bank[n % 2][:, 0:P], xg[:, n % 4, 0:D], ident[:, :]).then_inc(xt_ps, 1)

                def step(j, n):
                    if n < J:
                        pe.wait_ge(up_ok, j + 1)
                        pe.wait_ge(xt_ok, j + 1)
                        if n >= 2:
                            pe.wait_ge(h_ok, j - 1)
                        for c in range(HC):
                            last = pe.matmul(bank[2 + n % 2][:, P * c:P * c + P], up[:, n % 2, P * c:P * c + P],
                                             xgT[:, n % 2, :], start=True, stop=True)
                        last.then_inc(h_ps, 1)
                    if n >= 1:
                        start = pe.value_load(tile_w[0:1, bass.ds(j - 1, 1)], min_val=0, max_val=(E_N - 1) * HID)
                    if n + 1 < J:
                        turn_x(j + 1, n + 1)
                    if n >= 1:
                        m = (n - 1) % 2
                        pe.wait_ge(h_ok, j)
                        if n >= 3:
                            pe.wait_ge(y_ok, j - 2)
                        for c in range(HC):
                            last = pe.matmul(bank[4 + m][:, 0:D], hT[:, m, P * c:P * c + P],
                                             w["e2"][:, bass.ds(start + c * D, D)], start=(c == 0),
                                             stop=(c == HC - 1))
                        last.then_inc(y_ps, 1)

                pe.wait_ge(tile_ok, 1)
                pe.wait_ge(sh_ok, GROUPS * HC)
                turn_x(0, 0)
                slot_steps(pe, step, J + 1)
NH = 4
HD = 64
CH = NH * HD
TAPS = 4


def mixer_phase(nc, sems, dram, X):
    ROWS = 2
    G = B // ROWS
    GT = ROWS * TB
    BLK = 3
    with ExitStack() as ctx:
        def sb(name, shape, dt=F32):
            return ctx.enter_context(nc.sbuf_tensor(f"m_{name}", shape, dt))

        def sem(name):
            return phase_semaphore(nc, sems, f"m_{name}")

        w_in = sb("w_in", [P, 3 * CH + NH])
        conv_w = sb("conv_w", [P, 4, TAPS])
        conv_b = sb("conv_b", [P, 4])
        dt_bias = sb("dt_bias", [P, NH])
        a_log = sb("a_log", [P, NH])
        d_skip = sb("d_skip", [P, NH])
        norm_w = sb("norm_w", [P, 2])
        w_out = sb("w_out", [P, 2, D])
        stats = sb("stats", [P, T, 6])
        mv = sb("mv", [P, T, 2])
        veps = sb("veps", [P, T])
        half = sb("half", [P, T])
        rstd = sb("rstd", [P, T])
        xn = sb("xn", [P, T, D])
        xT = sb("xT", [P, T * P])
        ident = sb("ident", [P, P])
        upto = sb("upto", [P, P])
        mask = sb("mask", [P, BLK, P])
        a_neg = sb("a_neg", [P, NH])
        raw = sb("raw", [P, T, NH])
        mag = sb("mag", [P, T, NH])
        small = sb("small", [P, T, NH])
        onep = sb("onep", [P, T, NH])
        step_ = sb("step_", [P, T, NH])
        inv = sb("inv", [P, T, NH])
        log1 = sb("log1", [P, T, NH])
        tiny = sb("tiny", [P, T, NH])
        dt = sb("dt", [P, T, NH])
        dA = sb("dA", [P, T * NH])
        cum = sb("cum", [P, T * NH])
        cum_rows = sb("cum_rows", [T * NH, P])
        spread = sb("spread", [P, T * NH, P])
        to_end = sb("to_end", [P, T * NH])
        z = sb("z", [P, T, CH])
        U = sb("U", [P, 4, ROWS, TAPS - 1 + N])
        acc = sb("acc", [P, 4, ROWS * N])
        xbc = sb("xbc", [P, 4, ROWS * N])
        xs = sb("xs", [P, GT, CH])
        xdt = sb("xdt", [P, GT, CH])
        xskip = sb("xskip", [P, GT, CH])
        cb = sb("cb", [P, ROWS, BLK, P])
        decay = sb("decay", [P, ROWS, BLK, NH, P])
        y = sb("y", [P, GT, CH])
        squares = sb("squares", [P, GT, CH])
        ssq = sb("ssq", [P, GT])
        msq = sb("msq", [P, GT])
        yr = sb("yr", [P, GT])
        yT = sb("yT", [P, 2, GT * P])
        bank = [ctx.enter_context(nc.psum_tensor(f"m_bank{i}", [P, 512], F32)) for i in range(8)]

        w_ok = sem("w_ok")
        p_in = sem("p_in")
        consts = sem("consts")
        stat = sem("stat")
        var_ok = sem("var_ok")
        rstd_ok = sem("rstd_ok")
        xn_ok = sem("xn_ok")
        xT_ps = sem("xT_ps")
        xT_ok = sem("xT_ok")
        dt_ps = sem("dt_ps")
        raw_ok = sem("raw_ok")
        small_ok = sem("small_ok")
        onep_ok = sem("onep_ok")
        log_ok = sem("log_ok")
        dA_ok = sem("dA_ok")
        cum_ps = sem("cum_ps")
        cum_ok = sem("cum_ok")
        rows_ps = sem("rows_ps")
        rows_ok = sem("rows_ok")
        rows_out = sem("rows_out")
        spread_in = sem("spread_in")
        end_ok = sem("end_ok")
        z_ps = sem("z_ps")
        z_ok = sem("z_ok")
        xbc_ps = sem("xbc_ps")
        tap_ok = sem("tap_ok")
        conv = sem("conv")
        xbc_ok = sem("xbc_ok")
        seg_ok = sem("seg_ok")
        min_ok = sem("min_ok")
        decay_ok = sem("decay_ok")
        x_ps = sem("x_ps")
        xs_ok = sem("xs_ok")
        xdt_ok = sem("xdt_ok")
        cb_ps = sem("cb_ps")
        cb_ok = sem("cb_ok")
        m_ok = sem("m_ok")
        skip_ok = sem("skip_ok")
        y_ps = sem("y_ps")
        y1_ok = sem("y1_ok")
        yg_ok = sem("yg_ok")
        ssq_ok = sem("ssq_ok")
        msq_ok = sem("msq_ok")
        yr_ok = sem("yr_ok")
        yT_ps = sem("yT_ps")
        yT_ok = sem("yT_ok")
        o_ps = sem("o_ps")
        x_ok = sem("x_ok")

        with nc.Block() as block:
            @block.sync
            def _(sp):
                for name, tile in (("w_in", w_in), ("conv_w", conv_w), ("conv_b", conv_b), ("norm_w", norm_w),
                                   ("w_out", w_out)):
                    sp.dma_start(tile[:], dram[name]).then_inc(w_ok, 16)
                for name, tile in (("dt_bias", dt_bias), ("a_log", a_log), ("d_skip", d_skip)):
                    sp.dma_start(tile[:, :], dram[name].broadcast_to([P, NH])).then_inc(p_in, 16)
                sp.wait_ge(rows_ok, 1)
                sp.dma_start(dram["cum_rows"], cum_rows[:, :]).then_inc(rows_out, 16)
                sp.wait_ge(rows_out, 16)
                for g in range(G):
                    r = GT * NH
                    sp.dma_start(spread[:, g * r:(g + 1) * r, :],
                                 dram["cum_rows"][g * r:(g + 1) * r, :].rearrange("(a r) l -> a r l", a=1)
                                 .broadcast_to([P, r, P])).then_inc(spread_in, 16)

            @block.gpsimd
            def _(pool):
                pool.memset(ident[:, :], 1.0).then_inc(consts, 1)
                pool.memset(upto[:, :], 1.0).then_inc(consts, 1)
                pool.memset(mask[:, :, :], 1.0).then_inc(consts, 1)
                pool.memset(half[:, :], -0.5).then_inc(consts, 1)
                pool.memset(U[:, :, :, 0:TAPS - 1], 0.0).then_inc(consts, 1)
                pool.wait_ge(consts, 5)
                pool.affine_select(out=ident[:, :], in_=ident[:, :], compare_op=ALU.is_equal, fill=0.0,
                                   base=0, pattern=[[-1, P]], channel_multiplier=1).then_inc(consts, 1)
                for tri in (upto[:, :], mask[:, 0, :], mask[:, 2, :]):
                    pool.affine_select(out=tri, in_=tri, compare_op=ALU.is_ge, fill=0.0,
                                       base=0, pattern=[[1, P]], channel_multiplier=-1).then_inc(consts, 1)
                pool.wait_ge(var_ok, 1)
                pool.tensor_tensor(rstd[:, :], veps[:, :], half[:, :], ALU.pow).then_inc(rstd_ok, 1)

                def over(x, n):
                    return x.rearrange("p (h a) -> p h a", a=1).broadcast_to([P, NH, n])

                def segments(g):
                    if not (isinstance(g, int) and g == 0):
                        pool.wait_ge(decay_ok, g * ROWS)
                        pool.wait_ge(y_ps, g)
                    for q in range(ROWS):
                        c0 = (g * GT + q * TB) * NH
                        near, far = bass.ds(c0, NH), bass.ds(c0 + NH, NH)
                        pool.tensor_tensor(decay[:, q, 0, :, :], spread[:, near, :], over(cum[:, near], P),
                                           ALU.subtract)
                        pool.tensor_tensor(decay[:, q, 1, :, :], spread[:, far, :], over(to_end[:, near], P),
                                           ALU.add)
                        pool.tensor_tensor(decay[:, q, 2, :, :], spread[:, far, :], over(cum[:, far], P),
                                           ALU.subtract).then_inc(seg_ok, 1)

                def skip(g):
                    pool.wait_ge(xs_ok, (g + 1) * 2)
                    pool.wait_ge(y1_ok, g * ROWS + 1)
                    for t in range(GT):
                        last = pool.tensor_tensor(xskip[:, t, :].rearrange("p (h d) -> p h d", h=NH),
                                                  xs[:, t, :].rearrange("p (h d) -> p h d", h=NH),
                                                  over(d_skip[:, :], HD), ALU.mult)
                    last.then_inc(skip_ok, 1)

                def mean_square(g):
                    pool.wait_ge(msq_ok, g + 1)
                    pool.wait_ge(x_ok, g * GT + 1)
                    pool.tensor_tensor(yr[:, :], msq[:, :], half[:, 0:GT], ALU.pow).then_inc(yr_ok, 1)

                pool.wait_ge(end_ok, 1)
                pool.wait_ge(p_in, 48)
                segments(0)

                def turn(g, has_next):
                    skip(g)
                    if has_next:
                        segments(g + 1)
                    mean_square(g)

                with pool.Fori(0, G - 1) as g:
                    turn(g, True)
                turn(G - 1, False)

            @block.vector
            def _(dve):
                n = 0

                def chain(instruction):
                    nonlocal n
                    n += 1
                    instruction.then_inc(stat, 1)
                    dve.wait_ge(stat, n)

                def every(x):
                    return x.rearrange("p (a h) -> p a h", a=1).broadcast_to([P, T, NH])

                with dve.Fori(0, T) as t:
                    dve.bn_stats(stats[:, bass.ds(t, 1), :], X[:, bass.ds(t, 1), :]).then_inc(stat, 1)
                dve.wait_ge(stat, T)
                for t in range(T):
                    dve.bn_aggr(mv[:, t, :], stats[:, t, :]).then_inc(stat, 1)
                n = 2 * T
                dve.wait_ge(stat, n)
                dve.tensor_scalar(veps[:, :], mv[:, :, 1], EPS, None, ALU.add).then_inc(var_ok, 1)
                dve.wait_ge(rstd_ok, 1)
                with dve.Fori(0, T) as t:
                    dve.tensor_scalar(xn[:, bass.ds(t, 1), :], X[:, bass.ds(t, 1), :], mv[:, bass.ds(t, 1), 0],
                                      rstd[:, bass.ds(t, 1)], ALU.subtract, ALU.mult).then_inc(xn_ok, 1)
                for g in range(2):
                    dve.wait_ge(xT_ps, 2 * g + 2)
                    dve.tensor_copy(xT[:, 512 * (2 * g + 1):512 * (2 * g + 2)], bank[2 * g + 1][:, :])\
                       .then_inc(xT_ok, 1)

                dve.wait_ge(dt_ps, 1)
                dve.wait_ge(p_in, 48)
                chain(dve.tensor_tensor(raw[:, :, :], bank[4][:, 0:T * NH].rearrange("p (t h) -> p t h", h=NH),
                                        every(dt_bias[:, :]), ALU.add))
                chain(dve.tensor_scalar(mag[:, :, :], raw[:, :, :], -1.0, None, ALU.mult))
                dve.tensor_tensor(mag[:, :, :], raw[:, :, :], mag[:, :, :], ALU.max).then_inc(raw_ok, 1)
                dve.wait_ge(small_ok, 2)
                dve.tensor_scalar(onep[:, :, :], small[:, :, :], 1.0, None, ALU.add).then_inc(onep_ok, 1)
                dve.wait_ge(onep_ok, 1)
                chain(dve.tensor_scalar(step_[:, :, :], onep[:, :, :], -1.0, None, ALU.add))
                chain(dve.tensor_scalar(tiny[:, :, :], step_[:, :, :], 0.0, None, ALU.is_equal))
                chain(dve.tensor_tensor(inv[:, :, :], step_[:, :, :], tiny[:, :, :], ALU.add))
                chain(dve.reciprocal(inv[:, :, :], inv[:, :, :]))
                chain(dve.tensor_tensor(inv[:, :, :], inv[:, :, :], small[:, :, :], ALU.mult))
                chain(dve.tensor_tensor(tiny[:, :, :], tiny[:, :, :], small[:, :, :], ALU.mult))
                chain(dve.scalar_tensor_tensor(out=tiny[:, :, :], in0=raw[:, :, :], scalar=0.0, in1=tiny[:, :, :],
                                               op0=ALU.max, op1=ALU.add))
                dve.wait_ge(log_ok, 1)
                chain(dve.tensor_tensor(inv[:, :, :], inv[:, :, :], log1[:, :, :], ALU.mult))
                chain(dve.tensor_tensor(dt[:, :, :], inv[:, :, :], tiny[:, :, :], ALU.add))
                chain(dve.tensor_scalar(a_neg[:, :], a_neg[:, :], -1.0, None, ALU.mult))
                dve.tensor_tensor(dA[:, :].rearrange("p (t h) -> p t h", h=NH), dt[:, :, :], every(a_neg[:, :]),
                                  ALU.mult).then_inc(dA_ok, 1)
                dve.wait_ge(cum_ps, 1)
                dve.tensor_copy(cum[:, :], bank[5][:, 0:T * NH]).then_inc(cum_ok, 1)
                dve.wait_ge(rows_ps, 1)
                dve.tensor_copy(cum_rows[:, :], bank[6][0:T * NH, 0:P]).then_inc(rows_ok, 1)
                n0 = n

                def convolve(g):
                    for c in range(4):
                        dve.wait_ge(tap_ok, (g * 4 + c) * 2 + 2)
                        for k in range(TAPS - 1):
                            a = acc[:, c, :].rearrange("p (r l) -> p r l", r=ROWS)
                            dve.scalar_tensor_tensor(out=a, in0=U[:, c, :, k:k + N], scalar=conv_w[:, c, k:k + 1],
                                                     in1=a, op0=ALU.mult, op1=ALU.add).then_inc(conv, 1)
                            dve.wait_ge(conv, (g * 4 + c) * (TAPS - 1) + k + 1)

                dve.wait_ge(w_ok, 80)
                convolve(0)
                dve.wait_ge(spread_in, 16 * G)
                dve.tensor_tensor(to_end[:, :], spread[:, :, P - 1], cum[:, :], ALU.subtract).then_inc(end_ok, 1)

                dve.sem_inc(y1_ok, 1)
                dve.sem_inc(x_ok, 1)

                def turn(g, has_next):
                    for q in range(ROWS):
                        dve.wait_ge(seg_ok, g * ROWS + q + 1)
                        dve.tensor_scalar(decay[:, q, :, :, :], decay[:, q, :, :, :], 0.0, None, ALU.min)\
                           .then_inc(min_ok, 1)
                    for q in range(ROWS):
                        dve.wait_ge(x_ps, g * ROWS + q + 1)
                        for u in range(TB):
                            t = q * TB + u
                            last = dve.tensor_tensor(
                                xdt[:, t, :].rearrange("p (h d) -> p h d", h=NH),
                                bank[q][:, CH * u:CH * u + CH].rearrange("p (h d) -> p h d", h=NH),
                                dt[:, bass.ds(g * GT + t, 1), :].rearrange("p b (h a) -> p (b h) a", a=1)
                                .broadcast_to([P, NH, HD]), ALU.mult)
                        last.then_inc(xdt_ok, 1)
                    for q in range(ROWS):
                        dve.wait_ge(cb_ps, g * ROWS + q + 1)
                        dve.tensor_tensor(cb[:, q, :, :], bank[2 + q][:, 0:BLK * P].rearrange("p (k l) -> p k l", k=BLK),
                                          mask[:, :, :], ALU.mult).then_inc(cb_ok, 1)
                        dve.wait_ge(cb_ok, g * ROWS + q + 1)
                        dve.wait_ge(decay_ok, g * ROWS + q + 1)
                        dve.tensor_tensor(decay[:, q, :, :, :], decay[:, q, :, :, :],
                                          cb[:, q, :, :].rearrange("p k (a l) -> p k a l", a=1)
                                          .broadcast_to([P, BLK, NH, P]), ALU.mult).then_inc(m_ok, 1)
                    if has_next:
                        convolve(g + 1)
                    dve.wait_ge(skip_ok, g + 1)
                    for q in range(ROWS):
                        dve.wait_ge(y_ps, g + 1)
                        yq = y[:, q * TB:q * TB + TB, :].rearrange("p t c -> p (t c)")
                        dve.tensor_tensor(yq, bank[4 + q][:, :],
                                          xskip[:, q * TB:q * TB + TB, :].rearrange("p t c -> p (t c)"), ALU.add)\
                           .then_inc(y1_ok, 1)
                        dve.wait_ge(y1_ok, g * ROWS + q + 2)
                        dve.tensor_tensor(yq, yq, z[:, bass.ds(g * GT + q * TB, TB), :].rearrange("p t c -> p (t c)"),
                                          ALU.mult).then_inc(yg_ok, 1)
                    dve.wait_ge(ssq_ok, (g + 1) * GT + 1)
                    dve.tensor_scalar(msq[:, :], ssq[:, :], 1.0 / CH, EPS, ALU.mult, ALU.add).then_inc(msq_ok, 1)
                    dve.wait_ge(yr_ok, g + 1)
                    dve.wait_ge(o_ps, g + 1)
                    for t in range(GT):
                        Xt = X[:, bass.ds(g * GT + t, 1), :].rearrange("p a d -> p (a d)")
                        dve.scalar_tensor_tensor(out=Xt, in0=bank[6][:, D * t:D * t + D], scalar=yr[:, t:t + 1],
                                                 in1=Xt, op0=ALU.mult, op1=ALU.add).then_inc(x_ok, 1)

                with dve.Fori(0, G - 1) as g:
                    turn(g, True)
                turn(G - 1, False)

            @block.scalar
            def _(act):
                for g in range(2):
                    act.wait_ge(xT_ps, 2 * g + 1)
                    act.activation(xT[:, 1024 * g:1024 * g + 512], bank[2 * g][:, :], ACT.Copy).then_inc(xT_ok, 1)
                act.wait_ge(p_in, 48)
                act.activation(a_neg[:, :], a_log[:, :], ACT.Exp).then_inc(small_ok, 1)
                act.wait_ge(raw_ok, 1)
                act.activation(small[:, :, :], mag[:, :, :], ACT.Exp, scale=-1.0).then_inc(small_ok, 1)
                act.wait_ge(onep_ok, 1)
                act.activation(log1[:, :, :], onep[:, :, :], ACT.Ln).then_inc(log_ok, 1)

                def taps(g):
                    for c in range(4):
                        act.wait_ge(xbc_ps, g * 4 + c + 1)
                        ps = bank[(0, 1, 2, 7)[c]][:, :]
                        act.activation(U[:, c, :, TAPS - 1:TAPS - 1 + N], ps.rearrange("p (r l) -> p r l", r=ROWS),
                                       ACT.Copy).then_inc(tap_ok, 1)
                        act.activation(acc[:, c, :], ps, ACT.Identity, bias=conv_b[:, c:c + 1],
                                       scale=conv_w[:, c, TAPS - 1:TAPS]).then_inc(tap_ok, 1)

                def silu(g):
                    for c in range(4):
                        act.wait_ge(conv, (g * 4 + c + 1) * (TAPS - 1))
                        act.activation(xbc[:, c, :], acc[:, c, :], ACT.Silu).then_inc(xbc_ok, 1)

                act.wait_ge(w_ok, 80)
                taps(0)
                for t in range(T // 2):
                    act.wait_ge(z_ps, t + 1)
                    act.activation(z[:, 2 * t:2 * t + 2, :], bank[(3, 4, 5, 6)[t % 4]][:, :]
                                   .rearrange("p (t c) -> p t c", t=2), ACT.Silu).then_inc(z_ok, 1)
                silu(0)

                act.sem_inc(ssq_ok, 1)

                def turn(g, has_next):
                    for q in range(ROWS):
                        act.wait_ge(min_ok, g * ROWS + q + 1)
                        act.activation(decay[:, q, :, :, :], decay[:, q, :, :, :], ACT.Exp).then_inc(decay_ok, 1)
                    for q in range(ROWS):
                        act.wait_ge(x_ps, g * ROWS + q + 1)
                        act.wait_ge(xdt_ok, g * ROWS + q + 1)
                        act.activation(xs[:, q * TB:q * TB + TB, :], bank[q][:, :].rearrange("p (t c) -> p t c", t=TB),
                                       ACT.Copy).then_inc(xs_ok, 1)
                    if has_next:
                        taps(g + 1)
                        silu(g + 1)
                    act.wait_ge(ssq_ok, g * GT + 1)
                    for t in range(GT):
                        act.wait_ge(yg_ok, g * ROWS + t // TB + 1)
                        act.activation(squares[:, t, :], y[:, t, :], ACT.Square, accum_out=ssq[:, t:t + 1])\
                           .then_inc(ssq_ok, 1)
                    for k in range(2):
                        act.wait_ge(yT_ps, g * 2 + k + 1)
                        act.activation(yT[:, k, :], bank[4 + k][:, :], ACT.Copy, scale=norm_w[:, k:k + 1])\
                           .then_inc(yT_ok, 1)

                with act.Fori(0, G - 1) as g:
                    turn(g, True)
                turn(G - 1, False)

            @block.tensor
            def _(pe):
                pe.wait_ge(consts, 9)
                pe.wait_ge(xn_ok, T)
                for t in range(T):
                    last = pe.transpose(bank[t // 4][:, P * (t % 4):P * (t % 4) + P], xn[:, t, :], ident[:, :])
                    if t % 4 == 3:
                        last.then_inc(xT_ps, 1)
                pe.wait_ge(xT_ok, 4)
                pe.wait_ge(w_ok, 80)
                for t in range(T):
                    last = pe.matmul(bank[4][:, NH * t:NH * t + NH], xT[:, P * t:P * t + P],
                                     w_in[:, 3 * CH:3 * CH + NH], start=True, stop=True)
                last.then_inc(dt_ps, 1)

                def project(g):
                    for c in range(4):
                        pe.matmul(bank[(0, 1, 2, 7)[c]][:, :], w_in[:, CH + P * c:CH + P * c + P],
                                  xT[:, bass.ds(g * ROWS * N, ROWS * N)], start=True, stop=True).then_inc(xbc_ps, 1)

                project(0)
                pe.wait_ge(dA_ok, 1)
                pe.matmul(bank[5][:, 0:T * NH], upto[:, :], dA[:, :], start=True, stop=True).then_inc(cum_ps, 1)
                pe.wait_ge(cum_ok, 1)
                pe.transpose(bank[6][0:T * NH, 0:P], cum[:, :], ident[:, :]).then_inc(rows_ps, 1)
                pe.wait_ge(rows_ok, 1)
                for t in range(T):
                    if t % 2 == 0 and t >= 8:
                        pe.wait_ge(z_ok, t // 2 - 3)
                    last = pe.matmul(bank[(3, 4, 5, 6)[t // 2 % 4]][:, CH * (t % 2):CH * (t % 2) + CH],
                                     xT[:, P * t:P * t + P], w_in[:, 0:CH], start=True, stop=True)
                    if t % 2:
                        last.then_inc(z_ps, 1)
                pe.wait_ge(z_ok, T // 2)

                def turn(g, has_next):
                    pe.wait_ge(xbc_ok, g * 4 + 4)
                    for q in range(ROWS):
                        for u in range(TB):
                            for k in range(2):
                                last = pe.transpose(bank[q][:, CH * u + P * k:CH * u + P * k + P],
                                                    xbc[:, k, P * (q * TB + u):P * (q * TB + u) + P], ident[:, :])
                        last.then_inc(x_ps, 1)
                    for q in range(ROWS):
                        s = N * q
                        pe.matmul(bank[2 + q][:, 0:N], xbc[:, 2, s:s + P], xbc[:, 3, s:s + N], start=True, stop=True)
                        pe.matmul(bank[2 + q][:, N:N + P], xbc[:, 2, s + P:s + N], xbc[:, 3, s + P:s + N],
                                  start=True, stop=True).then_inc(cb_ps, 1)
                    if has_next:
                        pe.wait_ge(xs_ok, g * 2 + 2)
                        pe.wait_ge(cb_ok, g * ROWS + 2)
                        project(g + 1)
                    for q in range(ROWS):
                        pe.wait_ge(m_ok, g * ROWS + q + 1)
                        pe.wait_ge(xdt_ok, g * ROWS + q + 1)
                        for u in range(TB):
                            for h in range(NH):
                                for s in range(u + 1):
                                    last = pe.matmul(bank[4 + q][:, CH * u + HD * h:CH * u + HD * h + HD],
                                                     decay[:, q, u + s, h, :],
                                                     xdt[:, q * TB + s, HD * h:HD * h + HD],
                                                     start=(s == 0), stop=(s == u))
                    last.then_inc(y_ps, 1)
                    pe.wait_ge(yg_ok, g * ROWS + ROWS)
                    for k in range(2):
                        for t in range(GT):
                            last = pe.transpose(bank[4 + k][:, P * t:P * t + P], y[:, t, P * k:P * k + P], ident[:, :])
                        last.then_inc(yT_ps, 1)
                    pe.wait_ge(yT_ok, g * 2 + 2)
                    pe.wait_ge(x_ok, g * GT + 1)
                    for t in range(GT):
                        for k in range(2):
                            last = pe.matmul(bank[6][:, D * t:D * t + D], yT[:, k, P * t:P * t + P], w_out[:, k, :],
                                             start=(k == 0), stop=(k == 1))
                    last.then_inc(o_ps, 1)

                with pe.Fori(0, G - 1) as g:
                    turn(g, True)
                turn(G - 1, False)


W_SHAPES = {"s1": [P, HID], "s2": [P, HC * D], "e1": [P, E_N * HID], "e2": [P, E_N * HC * D], "gate": [P, E_N]}


def hybrid_kernel(nc, dram, out, phases="afmf"):
    dram = dict(dram)
    for layer in range(LAYERS):
        dram[f"slots{layer}"] = nc.dram_tensor(f"slots{layer}", [NSLOT * P, ROW], F32).ap()
        dram[f"results{layer}"] = nc.dram_tensor(f"results{layer}", [RESULTS + NSLOT * P, D], F32).ap()
    dram["cum_rows"] = nc.dram_tensor("cum_rows", [T * NH, P], F32).ap()
    with ExitStack() as ctx:
        X = ctx.enter_context(nc.sbuf_tensor("X", [P, T, D], F32))
        w = {n: ctx.enter_context(nc.sbuf_tensor(f"w_{n}", s, F32)) for n, s in W_SHAPES.items()}
        stored = ctx.enter_context(nc.semaphore("stored"))
        layer = 0
        sems = []
        for phase in phases:
            if phase == "a":
                attention_phase(nc, sems, dram, X, w)
            elif phase == "f":
                ffn_phase(nc, sems, dram, X, w, layer)
                layer += 1
            elif phase == "m":
                mixer_phase(nc, sems, dram, X)
            end_phase(nc, sems)
        with nc.Block() as block:
            @block.sync
            def _(sp):
                sp.dma_start(out.rearrange("(t p) d -> p t d", p=P), X[:, :, :]).then_inc(stored, 16)
                sp.wait_ge(stored, 16)


def laid_out(i):
    c = np.ascontiguousarray
    a, b, f = (lambda n, k=k: np.asarray(i[k + n]) for k in ("L0_attn_a_", "L0_attn_b_", "L0_ffn_"))
    return {
        "x": c(a("x").reshape(B * N, D)), "wq": c(a("Wq")), "wk": c(a("Wk")), "wv": c(a("Wv")),
        "wo": c(a("Wo")), "bo": c(a("bo")),
        "s1": c(f("shared_w1").T),
        "s2": c(f("shared_w2").reshape(D, HC, P).transpose(2, 1, 0).reshape(P, HC * D)),
        "e1": c(f("experts_w1").transpose(2, 0, 1).reshape(D, E_N * HID)),
        "e2": c(f("experts_w2").reshape(E_N, D, HC, P).transpose(3, 0, 2, 1).reshape(P, E_N * HC * D)),
        "gate": c(f("gate_w").T),
        "w_in": c(b("W_in").T), "conv_w": c(b("conv_w").reshape(4, P, 4).transpose(1, 0, 2)),
        "conv_b": c(b("conv_b").reshape(4, P).T), "dt_bias": c(b("dt_bias").reshape(1, 4)),
        "a_log": c(b("A_log").reshape(1, 4)), "d_skip": c(b("D").reshape(1, 4)),
        "norm_w": c(b("norm_w").reshape(2, P).T),
        "w_out": c(b("W_out").T.reshape(2, P, D).transpose(1, 0, 2)),
    }


def kernel(**inputs):
    import concourse.bacc as bacc
    from concourse.bass_utils import run_bass_kernel_spmd

    nc = bacc.Bacc("TRN2", target_bir_lowering=False, num_devices=1)
    arrays = {f"in_{n}": a for n, a in laid_out(inputs).items()}
    dram = {n[3:]: nc.dram_tensor(n, list(a.shape), F32, kind="ExternalInput").ap() for n, a in arrays.items()}
    out = nc.dram_tensor("out_x", [B * N, D], F32, kind="ExternalOutput").ap()
    hybrid_kernel(nc, dram, out)
    result = run_bass_kernel_spmd(nc, [arrays], core_ids=[0])
    return result.results[0]["out_x"].reshape(B, N, D)
```

```python
from contextlib import ExitStack

import numpy as np
import concourse.bass as bass
from concourse import mybir
from concourse.alu_op_type import AluOpType as ALU

F32 = mybir.dt.float32
F32R = mybir.dt.float32r
BF16 = mybir.dt.bfloat16
I32 = mybir.dt.int32
U32 = mybir.dt.uint32
ACT = mybir.ActivationFunctionType
AX = mybir.AxisListType

P = 128
B, N, D = 8, 256, 128
T = B * N // P
TB = N // P
GROUP = 4
GROUPS = T // GROUP
STREAM = 96
H, DH = 16, 64
PAIRS = H // 2
EPS = 1e-5
SCALE = DH ** -0.5
LARGE = 3.0e38


def phase_semaphore(nc, sems, name):
    sems.append(nc.alloc_semaphore(name))
    return sems[-1]


def end_phase(nc, sems):
    nc.clear_and_free_semaphores(sems)
    nc.all_engine_barrier()
    sems.clear()


class Norm:

    def __init__(self, nc, ctx):
        def sb(name, shape):
            return ctx.enter_context(nc.sbuf_tensor(f"norm_{name}", shape, F32))

        self.stats = sb("stats", [P, T, 6])
        self.mv = sb("mv", [P, T, 2])
        self.veps = sb("veps", [P, T])
        self.half = sb("half", [P, T])
        self.rstd = sb("rstd", [P, T])
        self.shift = sb("shift", [P, T])
        self.xn = sb("xn", [P, T, ROW])
        self.ident = sb("ident", [P, P])

    def statistics(self, dve, X, g, mean_ok):
        tiles = range(GROUP * g, GROUP * g + GROUP)
        for t in tiles:
            dve.bn_stats(self.stats[:, t, :], X[:, t, :]).then_inc(mean_ok, 1)
        dve.wait_ge(mean_ok, 2 * GROUP * g + GROUP)
        for t in tiles:
            dve.bn_aggr(self.mv[:, t, :], self.stats[:, t, :]).then_inc(mean_ok, 1)

    def roots(self, pool, g, mean_ok, root_ok):
        s = slice(GROUP * g, GROUP * g + GROUP)
        pool.wait_ge(mean_ok, 2 * GROUP * (g + 1))
        pool.tensor_scalar(self.veps[:, s], self.mv[:, s, 1], EPS, None, ALU.add).then_inc(root_ok, 1)
        pool.wait_ge(root_ok, 3 * g + 1)
        pool.tensor_tensor(self.rstd[:, s], self.veps[:, s], self.half[:, s], ALU.pow).then_inc(root_ok, 1)
        pool.wait_ge(root_ok, 3 * g + 2)
        pool.tensor_tensor(self.shift[:, s], self.mv[:, s, 0], self.rstd[:, s], ALU.mult).then_inc(root_ok, 1)

    def normalise(self, act, X, g, root_ok, neg_ok, xn_ok):
        act.wait_ge(root_ok, 3 * (g + 1))
        s = slice(GROUP * g, GROUP * g + GROUP)
        act.activation(self.shift[:, s], self.shift[:, s], ACT.Copy, scale=-1.0).then_inc(neg_ok, 1)
        act.wait_ge(neg_ok, g + 1)
        for t in range(GROUP * g, GROUP * g + GROUP):
            act.activation(self.xn[:, t, 0:D], X[:, t, :], ACT.Identity, scale=self.rstd[:, t:t + 1],
                           bias=self.shift[:, t:t + 1]).then_inc(xn_ok, 1)


def product(pe, out, lhsT, rhs, start=True, stop=True):
    for i, (a, b) in enumerate(((0, 0), (0, 1), (1, 0))):
        last = pe.matmul(out, lhsT[a], rhs[b], start=start and i == 0, stop=stop and i == 2)
    return last


def attention_steps(behind, jobs, ahead):
    s = []
    for p in range(PAIRS):
        s.append(("scores", p))
        if behind and p == 0:
            s.append(("outT", -2))
        if jobs:
            s.append(("q", p))
        if behind and p == 0:
            s.append(("outT", -1))
        if p == 1 and behind:
            s.append(("project", 0))
        if p >= 1:
            s.append(("turn", p - 1))
        s.append(("exps", p))
        if jobs:
            s.append(("k", p))
        if p >= 2:
            s.append(("values", p - 2))
        if p >= 3:
            s.append(("outT", p - 3))
        if behind and p in (1, 4):
            s.append(("next_stats" if p == 1 else "next_norm", 0))
        if ahead and p in (3, 5):
            s.append(("stats" if p == 3 else "norm", 0))
    v = [[("v", i)] if jobs else [] for i in range(4)]
    s += v[0] + [("turn", 7), ("values", 6)] + v[1] + [("outT", 5), ("values", 7)]
    if not jobs:
        return s + [("outT", 6), ("outT", 7), ("project", 1)]
    return s + v[2] + v[3] + ([("xT", 0)] if ahead else [])


def attention_phase(nc, sems, dram, X, w, norm):
    QW = 3 * P
    with ExitStack() as ctx:
        def sb(name, shape, dt=F32):
            return ctx.enter_context(nc.sbuf_tensor(name, shape, dt))

        def sem(name):
            return phase_semaphore(nc, sems, name)

        wq = sb("wq", [P, 2, H * DH], F32R)
        wk = sb("wk", [P, 2, H * DH], F32R)
        wv = sb("wv", [P, 2, H * DH], F32R)
        xT = sb("xT", [P, 2, N], F32R)
        w_raw = sb("w_raw", [P, 2, H * DH])
        wo = sb("wo", [P, PAIRS * D])
        bo = sb("bo", [P, D])
        ident = norm.ident
        rel_i = sb("rel_i", [P, QW], I32)
        rel = sb("rel", [P, QW])
        relm = sb("relm", [P, QW])
        bias = sb("bias", [P, H, QW])
        stats = sb("stats", [P, TB, 6])
        mv = sb("mv", [P, TB, 2])
        veps = sb("veps", [P, TB])
        half = sb("half", [P, TB])
        rstd = sb("rstd", [P, TB])
        xn = sb("xn", [P, TB, D])
        next_stats = sb("next_stats", [P, TB, 6])
        next_mv = sb("next_mv", [P, TB, 2])
        next_veps = sb("next_veps", [P, TB])
        next_rstd = sb("next_rstd", [P, TB])
        qT = sb("qT", [P, PAIRS, N])
        kT = sb("kT", [P, PAIRS, N])
        V = sb("V", [P, TB, H, DH + 1])
        S = sb("S", [P, 4, QW])
        low = sb("low", [P, 4, 2])
        E = sb("E", [P, 4, QW])
        ET = sb("ET", [P, 2, 2, QW])
        rden = sb("rden", [P, 2, 4])
        O = sb("O", [P, TB, H * DH])
        OT = sb("OT", [P, PAIRS, N])
        bank = [ctx.enter_context(nc.psum_tensor(f"bank{i}", [P, 512], F32)) for i in range(8)]
        turned = [bank[4], bank[5]]
        O_ps, side = bank[6], bank[7]
        job = bank[3]
        first_q, first_k = bank[2:4], bank[5:7]
        v_bank = [bank[1], bank[2], bank[3], bank[4]]

        CLEAR = NSLOT // 3
        clear = sb("clear", [P, CLEAR, ROW])
        clear_i = sb("clear_i", [P, NSLOT], I32)

        later_in = sem("later_in")
        clear_ok = sem("clear_ok")
        cleared = sem("cleared")
        x_in = sem("x_in")
        x_rest = sem("x_rest")
        w_in = {name: sem(f"{name}_in") for name in ("wq", "wk", "wv")}
        wo_in = sem("wo_in")
        lead_ok = sem("lead_ok")
        rest_ok = sem("rest_ok")
        bo_in = sem("bo_in")
        consts = sem("consts")
        bias_ok = sem("bias_ok")
        xb_ok = sem("xb_ok")
        mean_ok = sem("mean_ok")
        var_ok = sem("var_ok")
        rstd_ok = sem("rstd_ok")
        xn_ok = sem("xn_ok")
        next_mean = sem("next_mean")
        next_var = sem("next_var")
        next_root = sem("next_root")
        next_xn = sem("next_xn")
        s_ok = sem("s_ok")
        low_ok = sem("low_ok")
        e_ok = sem("e_ok")
        et_ps = sem("et_ps")
        et_even = sem("et_even")
        et_odd = sem("et_odd")
        o_ps = sem("o_ps")
        rden_ok = sem("rden_ok")
        o_ok = sem("o_ok")
        outT_ps = sem("outT_ps")
        outT_ok = sem("outT_ok")
        xT_ps = sem("xT_ps")
        xT_ok = sem("xT_ok")
        xT_rest = sem("xT_rest")
        q_ps = sem("q_ps")
        q_ok = sem("q_ok")
        k_ps = sem("k_ps")
        k_ok = sem("k_ok")
        v_ps = sem("v_ps")
        v_even = sem("v_even")
        v_odd = sem("v_odd")
        y_ps = sem("y_ps")
        x_ok = sem("x_ok")
        passed = sem("passed")

        WEIGHTS = {"wq": wq, "wk": wk, "wv": wv}

        def v_part(i):
            return V[:, i // 2, 8 * (i % 2):8 * (i % 2) + 8, 0:DH]

        def rows(run, eng):
            run(0, attention_steps(False, True, True))
            with eng.Fori(1, B - 2) as b:
                run(b, attention_steps(True, True, True))
            run(B - 2, attention_steps(True, True, False))
            run(B - 1, attention_steps(True, False, False))

        with nc.Block() as block:
            @block.sync
            def _(sp):
                x_tiles = dram["x"].rearrange("(t p) d -> p t d", p=P)
                sp.dma_start(X[:, 0:2 * TB, :], x_tiles[:, 0:2 * TB, :]).then_inc(x_in, 16)
                for i, name in enumerate(WEIGHTS):
                    if i >= 2:
                        sp.wait_ge(rest_ok, i - 1)
                    sp.dma_start(w_raw[:, i % 2, :], dram[name]).then_inc(w_in[name], 16)
                    if i == 1:
                        sp.dma_start(wo[:, :], dram["wo"]).then_inc(wo_in, 16)
                        sp.dma_start(X[:, 2 * TB:T, :], x_tiles[:, 2 * TB:T, :]).then_inc(x_rest, 16)
                for name in w:
                    sp.dma_start(w[name][:, :], dram[name]).then_inc(later_in, 16)
                sp.wait_ge(clear_ok, 1)
                for c in range(3):
                    sp.wait_ge(clear_ok, c + 1)
                    for layer in range(LAYERS):
                        sp.dma_start(dram[f"slots{layer}"].rearrange("(c t p) d -> c p t d", p=P, c=3)[c],
                                     clear[:, :, :]).then_inc(cleared, 16)
                sp.wait_ge(later_in, 16 * len(w))
                sp.wait_ge(cleared, 16 * 3 * LAYERS)

            @block.gpsimd
            def _(pool):
                def reciprocal_root(b):
                    pool.wait_ge(var_ok, b + 1)
                    pool.tensor_tensor(rstd[:, :], veps[:, :], half[:, :], ALU.pow).then_inc(rstd_ok, 1)

                pool.dma_start(bo[:, :], dram["bo"].rearrange("(a d) -> a d", a=1).broadcast_to([P, D]))\
                    .then_inc(bo_in, 16)
                pool.memset(ident[:, :], 1.0).then_inc(consts, 1)
                pool.wait_ge(consts, 1)
                pool.affine_select(out=ident[:, :], in_=ident[:, :], compare_op=ALU.is_equal, fill=0.0,
                                   base=0, pattern=[[-1, P]], channel_multiplier=1).then_inc(consts, 1)
                pool.memset(half[:, :], -0.5).then_inc(consts, 1)
                pool.memset(norm.half[:, :], -0.5)
                pool.memset(V[:, :, :, DH:DH + 1], 1.0).then_inc(consts, 1)
                pool.wait_ge(consts, 4)
                reciprocal_root(0)
                pool.iota(rel_i[:, 0:P], [[-1, P]], base=0, channel_multiplier=1).then_inc(consts, 1)
                pool.iota(rel_i[:, P:QW], [[-1, N]], base=P, channel_multiplier=1).then_inc(consts, 1)
                pool.wait_ge(consts, 6)
                pool.tensor_copy(rel[:, :], rel_i[:, :]).then_inc(consts, 1)
                pool.wait_ge(consts, 7)
                pool.affine_select(out=relm[:, 0:P], in_=rel[:, 0:P], compare_op=ALU.is_ge, fill=-1e33,
                                   base=0, pattern=[[-1, P]], channel_multiplier=1).then_inc(consts, 1)
                pool.affine_select(out=relm[:, P:QW], in_=rel[:, P:QW], compare_op=ALU.is_ge, fill=-1e33,
                                   base=P, pattern=[[-1, N]], channel_multiplier=1).then_inc(consts, 1)
                pool.wait_ge(consts, 9)
                root = np.float32((2.0 ** 8) ** (1.0 / H))
                slopes = (np.float32(1.0) / root ** np.arange(1, H + 1, dtype=np.float32)) / np.float32(SCALE)

                for h in range(H):
                    if h == 6:
                        reciprocal_root(1)
                    pool.tensor_scalar(bias[:, h, :], relm[:, :], float(slopes[h]), None, ALU.mult)\
                        .then_inc(bias_ok, 1)

                def add_bo(b):
                    pool.wait_ge(xn_ok, b + 1)
                    Xb = X[:, bass.ds(b * TB, TB), :]
                    pool.tensor_tensor(Xb, Xb, bo[:, :].rearrange("p (a d) -> p a d", a=1).broadcast_to([P, TB, D]),
                                       ALU.add).then_inc(xb_ok, 1)

                pool.wait_ge(bo_in, 16)
                for b in range(2):
                    add_bo(b)

                def next_reciprocal_root(b):
                    pool.wait_ge(next_var, b + 1)
                    if not (isinstance(b, int) and b == 0):
                        pool.wait_ge(next_xn, b)
                    pool.tensor_tensor(next_rstd[:, :], next_veps[:, :], half[:, :], ALU.pow)\
                        .then_inc(next_root, 1)

                reciprocal_root(2)
                add_bo(2)
                next_reciprocal_root(0)
                reciprocal_root(3)
                add_bo(3)
                with pool.Fori(1, B - 3) as b:
                    next_reciprocal_root(b)
                    reciprocal_root(b + 3)
                    add_bo(b + 3)
                pool.memset(clear[:, :, :], 0.0).then_inc(consts, 1)
                pool.iota(clear_i[:, :], [[P, NSLOT]], base=RESULTS, channel_multiplier=1).then_inc(consts, 1)
                pool.wait_ge(consts, 11)
                for c in range(3):
                    if c:
                        pool.wait_ge(cleared, 16 * LAYERS * c)
                    pool.tensor_copy(clear[:, :, D], clear_i[:, CLEAR * c:CLEAR * c + CLEAR]).then_inc(clear_ok, 1)
                for b in range(B - 3, B):
                    next_reciprocal_root(b)

            @block.vector
            def _(dve):
                def row_stats(b):
                    for t in range(TB):
                        dve.bn_stats(stats[:, t, :], X[:, bass.ds(b * TB + t, 1), :]).then_inc(mean_ok, 1)
                    dve.wait_ge(mean_ok, b * 4 + 2)
                    dve.sem_inc(passed, 1)
                    for t in range(TB):
                        dve.bn_aggr(mv[:, t, :], stats[:, t, :]).then_inc(mean_ok, 1)
                    dve.wait_ge(mean_ok, b * 4 + 4)
                    dve.tensor_scalar(veps[:, :], mv[:, :, 1], EPS, None, ALU.add).then_inc(var_ok, 1)

                def row_norm(b):
                    dve.wait_ge(rstd_ok, b + 1)
                    if not (isinstance(b, int) and b == 0):
                        dve.wait_ge(xT_ps, b)
                    for t in range(TB):
                        last = dve.tensor_scalar(xn[:, t, :], X[:, bass.ds(b * TB + t, 1), :],
                                                 mv[:, t, 0:1], rstd[:, t:t + 1], ALU.subtract, ALU.mult)
                    last.then_inc(xn_ok, 1)

                def stats_after(b):
                    dve.wait_ge(x_ok, b + 1)
                    dve.sem_inc(passed, 1)
                    for t in range(TB):
                        dve.bn_stats(next_stats[:, t, :], X[:, bass.ds(b * TB + t, 1), :]).then_inc(next_mean, 1)
                    dve.wait_ge(next_mean, b * 4 + 2)
                    dve.sem_inc(passed, 1)
                    for t in range(TB):
                        dve.bn_aggr(next_mv[:, t, :], next_stats[:, t, :]).then_inc(next_mean, 1)
                    dve.wait_ge(next_mean, b * 4 + 4)
                    dve.tensor_scalar(next_veps[:, :], next_mv[:, :, 1], EPS, None, ALU.add).then_inc(next_var, 1)

                def norm_after(b):
                    dve.wait_ge(next_root, b + 1)
                    for t in range(TB):
                        last = dve.tensor_scalar(norm.xn[:, bass.ds(b * TB + t, 1), 0:D],
                                                 X[:, bass.ds(b * TB + t, 1), :], next_mv[:, t, 0:1],
                                                 next_rstd[:, t:t + 1], ALU.subtract, ALU.mult)
                    last.then_inc(next_xn, 1)

                def xT_left(b):
                    dve.wait_ge(xT_ok, b + 1)
                    dve.tensor_tensor(xT[:, 1, :], side[:, 0:N], xT[:, 0, :], ALU.subtract).then_inc(xT_rest, 1)

                def k_out(b, p, ps):
                    dve.wait_ge(k_ps, b * PAIRS + p + 1)
                    dve.tensor_copy(kT[:, p, :], ps[:, 0:N]).then_inc(k_ok, 1)

                def v_out(b, i):
                    if i % 2:
                        dve.wait_ge(v_ps, b * 4 + i + 1)
                        dve.tensor_copy(v_part(i), v_bank[i][:, :].rearrange("p (h d) -> p h d", d=DH))\
                           .then_inc(v_odd, 1)

                def run(b, steps):
                    for step, p in steps:
                        if step == "scores":
                            for h in (2 * p, 2 * p + 1):
                                dve.wait_ge(bias_ok, h + 1)
                                dve.wait_ge(s_ok, b * H + h + 1)
                                if h >= 4:
                                    dve.wait_ge(e_ok, b * H + h - 3)
                                dve.sem_inc(passed, 1)
                                sc = bank[h % 3]
                                for q, (c0, c1) in enumerate(((0, P), (P, QW))):
                                    last = dve.tensor_tensor_reduce(
                                        S[:, h % 4, c0:c1], sc[:, c0:c1], bias[:, h, c0:c1], -SCALE, LARGE,
                                        ALU.add, ALU.min, low[:, h % 4, q:q + 1])
                                last.then_inc(low_ok, 1)
                        elif step == "turn":
                            dve.wait_ge(et_ps, b * H + 2 * p + 2)
                            if p >= 2:
                                dve.wait_ge(o_ps, b * PAIRS + p - 1)
                            dve.tensor_copy(ET[:, p % 2, 1, :], turned[1][:, 0:QW]).then_inc(et_odd, 1)
                        elif step == "values":
                            dve.wait_ge(o_ps, b * PAIRS + p + 1)
                            ov = O_ps[:, 0:4 * (DH + 1)].rearrange("p (h t d) -> p t h d", h=2, t=TB)
                            dve.reciprocal(rden[:, p % 2, :].rearrange("p (t h) -> p t h", t=TB),
                                           ov[:, :, :, DH]).then_inc(rden_ok, 1)
                            dve.wait_ge(rden_ok, b * PAIRS + p + 1)
                            for t in range(TB):
                                last = dve.tensor_tensor(
                                    O[:, t, P * p:P * p + P].rearrange("p (h d) -> p h d", h=2),
                                    ov[:, t, :, 0:DH],
                                    rden[:, p % 2, 2 * t:2 * t + 2].rearrange("p (h a) -> p h a", a=1)
                                    .broadcast_to([P, 2, DH]), ALU.mult)
                            last.then_inc(o_ok, 1)
                            if p == PAIRS - 1 and ("v", 0) in steps:
                                v_out(b + 1, 1)
                        elif step == "v" and p == 3:
                            v_out(b + 1, p)
                        elif step == "k":
                            k_out(b + 1, p, job)
                        elif step == "stats":
                            row_stats(b + 2)
                        elif step == "norm":
                            row_norm(b + 2)
                        elif step == "project":
                            r = b - 1 + p
                            dve.wait_ge(y_ps, r + 1)
                            dve.wait_ge(xb_ok, r + 1)
                            Xr = X[:, bass.ds(r * TB, TB), :]
                            dve.tensor_tensor(Xr, O_ps[:, 0:TB * D].rearrange("p (t d) -> p t d", t=TB), Xr,
                                              ALU.add).then_inc(x_ok, 1)
                        elif step == "xT":
                            xT_left(b + 2)
                        elif step == "next_stats":
                            stats_after(b - 1)
                        elif step == "next_norm":
                            norm_after(b - 1)

                def weights_left(i, name):
                    dve.wait_ge(lead_ok, i + 1)
                    dve.tensor_tensor(WEIGHTS[name][:, 1, :], w_raw[:, i % 2, :], WEIGHTS[name][:, 0, :],
                                      ALU.subtract).then_inc(rest_ok, 1)

                dve.wait_ge(x_in, 16)
                row_stats(0)
                row_norm(0)
                weights_left(0, "wq")
                xT_left(0)
                weights_left(1, "wk")
                for p in range(PAIRS):
                    k_out(0, p, first_k[p % 2])
                    if p == 2:
                        weights_left(2, "wv")
                    elif p == 4:
                        row_stats(1)
                row_norm(1)
                for i in range(4):
                    v_out(0, i)
                xT_left(1)
                dve.wait_ge(x_rest, 16)
                rows(run, dve)
                stats_after(B - 1)
                norm_after(B - 1)

            @block.scalar
            def _(act):
                def q_out(b, p, ps):
                    act.wait_ge(q_ps, b * PAIRS + p + 1)
                    act.activation(qT[:, p, :], ps[:, 0:N], ACT.Copy).then_inc(q_ok, 1)

                def v_out(b, i):
                    if i % 2 == 0:
                        act.wait_ge(v_ps, b * 4 + i + 1)
                        act.activation(v_part(i), v_bank[i][:, :].rearrange("p (h d) -> p h d", d=DH), ACT.Copy)\
                           .then_inc(v_even, 1)

                def xT_out(b):
                    act.wait_ge(xT_ps, b + 1)
                    act.activation(xT[:, 0, :], side[:, 0:N], ACT.Copy).then_inc(xT_ok, 1)

                def weights_lead(i, name):
                    act.wait_ge(w_in[name], 16)
                    act.activation(WEIGHTS[name][:, 0, :], w_raw[:, i % 2, :], ACT.Copy).then_inc(lead_ok, 1)

                def run(b, steps):
                    for step, p in steps:
                        if step == "exps":
                            for h in (2 * p, 2 * p + 1):
                                act.wait_ge(low_ok, b * H + h + 1)
                                if h >= 4:
                                    act.wait_ge(et_ps, b * H + h - 3)
                                for q, (c0, c1) in enumerate(((0, P), (P, QW))):
                                    last = act.activation(E[:, h % 4, c0:c1], S[:, h % 4, c0:c1], ACT.Exp,
                                                          bias=low[:, h % 4, q:q + 1], scale=-1.0)
                                last.then_inc(e_ok, 1)
                        elif step == "turn":
                            act.wait_ge(et_ps, b * H + 2 * p + 1)
                            if p >= 2:
                                act.wait_ge(o_ps, b * PAIRS + p - 1)
                            act.activation(ET[:, p % 2, 0, :], turned[0][:, 0:QW], ACT.Copy)\
                               .then_inc(et_even, 1)
                        elif step == "outT":
                            act.wait_ge(outT_ps, b * PAIRS + p + 1)
                            act.activation(OT[:, p % PAIRS, :], side[:, 0:N], ACT.Copy).then_inc(outT_ok, 1)
                        elif step == "q":
                            q_out(b + 1, p, job)
                        elif step == "v" and p == 2:
                            act.wait_ge(o_ps, b * PAIRS + PAIRS)
                            v_out(b + 1, 0)
                            v_out(b + 1, 2)
                        elif step == "xT":
                            xT_out(b + 2)

                weights_lead(0, "wq")
                xT_out(0)
                weights_lead(1, "wk")
                for p in range(PAIRS):
                    q_out(0, p, first_q[p % 2])
                    if p == 2:
                        weights_lead(2, "wv")
                for i in range(4):
                    v_out(0, i)
                xT_out(1)
                rows(run, act)

            @block.tensor
            def _(pe):
                def parts(x, start, width):
                    return [x[:, i, start:start + width] for i in range(2)]

                def transposes_x(b):
                    pe.wait_ge(xn_ok, b + 1)
                    for t in range(TB):
                        last = pe.transpose(side[:, P * t:P * t + P], xn[:, t, :], ident[:, :])
                    last.then_inc(xT_ps, 1)

                def q_chunk(b, p, ps):
                    product(pe, ps[:, 0:N], parts(wq, P * p, P), parts(xT, 0, N)).then_inc(q_ps, 1)

                def k_chunk(b, p, ps):
                    product(pe, ps[:, 0:N], parts(wk, P * p, P), parts(xT, 0, N)).then_inc(k_ps, 1)

                def v_quarter(b, i):
                    product(pe, v_bank[i][:, :], parts(xT, P * (i // 2), P), parts(wv, 512 * (i % 2), 512))\
                        .then_inc(v_ps, 1)

                def run(b, steps):
                    behind = ("project", 0) in steps
                    jobs = ("v", 0) in steps
                    ahead = ("xT", 0) in steps
                    for step, p in steps:
                        if step == "scores":
                            if p == 0:
                                pe.wait_ge(q_ok, (b + 1) * PAIRS)
                                pe.wait_ge(k_ok, (b + 1) * PAIRS)
                            for h in (2 * p, 2 * p + 1):
                                if h >= 3:
                                    pe.wait_ge(low_ok, b * H + h - 2)
                                elif h == 1:
                                    pe.wait_ge(v_even, b * 2 + 1)
                                elif h == 2:
                                    pe.wait_ge(v_odd, b * 2 + 1)
                                r = slice(DH * (h % 2), DH * (h % 2) + DH)
                                sc = bank[h % 3]
                                pe.matmul(sc[:, 0:P], qT[r, p, 0:P], kT[r, p, 0:P], start=True, stop=True)
                                pe.matmul(sc[:, P:QW], qT[r, p, P:N], kT[r, p, :], start=True, stop=True)\
                                  .then_inc(s_ok, 1)
                        elif step == "turn":
                            for h in (2 * p, 2 * p + 1):
                                pe.wait_ge(e_ok, b * H + h + 1)
                                if p >= 1:
                                    pe.wait_ge(et_odd if h % 2 else et_even, b * PAIRS + p)
                                elif h == 0:
                                    pe.wait_ge(v_odd, b * 2 + 2)
                                for k in range(3):
                                    last = pe.transpose(turned[h % 2][:, P * k:P * k + P],
                                                        E[:, h % 4, P * k:P * k + P], ident[:, :])
                                last.then_inc(et_ps, 1)
                        elif step == "values":
                            if p == 0:
                                if behind:
                                    pe.wait_ge(x_ok, b)
                                pe.wait_ge(v_even, b * 2 + 2)
                                pe.wait_ge(v_odd, b * 2 + 2)
                            else:
                                pe.wait_ge(o_ok, b * PAIRS + p)
                            pe.wait_ge(et_even, b * PAIRS + p + 1)
                            pe.wait_ge(et_odd, b * PAIRS + p + 1)
                            for e in range(2):
                                h = 2 * p + e
                                for t in range(TB):
                                    c = (2 * e + t) * (DH + 1)
                                    for k in range(t + 1):
                                        last = pe.matmul(O_ps[:, c:c + DH + 1],
                                                         ET[:, p % 2, e, P * (t + k):P * (t + k) + P],
                                                         V[:, k, h, :], start=(k == 0), stop=(k == t))
                            last.then_inc(o_ps, 1)
                        elif step == "outT":
                            pe.wait_ge(o_ok, b * PAIRS + p + 1)
                            if p == -2 and jobs:
                                pe.wait_ge(xT_rest, b + 2)
                            elif p != 0 or behind:
                                pe.wait_ge(outT_ok, b * PAIRS + p)
                            else:
                                pe.wait_ge(xT_rest, 2)
                            q = p % PAIRS
                            for t in range(TB):
                                last = pe.transpose(side[:, P * t:P * t + P], O[:, t, P * q:P * q + P], ident[:, :])
                            last.then_inc(outT_ps, 1)
                        elif step == "xT":
                            pe.wait_ge(outT_ok, b * PAIRS + PAIRS - 2)
                            transposes_x(b + 2)
                        elif step == "q":
                            if p == 0:
                                pe.wait_ge(xT_rest, b + 2)
                                pe.wait_ge(v_even, b * 2 + 2)
                            else:
                                pe.wait_ge(k_ok, (b + 1) * PAIRS + p)
                            q_chunk(b + 1, p, job)
                        elif step == "k":
                            pe.wait_ge(q_ok, (b + 1) * PAIRS + p + 1)
                            k_chunk(b + 1, p, job)
                        elif step == "v":
                            if p == 0:
                                pe.wait_ge(low_ok, b * H + H)
                            elif p == 2:
                                pe.wait_ge(k_ok, (b + 2) * PAIRS)
                            elif p == 3:
                                pe.wait_ge(et_even, b * PAIRS + PAIRS)
                            v_quarter(b + 1, p)
                        elif step == "project":
                            r = b - 1 + p
                            pe.wait_ge(outT_ok, r * PAIRS + PAIRS)
                            pe.wait_ge(o_ok, r * PAIRS + PAIRS)
                            pe.wait_ge(wo_in, 16)
                            for t in range(TB):
                                for c in range(PAIRS):
                                    last = pe.matmul(O_ps[:, D * t:D * t + D], OT[:, c, P * t:P * t + P],
                                                     wo[:, D * c:D * c + D], start=(c == 0), stop=(c == PAIRS - 1))
                            last.then_inc(y_ps, 1)

                pe.wait_ge(consts, 4)
                transposes_x(0)
                pe.wait_ge(xT_rest, 1)
                for p in range(PAIRS):
                    if p < 2:
                        pe.wait_ge(rest_ok, 1)
                    else:
                        pe.wait_ge(q_ok, p - 1)
                    q_chunk(0, p, first_q[p % 2])
                    if p < 2:
                        pe.wait_ge(rest_ok, 2)
                    else:
                        pe.wait_ge(k_ok, p - 1)
                    k_chunk(0, p, first_k[p % 2])
                pe.wait_ge(rest_ok, 3)
                pe.wait_ge(q_ok, PAIRS)
                pe.wait_ge(k_ok, PAIRS)
                for i in range(4):
                    v_quarter(0, i)
                transposes_x(1)
                rows(run, pe)


E_N = 8
HID = 512
HC = HID // P
NSLOT = 2 * B * N // P + E_N - 1
LAYERS = 2
ROW = D + 2
RESULTS = 2 * T * P


def slot_steps(eng, step, end):
    for j in range(7):
        step(j, j)
    with eng.Fori(0, 7) as i:
        for u in range(7, 11):
            step(i * 4 + u, u)
    for j in range(35, end):
        step(j, j)


def uses_before(j, n):
    return (j - n % 4) * 4


def ffn_phase(nc, sems, dram, X, w, norm, layer, out=None):
    with ExitStack() as ctx:
        def sb(name, shape, dt=F32):
            return ctx.enter_context(nc.sbuf_tensor(f"f{layer}_{name}", shape, dt))

        def sem(name):
            return phase_semaphore(nc, sems, f"f{layer}_{name}")

        xn2 = sb("xn2", [P, T, ROW])
        rows = (norm.xn, xn2)
        xT = sb("xT", [P, T * P])
        ident = norm.ident
        prior_i = sb("prior_i", [P, E_N], I32)
        prior = sb("prior", [P, E_N])
        tile_i = sb("tile_i", [1, NSLOT], I32)
        tile_no = sb("tile_no", [1, NSLOT])
        result_i = sb("result_i", [P, T, 2], I32)
        below_f = sb("below_f", [P, P])
        below = sb("below", [P, P], BF16)
        ones = sb("ones", [P, P], BF16)
        L = sb("L", [P, T, E_N])
        eq = sb("eq", [P, T, E_N])
        rank = sb("rank", [P, T, E_N])
        first = sb("first", [P, T, E_N])
        second = sb("second", [P, T, E_N])
        best = sb("best", [P, 2, T])
        top = sb("top", [P, 2, T])
        gap = sb("gap", [P, T])
        ratio = sb("ratio", [P, T])
        whole = sb("whole", [P, T])
        picked = sb("picked", [P, 2 * T + 1, E_N], BF16)
        count_i = sb("count_i", [P, E_N], I32)
        tiles_i = sb("tiles_i", [P, E_N], I32)
        tiles = sb("tiles", [P, E_N])
        one8 = sb("one8", [P, E_N])
        ends = sb("ends", [P, E_N])
        starts = sb("starts", [P, E_N])
        place = sb("place", [P, T, E_N])
        slot = sb("slot", [P, 2, T])
        slot_i = sb("slot_i", [P, 2, T], I32)
        after = sb("after", [1, NSLOT, E_N])
        tile_e = sb("tile_e", [1, NSLOT])
        tile_w = sb("tile_w", [1, NSLOT], I32)
        hT_s = sb("hT_s", [P, 2, HC, GROUP * P])
        xg = sb("xg", [P, 4, ROW])
        xgT = sb("xgT", [P, 2, P])
        up = sb("up", [P, 2, HID])
        hT = sb("hT", [P, 2, HID])
        yo = sb("yo", [P, 4, D])
        to = sb("to", [P, 4], I32)
        gate = sb("gate", [P, 4])
        Y = sb("Y", [P, T, 2, D])
        bank = [ctx.enter_context(nc.psum_tensor(f"f{layer}_bank{i}", [P, 512], F32)) for i in range(8)]

        consts = sem("consts")
        copied = sem("copied")
        xT_ps = sem("xT_ps")
        xT_ok = sem("xT_ok")
        logit_ps = sem("logit_ps")
        stat = sem("stat")
        gap_ok = sem("gap_ok")
        ratio_ok = sem("ratio_ok")
        picked_ok = sem("picked_ok")
        place_ps = sem("place_ps")
        slot_ok = sem("slot_ok")
        tile_ok = sem("tile_ok")
        sent = sem("sent")
        sh_ps = sem("sh_ps")
        sh_ok = sem("sh_ok")
        so_ps = sem("so_ps")
        so_ok = sem("so_ok")
        xg_in = [sem(f"xg_in{i}") for i in range(4)]
        y_out = [sem(f"y_out{i}") for i in range(4)]
        up_ok = sem("up_ok")
        xt_ps = sem("xt_ps")
        xt_ok = sem("xt_ok")
        tag_ok = sem("tag_ok")
        h_ps = sem("h_ps")
        h_ok = sem("h_ok")
        y_ps = sem("y_ps")
        y_ok = sem("y_ok")
        back = [sem(f"back{g}") for g in range(GROUPS)]
        stored = sem("stored")
        mean_ok = sem("mean_ok")
        root_ok = sem("root_ok")
        neg_ok = sem("neg_ok")
        xn_ok = sem("xn_ok")
        pool_x = sem("pool_x")
        dve_x = sem("dve_x")
        passed = sem("passed")

        slots, results = dram[f"slots{layer}"], dram[f"results{layer}"]
        J = NSLOT

        def add_results(eng, g, s, done):
            eng.wait_ge(so_ok, GROUPS)
            eng.wait_ge(back[g], 16)
            for k in range(2):
                eng.tensor_tensor(X[:, s, :], X[:, s, :], Y[:, s, k, :], ALU.add).then_inc(done, 1)
                eng.wait_ge(done, 2 * g + k + 1)

        with nc.Block() as block:
            @block.sync
            def _(sp):
                def load(j, n):
                    sp.dma_start(xg[:, n % 4, :], slots[bass.ds(j * P, P), :]).then_inc(xg_in[n % 4], 16)

                def step(j, n):
                    if n + 4 < J:
                        sp.wait_ge(tag_ok, j + 1)
                        load(j + 4, n)

                sp.wait_ge(sent, 16 * 2 * T)
                for j in range(4):
                    load(j, j)
                slot_steps(sp, step, J)
                for n in range(4):
                    sp.wait_ge(y_out[n], 16 * ((J + 3 - n) // 4))
                for g in range(GROUPS):
                    s = slice(GROUP * g, GROUP * g + GROUP)
                    sp.dma_start(Y[:, s, :, :], results[0:RESULTS, :].rearrange("(p t k) d -> p t k d", p=P, k=2)
                                 [:, s, :, :]).then_inc(back[g], 16)
                if out is not None:
                    for g in range(GROUPS):
                        s = slice(GROUP * g, GROUP * g + GROUP)
                        sp.wait_ge(pool_x, 2 * (g + 1))
                        sp.wait_ge(dve_x, 2 * (g + 1))
                        sp.dma_start(out.rearrange("(t p) d -> p t d", p=P)[:, s, :], X[:, s, :])\
                          .then_inc(stored, 16)
                    sp.wait_ge(stored, 16 * GROUPS)

            @block.gpsimd
            def _(pool):
                pool.memset(below_f[:, :], 1.0).then_inc(consts, 1)
                pool.memset(ones[:, :], 1.0).then_inc(consts, 1)
                pool.memset(picked[:, :, :], 0.0).then_inc(consts, 1)
                pool.iota(prior_i[:, :], [[-1, E_N]], base=E_N, channel_multiplier=0).then_inc(consts, 1)
                pool.iota(tile_i[:, :], [[1, NSLOT]], base=0, channel_multiplier=0).then_inc(consts, 1)
                pool.iota(result_i[:, :, :], [[1, 2 * T]], base=0, channel_multiplier=2 * T).then_inc(consts, 1)
                pool.memset(one8[:, :], 1.0).then_inc(consts, 1)
                pool.wait_ge(consts, 7)
                pool.tensor_copy(prior[:, :], prior_i[:, :]).then_inc(consts, 1)
                pool.affine_select(out=below[:, :], in_=below_f[:, :], compare_op=ALU.is_gt, fill=0.0,
                                   base=0, pattern=[[1, P]], channel_multiplier=-1).then_inc(consts, 1)
                pool.tensor_copy(tile_no[:, :], tile_i[:, :]).then_inc(consts, 1)
                for k in range(2):
                    pool.tensor_copy(rows[k][:, :, D], result_i[:, :, k]).then_inc(consts, 1)
                pool.wait_ge(consts, 12)
                pool.wait_ge(copied, GROUPS)
                pool.wait_ge(slot_ok, 1)
                for t in range(T):
                    for k in range(2):
                        pool.indirect_dma_start(
                            slots, bass.IndirectOffsetOnAxis(ap=slot_i[:, k, t:t + 1].bitcast(U32), axis=0),
                            rows[k][:, t, :], None).then_inc(sent, 16)

                def step(j, n):
                    pool.wait_ge(y_ok, j + 1)
                    pool.sem_inc(passed, 1)
                    pool.indirect_dma_start(
                        results, bass.IndirectOffsetOnAxis(ap=to[:, n % 4:n % 4 + 1].bitcast(U32), axis=0),
                        yo[:, n % 4, :], None).then_inc(y_out[n % 4], 16)

                slot_steps(pool, step, J)
                for g in range(GROUPS):
                    add_results(pool, g, slice(GROUP * g, GROUP * g + 1), pool_x)
                    if out is None and g >= 1:
                        norm.roots(pool, g - 1, mean_ok, root_ok)
                if out is None:
                    norm.roots(pool, GROUPS - 1, mean_ok, root_ok)

            @block.vector
            def _(dve):
                n = 0

                def chain(instruction):
                    nonlocal n
                    n += 1
                    instruction.then_inc(stat, 1)
                    dve.wait_ge(stat, n)

                def over_experts(x):
                    return x.rearrange("p (t a) -> p t a", a=1).broadcast_to([P, T, E_N])

                dve.wait_ge(consts, 8)
                pr = prior[:, :].rearrange("p (a e) -> p a e", a=1).broadcast_to([P, T, E_N])
                for g in range(GROUPS):
                    dve.wait_ge(logit_ps, g + 1)
                    last = dve.tensor_copy(L[:, GROUP * g:GROUP * g + GROUP, :],
                                           bank[4 + g][:, 0:GROUP * STREAM].rearrange("p (t c) -> p t c", c=STREAM)
                                           [:, :, 0:E_N])
                chain(last)
                for k, choice in enumerate((first, second)):
                    chain(dve.tensor_reduce(best[:, k, :], L[:, :, :], AX.X, ALU.max))
                    chain(dve.tensor_tensor(eq[:, :, :], L[:, :, :], over_experts(best[:, k, :]), ALU.is_equal))
                    chain(dve.tensor_tensor(rank[:, :, :], eq[:, :, :], pr, ALU.mult))
                    chain(dve.tensor_reduce(top[:, k, :], rank[:, :, :], AX.X, ALU.max))
                    chain(dve.tensor_tensor(choice[:, :, :], over_experts(top[:, k, :]), pr, ALU.is_equal))
                    if k == 0:
                        chain(dve.scalar_tensor_tensor(out=L[:, :, :], in0=first[:, :, :], scalar=-LARGE,
                                                       in1=L[:, :, :], op0=ALU.mult, op1=ALU.add))
                dve.tensor_tensor(picked[:, T:2 * T, :], first[:, :, :], second[:, :, :], ALU.add)\
                   .then_inc(picked_ok, 1)
                dve.tensor_tensor(gap[:, :], best[:, 1, :], best[:, 0, :], ALU.subtract).then_inc(gap_ok, 1)
                dve.wait_ge(ratio_ok, 1)
                chain(dve.tensor_scalar(whole[:, :], ratio[:, :], 1.0, None, ALU.add))
                chain(dve.reciprocal(rows[0][:, :, D + 1], whole[:, :]))
                chain(dve.tensor_tensor(rows[1][:, :, D + 1], ratio[:, :], rows[0][:, :, D + 1], ALU.mult))

                dve.wait_ge(consts, 12)
                dve.wait_ge(place_ps, 1)
                pl = bank[5][:, 0:T * E_N].rearrange("p (t e) -> p t e", e=E_N)
                chain(dve.tensor_scalar(count_i[:, :], bank[5][:, T * E_N:(T + 1) * E_N], float(P - 1), None,
                                        ALU.add))
                chain(dve.tensor_scalar(tiles_i[:, :], count_i[:, :], 7, None, ALU.logical_shift_right))
                chain(dve.tensor_copy(tiles[:, :], tiles_i[:, :]))
                chain(dve.tensor_tensor_scan(ends[:, :], one8[:, :], tiles[:, :], 0.0, ALU.mult, ALU.add))
                chain(dve.tensor_tensor(starts[:, :], ends[:, :], tiles[:, :], ALU.subtract))
                chain(dve.tensor_scalar(starts[:, :], starts[:, :], float(P), None, ALU.mult))
                chain(dve.tensor_tensor(place[:, :, :], pl,
                                        starts[:, :].rearrange("p (a e) -> p a e", a=1)
                                        .broadcast_to([P, T, E_N]), ALU.add))
                for k, choice in enumerate((first, second)):
                    chain(dve.tensor_tensor(rank[:, :, :], choice[:, :, :], place[:, :, :], ALU.mult))
                    chain(dve.tensor_reduce(slot[:, k, :], rank[:, :, :], AX.X, ALU.add))
                dve.tensor_copy(slot_i[:, :, :], slot[:, :, :]).then_inc(slot_ok, 1)
                chain(dve.tensor_tensor(
                    after[:, :, :], tile_no[:, :].rearrange("p (j a) -> p j a", a=1).broadcast_to([1, NSLOT, E_N]),
                    ends[0:1, :].rearrange("p (a e) -> p a e", a=1).broadcast_to([1, NSLOT, E_N]), ALU.is_ge))
                chain(dve.tensor_reduce(tile_e[:, :], after[:, :, :], AX.X, ALU.add))
                dve.tensor_scalar(tile_w[:, :], tile_e[:, :], float(E_N - 1), float(HID), ALU.min, ALU.mult)\
                   .then_inc(tile_ok, 1)

                for g in range(GROUPS):
                    dve.wait_ge(so_ps, g + 1)
                    Xg = X[:, GROUP * g:GROUP * g + GROUP, :]
                    dve.tensor_tensor(Xg, bank[6][:, :].rearrange("p (t d) -> p t d", d=D), Xg, ALU.add)\
                       .then_inc(so_ok, 1)

                def weights(j, n):
                    start = dve.value_load(tile_w[0:1, bass.ds(j, 1)], min_val=0, max_val=(E_N - 1) * HID)
                    if n >= 2:
                        dve.wait_ge(h_ps, j - 1)
                    dve.tensor_copy(up[:, n % 2, :], w["e1"][:, bass.ds(start, HID)]).then_inc(up_ok, 1)

                def turn_x(j, n):
                    dve.wait_ge(xt_ps, j + 1)
                    dve.tensor_copy(xgT[:, n % 2, :], bank[n % 2][:, 0:P]).then_inc(xt_ok, 1)

                def step(j, n):
                    if n + 1 < J:
                        weights(j + 1, n + 1)
                        turn_x(j + 1, n + 1)
                    if n >= 1:
                        m = (n - 1) % 4
                        if n >= 5:
                            dve.wait_ge(y_out[m], uses_before(j - 1, n - 1))
                        dve.tensor_copy(to[:, m:m + 1], xg[:, m, D:D + 1])
                        dve.tensor_copy(gate[:, m:m + 1], xg[:, m, D + 1:D + 2]).then_inc(tag_ok, 1)

                dve.wait_ge(tile_ok, 1)
                weights(0, 0)
                turn_x(0, 0)
                slot_steps(dve, step, J + 1)
                for g in range(GROUPS):
                    add_results(dve, g, slice(GROUP * g + 1, GROUP * g + GROUP), dve_x)
                    if out is None:
                        dve.wait_ge(pool_x, 2 * (g + 1))
                        norm.statistics(dve, X, g, mean_ok)

            @block.scalar
            def _(act):
                for g in range(GROUPS):
                    act.wait_ge(xT_ps, g + 1)
                    act.activation(xT[:, 512 * g:512 * g + 512], bank[g][:, :], ACT.Copy).then_inc(xT_ok, 1)
                for g in range(GROUPS):
                    s = slice(GROUP * g, GROUP * g + GROUP)
                    act.activation(xn2[:, s, 0:D], norm.xn[:, s, 0:D], ACT.Copy).then_inc(copied, 1)
                act.wait_ge(gap_ok, 1)
                act.activation(ratio[:, :], gap[:, :], ACT.Exp).then_inc(ratio_ok, 1)
                for g in range(GROUPS):
                    for c in range(HC):
                        act.wait_ge(sh_ps, g * HC + c + 1)
                        if g >= 2:
                            act.wait_ge(so_ps, g - 1)
                        act.activation(hT_s[:, g % 2, c, :], bank[c][:, :], ACT.Silu).then_inc(sh_ok, 1)

                def step(j, n):
                    if n < J:
                        act.wait_ge(h_ps, j + 1)
                        if n >= 2:
                            act.wait_ge(y_ps, j - 1)
                        act.activation(hT[:, n % 2, :], bank[2 + n % 2][:, :], ACT.Silu).then_inc(h_ok, 1)
                    if n >= 1:
                        act.wait_ge(tag_ok, j)
                        act.wait_ge(y_ps, j)
                        act.activation(yo[:, (n - 1) % 4, :], bank[4 + (n - 1) % 2][:, 0:D], ACT.Copy,
                                       scale=gate[:, (n - 1) % 4:(n - 1) % 4 + 1]).then_inc(y_ok, 1)

                slot_steps(act, step, J + 1)
                if out is None:
                    for g in range(GROUPS):
                        norm.normalise(act, X, g, root_ok, neg_ok, xn_ok)

            @block.tensor
            def _(pe):
                def logits(g):
                    pe.wait_ge(xT_ok, g + 1)
                    for t in range(GROUP):
                        c = P * (GROUP * g + t)
                        last = pe.matmul(bank[4 + g][:, STREAM * t:STREAM * t + STREAM], xT[:, c:c + P],
                                         w["gate"][:, :].rearrange("p (a e) -> p a e", a=1)
                                         .broadcast_to([P, STREAM // E_N, E_N]), start=True, stop=True)
                    last.then_inc(logit_ps, 1)

                def hidden(g):
                    for c in range(HC):
                        if g >= 1:
                            pe.wait_ge(sh_ok, (g - 1) * HC + c + 1)
                        pe.matmul(bank[c][:, :], w["s1"][:, P * c:P * c + P],
                                  xT[:, g * GROUP * P:(g + 1) * GROUP * P], start=True, stop=True)\
                          .then_inc(sh_ps, 1)

                def shared_out(g):
                    pe.wait_ge(sh_ok, (g + 1) * HC)
                    if g >= 1:
                        pe.wait_ge(so_ok, g)
                    for t in range(GROUP):
                        for c in range(HC):
                            last = pe.matmul(bank[6][:, D * t:D * t + D], hT_s[:, g % 2, c, P * t:P * t + P],
                                             w["s2"][:, D * c:D * c + D], start=(c == 0), stop=(c == HC - 1))
                    last.then_inc(so_ps, 1)

                for g in range(GROUPS):
                    for t in range(GROUP):
                        last = pe.transpose(bank[g][:, P * t:P * t + P], norm.xn[:, GROUP * g + t, 0:D], ident[:, :])
                    last.then_inc(xT_ps, 1)
                    if g >= 1:
                        logits(g - 1)
                logits(GROUPS - 1)
                hidden(0)
                pe.wait_ge(consts, 9)
                pe.wait_ge(picked_ok, 1)
                width = (T + 1) * E_N
                flat = picked[:, :, :].rearrange("p t e -> p (t e)")
                pe.matmul(bank[5][:, 0:width], below[:, :], flat[:, T * E_N:T * E_N + width], start=True, stop=False)
                for k in range(1, T + 1):
                    last = pe.matmul(bank[5][:, 0:width], ones[:, :],
                                     flat[:, (T - k) * E_N:(T - k) * E_N + width], start=False, stop=(k == T))
                last.then_inc(place_ps, 1)
                for g in range(1, GROUPS):
                    hidden(g)
                    shared_out(g - 1)
                shared_out(GROUPS - 1)

                def turn_x(j, n):
                    pe.wait_ge(xg_in[n % 4], uses_before(j, n) + 16)
                    if n >= 2:
                        pe.wait_ge(xt_ok, j - 1)
                    pe.transpose(bank[n % 2][:, 0:P], xg[:, n % 4, 0:D], ident[:, :]).then_inc(xt_ps, 1)

                def step(j, n):
                    if n >= 1:
                        start = pe.value_load(tile_w[0:1, bass.ds(j - 1, 1)], min_val=0, max_val=(E_N - 1) * HID)
                    if n < J:
                        pe.wait_ge(up_ok, j + 1)
                        pe.wait_ge(xt_ok, j + 1)
                        if n >= 2:
                            pe.wait_ge(h_ok, j - 1)
                        for c in range(HC):
                            last = pe.matmul(bank[2 + n % 2][:, P * c:P * c + P], up[:, n % 2, P * c:P * c + P],
                                             xgT[:, n % 2, :], start=True, stop=True)
                        last.then_inc(h_ps, 1)
                    if n + 1 < J:
                        turn_x(j + 1, n + 1)
                    if n >= 1:
                        m = (n - 1) % 2
                        pe.wait_ge(h_ok, j)
                        if n >= 3:
                            pe.wait_ge(y_ok, j - 2)
                        for c in range(HC):
                            last = pe.matmul(bank[4 + m][:, 0:D], hT[:, m, P * c:P * c + P],
                                             w["e2"][:, bass.ds(start + c * D, D)], start=(c == 0),
                                             stop=(c == HC - 1))
                        last.then_inc(y_ps, 1)

                pe.wait_ge(tile_ok, 1)
                pe.wait_ge(sh_ok, GROUPS * HC)
                turn_x(0, 0)
                slot_steps(pe, step, J + 1)
NH = 4
HD = 64
CH = NH * HD
TAPS = 4
XBC = CH + NH


def mixer_phase(nc, sems, dram, X, norm):
    ROWS = 2
    G = B // ROWS
    GT = ROWS * TB
    BLK = 3
    with ExitStack() as ctx:
        def sb(name, shape, dt=F32):
            return ctx.enter_context(nc.sbuf_tensor(f"m_{name}", shape, dt))

        def sem(name):
            return phase_semaphore(nc, sems, f"m_{name}")

        w_in = sb("w_in", [P, 3 * CH + NH])
        conv_w = sb("conv_w", [P, 4, TAPS])
        conv_b = sb("conv_b", [P, 4])
        dt_bias = sb("dt_bias", [P, NH])
        a_log = sb("a_log", [P, NH])
        d_skip = sb("d_skip", [P, NH])
        norm_w = sb("norm_w", [P, 2])
        w_out = sb("w_out", [P, 2, D])
        conv_rows = sb("conv_rows", [P, TAPS, CH])
        w_taps = sb("w_taps", [P, TAPS, CH])
        xT = sb("xT", [P, T * P])
        ident = norm.ident
        upto = sb("upto", [P, P])
        mask = sb("mask", [P, BLK, P])
        a_neg = sb("a_neg", [P, NH])
        raw = sb("raw", [P, T, NH])
        mag = sb("mag", [P, T, NH])
        small = sb("small", [P, T, NH])
        onep = sb("onep", [P, T, NH])
        step_ = sb("step_", [P, T, NH])
        inv = sb("inv", [P, T, NH])
        log1 = sb("log1", [P, T, NH])
        tiny = sb("tiny", [P, T, NH])
        dt = sb("dt", [P, T, NH])
        dA = sb("dA", [P, T * NH])
        cum = sb("cum", [P, T * NH])
        cum_rows = sb("cum_rows", [T * NH, P])
        spread = sb("spread", [P, T * NH, P])
        to_end = sb("to_end", [P, T * NH])
        z = sb("z", [P, T, CH])
        U = sb("U", [P, 2, ROWS, TAPS - 1 + N])
        acc = sb("acc", [P, 2, ROWS * N])
        xbc = sb("xbc", [P, 4, ROWS * N])
        xs = sb("xs", [P, GT, CH])
        xdt = sb("xdt", [P, GT, CH])
        xskip = sb("xskip", [P, GT, CH])
        cb = sb("cb", [P, ROWS, BLK, P])
        decay = sb("decay", [P, 2, ROWS, BLK, NH, P])
        y = sb("y", [P, GT, CH])
        squares = sb("squares", [P, GT, CH])
        ssq = sb("ssq", [P, GT])
        msq = sb("msq", [P, GT])
        yr = sb("yr", [P, GT])
        yT = sb("yT", [P, 2, GT * P])
        bank = [ctx.enter_context(nc.psum_tensor(f"m_bank{i}", [P, 512], F32)) for i in range(8)]

        z_bank = bank[4:8] + bank[0:4]

        w_ok = sem("w_ok")
        p_in = sem("p_in")
        consts = sem("consts")
        mean_ok = sem("mean_ok")
        root_ok = sem("root_ok")
        neg_ok = sem("neg_ok")
        stat = sem("stat")
        rows_w = sem("rows_w")
        taps_ok = sem("taps_ok")
        xn_ok = sem("xn_ok")
        xT_ps = sem("xT_ps")
        xT_ok = sem("xT_ok")
        raw_in = sem("raw_in")
        raw_ok = sem("raw_ok")
        small_ok = sem("small_ok")
        onep_ok = sem("onep_ok")
        log_ok = sem("log_ok")
        dA_ok = sem("dA_ok")
        cum_ps = sem("cum_ps")
        cum_ok = sem("cum_ok")
        rows_ps = sem("rows_ps")
        rows_ok = sem("rows_ok")
        rows_out = sem("rows_out")
        spread_in = sem("spread_in")
        spread_rest = sem("spread_rest")
        end_ok = sem("end_ok")
        z_ps = sem("z_ps")
        z_ok = sem("z_ok")
        xbc_ps = sem("xbc_ps")
        tap_ok = sem("tap_ok")
        conv = sem("conv")
        xbc_ok = sem("xbc_ok")
        far_ok = sem("far_ok")
        near_ok = sem("near_ok")
        decay_ok = sem("decay_ok")
        x_ps = sem("x_ps")
        xs_ok = sem("xs_ok")
        xdt_ok = sem("xdt_ok")
        cb_ps = sem("cb_ps")
        cb_ok = sem("cb_ok")
        m_ok = sem("m_ok")
        skip_ok = sem("skip_ok")
        y_ps = sem("y_ps")
        y1_ok = sem("y1_ok")
        yg_ok = sem("yg_ok")
        ssq_ok = sem("ssq_ok")
        msq_ok = sem("msq_ok")
        yr_ok = sem("yr_ok")
        yT_ps = sem("yT_ps")
        yT_ok = sem("yT_ok")
        o_ps = sem("o_ps")
        x_ok = sem("x_ok")

        with nc.Block() as block:
            @block.sync
            def _(sp):
                for name, tile in (("w_in", w_in), ("conv_w", conv_w), ("conv_b", conv_b), ("norm_w", norm_w),
                                   ("w_out", w_out)):
                    sp.dma_start(tile[:], dram[name]).then_inc(w_ok, 16)
                for name, tile in (("dt_bias", dt_bias), ("a_log", a_log), ("d_skip", d_skip)):
                    sp.dma_start(tile[:, :], dram[name].broadcast_to([P, NH])).then_inc(p_in, 16)
                sp.dma_start(conv_rows[:, :, :], dram["conv_rows"].rearrange("(a k) c -> a k c", a=1)
                             .broadcast_to([P, TAPS, CH])).then_inc(rows_w, 16)
                sp.wait_ge(rows_ok, 1)
                sp.dma_start(dram["cum_rows"], cum_rows[:, :]).then_inc(rows_out, 16)
                sp.wait_ge(rows_out, 16)
                for g in range(G):
                    r = GT * NH
                    sp.dma_start(spread[:, g * r:(g + 1) * r, :],
                                 dram["cum_rows"][g * r:(g + 1) * r, :].rearrange("(a r) l -> a r l", a=1)
                                 .broadcast_to([P, r, P])).then_inc(spread_rest if g else spread_in, 16)

            @block.gpsimd
            def _(pool):
                pool.memset(upto[:, :], 1.0).then_inc(consts, 1)
                pool.memset(mask[:, :, :], 1.0).then_inc(consts, 1)
                pool.memset(U[:, :, :, 0:TAPS - 1], 0.0).then_inc(consts, 1)
                pool.wait_ge(consts, 3)
                for tri in (upto[:, :], mask[:, 0, :], mask[:, 2, :]):
                    pool.affine_select(out=tri, in_=tri, compare_op=ALU.is_ge, fill=0.0,
                                       base=0, pattern=[[1, P]], channel_multiplier=-1).then_inc(consts, 1)
                pool.wait_ge(w_ok, 80)
                pool.wait_ge(rows_w, 16)
                for k in range(TAPS):
                    last = pool.tensor_tensor(w_taps[:, k, :], w_in[:, XBC + CH:XBC + 2 * CH], conv_rows[:, k, :], ALU.mult)
                last.then_inc(taps_ok, 1)

                def over(x, n):
                    return x.rearrange("p (h a) -> p h a", a=1).broadcast_to([P, NH, n])

                def far_exponents(g):
                    pool.wait_ge(end_ok, 2 if g else 1)
                    if g >= 2:
                        pool.wait_ge(y_ps, (g - 1) * ROWS)
                    s = g % 2
                    for q in range(ROWS):
                        near = (g * GT + q * TB) * NH
                        far = near + NH
                        pool.tensor_tensor(decay[:, s, q, 1, :, :], spread[:, far:far + NH, :],
                                           over(to_end[:, near:near + NH], P), ALU.add).then_inc(far_ok, 1)

                def skip(g):
                    pool.wait_ge(xs_ok, 2 * (g + 1))
                    if g >= 1:
                        pool.wait_ge(y1_ok, g * ROWS)
                    for t in range(GT):
                        last = pool.tensor_tensor(xskip[:, t, :].rearrange("p (h d) -> p h d", h=NH),
                                                  xs[:, t, :].rearrange("p (h d) -> p h d", h=NH),
                                                  over(d_skip[:, :], HD), ALU.mult)
                    last.then_inc(skip_ok, 1)

                def mean_square(g):
                    pool.wait_ge(msq_ok, g + 1)
                    if g >= 1:
                        pool.wait_ge(x_ok, g * GT)
                    pool.tensor_tensor(yr[:, :], msq[:, :], norm.half[:, 0:GT], ALU.pow).then_inc(yr_ok, 1)

                pool.wait_ge(p_in, 48)
                far_exponents(0)
                for g in range(G):
                    skip(g)
                    if g + 1 < G:
                        far_exponents(g + 1)
                    if g >= 1:
                        norm.roots(pool, g - 1, mean_ok, root_ok)
                    mean_square(g)
                norm.roots(pool, G - 1, mean_ok, root_ok)

            @block.vector
            def _(dve):
                n = 0

                def chain(instruction):
                    nonlocal n
                    n += 1
                    instruction.then_inc(stat, 1)
                    dve.wait_ge(stat, n)

                def every(x):
                    return x.rearrange("p (a h) -> p a h", a=1).broadcast_to([P, T, NH])

                dve.wait_ge(p_in, 48)
                for t in range(T):
                    dve.wait_ge(z_ok, t + 1)
                    dve.tensor_tensor(raw[:, t, :], z_bank[t % 8][:, CH:XBC], dt_bias[:, :], ALU.add)\
                       .then_inc(raw_in, 1)
                dve.wait_ge(raw_in, T)
                chain(dve.tensor_scalar(mag[:, :, :], raw[:, :, :], -1.0, None, ALU.mult))
                dve.tensor_tensor(mag[:, :, :], raw[:, :, :], mag[:, :, :], ALU.max).then_inc(raw_ok, 1)
                dve.wait_ge(small_ok, 2)
                dve.tensor_scalar(onep[:, :, :], small[:, :, :], 1.0, None, ALU.add).then_inc(onep_ok, 1)
                dve.wait_ge(onep_ok, 1)
                chain(dve.tensor_scalar(step_[:, :, :], onep[:, :, :], -1.0, None, ALU.add))
                chain(dve.tensor_scalar(tiny[:, :, :], step_[:, :, :], 0.0, None, ALU.is_equal))
                chain(dve.tensor_tensor(inv[:, :, :], step_[:, :, :], tiny[:, :, :], ALU.add))
                chain(dve.reciprocal(inv[:, :, :], inv[:, :, :]))
                chain(dve.tensor_tensor(inv[:, :, :], inv[:, :, :], small[:, :, :], ALU.mult))
                chain(dve.tensor_tensor(tiny[:, :, :], tiny[:, :, :], small[:, :, :], ALU.mult))
                chain(dve.scalar_tensor_tensor(out=tiny[:, :, :], in0=raw[:, :, :], scalar=0.0, in1=tiny[:, :, :],
                                               op0=ALU.max, op1=ALU.add))
                dve.wait_ge(log_ok, 1)
                chain(dve.tensor_tensor(inv[:, :, :], inv[:, :, :], log1[:, :, :], ALU.mult))
                chain(dve.tensor_tensor(dt[:, :, :], inv[:, :, :], tiny[:, :, :], ALU.add))
                chain(dve.tensor_scalar(a_neg[:, :], a_neg[:, :], -1.0, None, ALU.mult))
                dve.tensor_tensor(dA[:, :].rearrange("p (t h) -> p t h", h=NH), dt[:, :, :], every(a_neg[:, :]),
                                  ALU.mult).then_inc(dA_ok, 1)
                dve.wait_ge(cum_ps, 1)
                dve.tensor_copy(cum[:, :], bank[5][:, 0:T * NH]).then_inc(cum_ok, 1)
                dve.wait_ge(rows_ps, 1)
                dve.tensor_copy(cum_rows[:, :], bank[6][0:T * NH, 0:P]).then_inc(rows_ok, 1)

                def convolve(g):
                    for c in range(2):
                        dve.wait_ge(tap_ok, (g * 2 + c) * 2 + 2)
                        for k in range(TAPS - 1):
                            a = acc[:, c, :].rearrange("p (r l) -> p r l", r=ROWS)
                            dve.scalar_tensor_tensor(out=a, in0=U[:, c, :, k:k + N], scalar=conv_w[:, c, k:k + 1],
                                                     in1=a, op0=ALU.mult, op1=ALU.add).then_inc(conv, 1)
                            dve.wait_ge(conv, (g * 2 + c) * (TAPS - 1) + k + 1)

                def ends(c0, c1):
                    dve.tensor_tensor(to_end[:, c0:c1], spread[:, c0:c1, P - 1], cum[:, c0:c1], ALU.subtract)\
                       .then_inc(end_ok, 1)

                def near_exponents(g):
                    if g >= 2:
                        dve.wait_ge(y_ps, (g - 1) * ROWS)
                    for q in range(ROWS):
                        for u in range(TB):
                            for h in range(NH):
                                c = (g * GT + q * TB + u) * NH + h
                                last = dve.tensor_scalar(decay[:, g % 2, q, 2 * u, h, :], spread[:, c, :],
                                                         cum[:, c:c + 1], 0.0, ALU.subtract, ALU.min)
                        last.then_inc(near_ok, 1)

                def times_dt(g):
                    for q in range(ROWS):
                        dve.wait_ge(x_ps, g * ROWS + q + 1)
                        for u in range(TB):
                            t = q * TB + u
                            last = dve.tensor_tensor(
                                xdt[:, t, :].rearrange("p (h d) -> p h d", h=NH),
                                bank[q][:, CH * u:CH * u + CH].rearrange("p (h d) -> p h d", h=NH),
                                dt[:, g * GT + t, :].rearrange("p (h a) -> p h a", a=1).broadcast_to([P, NH, HD]),
                                ALU.mult)
                        last.then_inc(xdt_ok, 1)

                def products(g):
                    for q in range(ROWS):
                        i = g * ROWS + q
                        dve.wait_ge(cb_ps, i + 1)
                        dve.tensor_tensor(cb[:, q, :, :], bank[2 + q][:, 0:BLK * P].rearrange("p (k l) -> p k l", k=BLK),
                                          mask[:, :, :], ALU.mult).then_inc(cb_ok, 1)
                    for q in range(ROWS):
                        i = g * ROWS + q
                        dve.wait_ge(cb_ok, i + 1)
                        dve.wait_ge(decay_ok, i + 1)
                        M = decay[:, g % 2, q, :, :, :]
                        dve.tensor_tensor(M, M, cb[:, q, :, :].rearrange("p k (a l) -> p k a l", a=1)
                                          .broadcast_to([P, BLK, NH, P]), ALU.mult).then_inc(m_ok, 1)

                def gated(g):
                    dve.wait_ge(skip_ok, g + 1)
                    if g >= 1:
                        dve.wait_ge(ssq_ok, g * GT)
                    for q in range(ROWS):
                        i = g * ROWS + q
                        dve.wait_ge(y_ps, i + 1)
                        yq = y[:, q * TB:q * TB + TB, :].rearrange("p t c -> p (t c)")
                        dve.tensor_tensor(yq, bank[4 + q][:, :],
                                          xskip[:, q * TB:q * TB + TB, :].rearrange("p t c -> p (t c)"), ALU.add)\
                           .then_inc(y1_ok, 1)
                        dve.wait_ge(y1_ok, i + 1)
                        dve.tensor_tensor(yq, yq, z[:, g * GT + q * TB:g * GT + q * TB + TB, :]
                                          .rearrange("p t c -> p (t c)"), ALU.mult).then_inc(yg_ok, 1)

                def mean_squares(g):
                    dve.wait_ge(ssq_ok, (g + 1) * GT)
                    dve.tensor_scalar(msq[:, :], ssq[:, :], 1.0 / CH, EPS, ALU.mult, ALU.add).then_inc(msq_ok, 1)

                def residual(g):
                    dve.wait_ge(yr_ok, g + 1)
                    dve.wait_ge(o_ps, g + 1)
                    for t in range(GT):
                        Xt = X[:, g * GT + t, :]
                        dve.scalar_tensor_tensor(out=Xt, in0=bank[6][:, D * t:D * t + D], scalar=yr[:, t:t + 1],
                                                 in1=Xt, op0=ALU.mult, op1=ALU.add).then_inc(x_ok, 1)
                    dve.wait_ge(x_ok, (g + 1) * GT)

                dve.wait_ge(w_ok, 80)
                convolve(0)
                dve.wait_ge(spread_in, 16)
                ends(0, GT * NH)
                near_exponents(0)
                for g in range(G):
                    times_dt(g)
                    products(g)
                    if g == 0:
                        dve.wait_ge(spread_rest, 16 * (G - 1))
                        ends(GT * NH, T * NH)
                    if g + 1 < G:
                        convolve(g + 1)
                    if g >= 1:
                        residual(g - 1)
                        norm.statistics(dve, X, g - 1, mean_ok)
                    if g + 1 < G:
                        near_exponents(g + 1)
                    gated(g)
                    mean_squares(g)
                residual(G - 1)
                norm.statistics(dve, X, G - 1, mean_ok)

            @block.scalar
            def _(act):
                for g in range(GROUPS):
                    act.wait_ge(xT_ps, g + 1)
                    act.activation(xT[:, 512 * g:512 * g + 512], bank[g][:, :], ACT.Copy).then_inc(xT_ok, 1)
                for t in range(T):
                    act.wait_ge(z_ps, t + 1)
                    act.activation(z[:, t, :], z_bank[t % 8][:, 0:CH], ACT.Silu).then_inc(z_ok, 1)
                act.wait_ge(p_in, 48)
                act.activation(a_neg[:, :], a_log[:, :], ACT.Exp).then_inc(small_ok, 1)
                act.wait_ge(raw_ok, 1)
                act.activation(small[:, :, :], mag[:, :, :], ACT.Exp, scale=-1.0).then_inc(small_ok, 1)
                act.wait_ge(onep_ok, 1)
                act.activation(log1[:, :, :], onep[:, :, :], ACT.Ln).then_inc(log_ok, 1)

                def taps(g):
                    for c in range(2):
                        act.wait_ge(xbc_ps, g * 4 + c + 1)
                        act.activation(U[:, c, :, TAPS - 1:TAPS - 1 + N],
                                       bank[c][:, :].rearrange("p (r l) -> p r l", r=ROWS), ACT.Copy)\
                           .then_inc(tap_ok, 1)
                        act.activation(acc[:, c, :], bank[c][:, :], ACT.Identity, bias=conv_b[:, c:c + 1],
                                       scale=conv_w[:, c, TAPS - 1:TAPS]).then_inc(tap_ok, 1)

                def silu(g):
                    for c in (2, 3):
                        act.wait_ge(xbc_ps, g * 4 + c + 1)
                        act.activation(xbc[:, c, :], bank[2 if c == 2 else 7][:, :], ACT.Silu,
                                       bias=conv_b[:, c:c + 1]).then_inc(xbc_ok, 1)
                    for c in range(2):
                        act.wait_ge(conv, (g * 2 + c + 1) * (TAPS - 1))
                        act.activation(xbc[:, c, :], acc[:, c, :], ACT.Silu).then_inc(xbc_ok, 1)

                def decays(g):
                    for q in range(ROWS):
                        act.wait_ge(far_ok, g * ROWS + q + 1)
                        act.wait_ge(near_ok, g * ROWS + q + 1)
                        d = decay[:, g % 2, q, :, :, :]
                        act.activation(d, d, ACT.Exp).then_inc(decay_ok, 1)

                def copy_x(g):
                    if g >= 1:
                        act.wait_ge(skip_ok, g)
                    for q in range(ROWS):
                        act.wait_ge(xdt_ok, g * ROWS + q + 1)
                        act.activation(xs[:, q * TB:q * TB + TB, :], bank[q][:, :].rearrange("p (t c) -> p t c", t=TB),
                                       ACT.Copy).then_inc(xs_ok, 1)

                def square(g):
                    if g >= 1:
                        act.wait_ge(msq_ok, g)
                    for t in range(GT):
                        act.wait_ge(yg_ok, g * ROWS + t // TB + 1)
                        act.activation(squares[:, t, :], y[:, t, :], ACT.Square, accum_out=ssq[:, t:t + 1])\
                           .then_inc(ssq_ok, 1)

                def turned_y(g):
                    for k in range(2):
                        act.wait_ge(yT_ps, g * 2 + k + 1)
                        act.activation(yT[:, k, :], bank[4 + k][:, :], ACT.Copy, scale=norm_w[:, k:k + 1])\
                           .then_inc(yT_ok, 1)

                act.wait_ge(w_ok, 80)
                taps(0)
                silu(0)
                decays(0)
                for g in range(G):
                    copy_x(g)
                    if g >= 1:
                        turned_y(g - 1)
                    if g + 1 < G:
                        taps(g + 1)
                        silu(g + 1)
                        decays(g + 1)
                    square(g)
                    if g == G - 1:
                        turned_y(g)
                    if g >= 1:
                        norm.normalise(act, X, g - 1, root_ok, neg_ok, xn_ok)
                norm.normalise(act, X, G - 1, root_ok, neg_ok, xn_ok)

            @block.tensor
            def _(pe):
                def gate_and_dt(g):
                    pe.wait_ge(xT_ok, g + 1)
                    for t in range(GROUP * g, GROUP * g + GROUP):
                        if 4 <= t < 8:
                            pe.wait_ge(xT_ok, t - 3)
                        elif t >= 8:
                            pe.wait_ge(z_ok, t - 7)
                            pe.wait_ge(raw_in, t - 7)
                        pe.matmul(z_bank[t % 8][:, 0:XBC], xT[:, P * t:P * t + P], w_in[:, 0:XBC],
                                  start=True, stop=True).then_inc(z_ps, 1)

                for g in range(GROUPS):
                    for t in range(GROUP):
                        last = pe.transpose(bank[g][:, P * t:P * t + P], norm.xn[:, GROUP * g + t, 0:D], ident[:, :])
                    last.then_inc(xT_ps, 1)
                pe.wait_ge(w_ok, 80)
                for g in range(GROUPS):
                    gate_and_dt(g)

                def project_x(g):
                    xg = xT[:, g * ROWS * N:(g + 1) * ROWS * N]
                    for c in range(2):
                        pe.matmul(bank[c][:, :], w_in[:, XBC + P * c:XBC + P * c + P], xg, start=True, stop=True)\
                          .then_inc(xbc_ps, 1)

                def project_bc(g):
                    xg = xT[:, g * ROWS * N:(g + 1) * ROWS * N]
                    for c in range(2):
                        ps = bank[7 if c else 2][:, :]
                        for k in range(TAPS - 1, -1, -1):
                            late = TAPS - 1 - k
                            last = pe.matmul(ps.rearrange("p (r l) -> p r l", r=ROWS)[:, :, late:N],
                                             w_taps[:, k, P * c:P * c + P],
                                             xg.rearrange("p (r l) -> p r l", r=ROWS)[:, :, 0:N - late],
                                             start=(late == 0), stop=(k == 0))
                        last.then_inc(xbc_ps, 1)

                pe.wait_ge(z_ok, T)
                pe.wait_ge(raw_in, T)
                project_x(0)
                pe.wait_ge(consts, 6)
                pe.wait_ge(dA_ok, 1)
                pe.matmul(bank[5][:, 0:T * NH], upto[:, :], dA[:, :], start=True, stop=True).then_inc(cum_ps, 1)
                pe.wait_ge(cum_ok, 1)
                pe.transpose(bank[6][0:T * NH, 0:P], cum[:, :], ident[:, :]).then_inc(rows_ps, 1)
                pe.wait_ge(taps_ok, 1)
                project_bc(0)

                def turn_x(g):
                    pe.wait_ge(xbc_ok, g * 4 + 4)
                    for q in range(ROWS):
                        for u in range(TB):
                            for k in range(2):
                                last = pe.transpose(bank[q][:, CH * u + P * k:CH * u + P * k + P],
                                                    xbc[:, k, P * (q * TB + u):P * (q * TB + u) + P], ident[:, :])
                        last.then_inc(x_ps, 1)

                def scores(g):
                    for q in range(ROWS):
                        s = N * q
                        pe.matmul(bank[2 + q][:, 0:N], xbc[:, 2, s:s + P], xbc[:, 3, s:s + N], start=True, stop=True)
                        pe.matmul(bank[2 + q][:, N:N + P], xbc[:, 2, s + P:s + N], xbc[:, 3, s + P:s + N],
                                  start=True, stop=True).then_inc(cb_ps, 1)

                def values(g):
                    for q in range(ROWS):
                        pe.wait_ge(m_ok, g * ROWS + q + 1)
                        for u in range(TB):
                            for h in range(NH):
                                for s in range(u + 1):
                                    last = pe.matmul(bank[4 + q][:, CH * u + HD * h:CH * u + HD * h + HD],
                                                     decay[:, g % 2, q, u + s, h, :],
                                                     xdt[:, q * TB + s, HD * h:HD * h + HD],
                                                     start=(s == 0), stop=(s == u))
                        last.then_inc(y_ps, 1)

                def turn_y(g):
                    pe.wait_ge(yg_ok, g * ROWS + ROWS)
                    for k in range(2):
                        for t in range(GT):
                            last = pe.transpose(bank[4 + k][:, P * t:P * t + P], y[:, t, P * k:P * k + P], ident[:, :])
                        last.then_inc(yT_ps, 1)

                def project_out(g):
                    pe.wait_ge(yT_ok, g * 2 + 2)
                    if g >= 1:
                        pe.wait_ge(x_ok, g * GT)
                    for t in range(GT):
                        for k in range(2):
                            last = pe.matmul(bank[6][:, D * t:D * t + D], yT[:, k, P * t:P * t + P], w_out[:, k, :],
                                             start=(k == 0), stop=(k == 1))
                    last.then_inc(o_ps, 1)

                pe.wait_ge(rows_ok, 1)
                for g in range(G):
                    turn_x(g)
                    scores(g)
                    if g >= 1:
                        turn_y(g - 1)
                    if g + 1 < G:
                        pe.wait_ge(xs_ok, g * 2 + 2)
                        project_x(g + 1)
                    if g >= 1:
                        project_out(g - 1)
                    if g + 1 < G:
                        pe.wait_ge(cb_ok, g * ROWS + 2)
                        project_bc(g + 1)
                    pe.wait_ge(xdt_ok, g * ROWS + ROWS)
                    values(g)
                turn_y(G - 1)
                project_out(G - 1)


W_SHAPES = {"s1": [P, HID], "s2": [P, HC * D], "e1": [P, E_N * HID], "e2": [P, E_N * HC * D], "gate": [P, E_N]}


def hybrid_kernel(nc, dram, out, phases="afmf"):
    dram = dict(dram)
    for layer in range(LAYERS):
        dram[f"slots{layer}"] = nc.dram_tensor(f"slots{layer}", [NSLOT * P, ROW], F32).ap()
        dram[f"results{layer}"] = nc.dram_tensor(f"results{layer}", [RESULTS + NSLOT * P, D], F32).ap()
    dram["cum_rows"] = nc.dram_tensor("cum_rows", [T * NH, P], F32).ap()
    with ExitStack() as ctx:
        X = ctx.enter_context(nc.sbuf_tensor("X", [P, T, D], F32))
        w = {n: ctx.enter_context(nc.sbuf_tensor(f"w_{n}", s, F32)) for n, s in W_SHAPES.items()}
        norm = Norm(nc, ctx)
        layer = 0
        sems = []
        for i, phase in enumerate(phases):
            if phase == "a":
                attention_phase(nc, sems, dram, X, w, norm)
            elif phase == "f":
                ffn_phase(nc, sems, dram, X, w, norm, layer, out if i == len(phases) - 1 else None)
                layer += 1
            elif phase == "m":
                mixer_phase(nc, sems, dram, X, norm)
            end_phase(nc, sems)
        if phases[-1] != "f":
            with nc.semaphore("stored") as stored, nc.Block() as block:
                @block.sync
                def _(sp):
                    sp.dma_start(out.rearrange("(t p) d -> p t d", p=P), X[:, :, :]).then_inc(stored, 16)
                    sp.wait_ge(stored, 16)


def laid_out(i):
    c = np.ascontiguousarray
    a, b, f = (lambda n, k=k: np.asarray(i[k + n]) for k in ("L0_attn_a_", "L0_attn_b_", "L0_ffn_"))
    return {
        "x": c(a("x").reshape(B * N, D)), "wq": c(a("Wq")), "wk": c(a("Wk")), "wv": c(a("Wv")),
        "wo": c(a("Wo").reshape(PAIRS, P, D).transpose(1, 0, 2).reshape(P, PAIRS * D)), "bo": c(a("bo")),
        "s1": c(f("shared_w1").T),
        "s2": c(f("shared_w2").reshape(D, HC, P).transpose(2, 1, 0).reshape(P, HC * D)),
        "e1": c(f("experts_w1").transpose(2, 0, 1).reshape(D, E_N * HID)),
        "e2": c(f("experts_w2").reshape(E_N, D, HC, P).transpose(3, 0, 2, 1).reshape(P, E_N * HC * D)),
        "gate": c(f("gate_w").T),
        "w_in": c(b("W_in")[[*range(CH), *range(3 * CH, 3 * CH + NH), *range(CH, 3 * CH)]].T),
        "conv_w": c(b("conv_w").reshape(4, P, 4).transpose(1, 0, 2)),
        "conv_rows": c(b("conv_w")[CH:].T),
        "conv_b": c(b("conv_b").reshape(4, P).T), "dt_bias": c(b("dt_bias").reshape(1, 4)),
        "a_log": c(b("A_log").reshape(1, 4)), "d_skip": c(b("D").reshape(1, 4)),
        "norm_w": c(b("norm_w").reshape(2, P).T),
        "w_out": c(b("W_out").T.reshape(2, P, D).transpose(1, 0, 2)),
    }


def kernel(**inputs):
    import concourse.bacc as bacc
    from concourse.bass_utils import run_bass_kernel_spmd

    nc = bacc.Bacc("TRN2", target_bir_lowering=False, num_devices=1)
    arrays = {f"in_{n}": a for n, a in laid_out(inputs).items()}
    dram = {n[3:]: nc.dram_tensor(n, list(a.shape), F32, kind="ExternalInput").ap() for n, a in arrays.items()}
    out = nc.dram_tensor("out_x", [B * N, D], F32, kind="ExternalOutput").ap()
    hybrid_kernel(nc, dram, out)
    result = run_bass_kernel_spmd(nc, [arrays], core_ids=[0])
    return result.results[0]["out_x"].reshape(B, N, D)
```
